# Optimizing a Trainium2 kernel written in Bass

```python
import numpy as np
import jax
import jax.numpy as jnp

def _softmax(x, axis=-1):
    return jax.nn.softmax(x, axis=axis)

def _gelu(x):
    return jax.nn.gelu(x, approximate=True)

def _silu(x):
    return jax.nn.silu(x)

def _sigmoid(x):
    return jax.nn.sigmoid(x)

def _layernorm(x, axis=-1, eps=1e-05):
    m = jnp.mean(x, axis=axis, keepdims=True)
    v = jnp.var(x, axis=axis, keepdims=True)
    return (x - m) / jnp.sqrt(v + eps)

def _scatter_add(tgt, idx, src, axis=0):
    return tgt.at[idx].add(src)

def _segment_sum(src, seg, n):
    return jax.ops.segment_sum(src, seg, n)
kernel_name = 'mk_decoder_preln_d1_seqx_r8_027419'

def setup_inputs(seed: int=0):
    np.random.seed(seed)
    _w = jnp.asarray

    def _rec_inputs():
        import jax
        import jax.numpy as jnp
        _rk = jax.random.key(seed)
        x = -0.000125 + 0.9999 * jax.random.normal(jax.random.fold_in(_rk, 1), (4, 256, 256), jnp.float32)
        _lenS = 256 - jax.random.randint(jax.random.fold_in(_rk, 7), (4,), 0, max(1, 256 // 4) + 1, jnp.int32)
        _lenS2 = 256 - jax.random.randint(jax.random.fold_in(_rk, 8), (4,), 0, max(1, 256 // 4) + 1, jnp.int32)
        itok_BxS_13_99985 = jax.random.randint(jax.random.fold_in(_rk, 11), (4, 256), 13, 99986, jnp.int32)
        _ctx_2048P = jax.random.normal(jax.random.fold_in(_rk, 12), (4, 16, 256), jnp.float32)
        _ctx_2048c = jax.random.dirichlet(jax.random.fold_in(_rk, 512), 0.3 * jnp.ones((16,), jnp.float32), (4, 256))
        _ctx_2048t = jnp.einsum('bsk,bkd->bsd', _ctx_2048c, _ctx_2048P)
        _ctx_2048t = _ctx_2048t * jax.lax.rsqrt(jnp.mean(jnp.square(_ctx_2048t)) + 1e-12) * 0.953939
        ctx_2048 = 6.82029e-06 + 0.0200006 * (_ctx_2048t + 0.3 * jax.random.normal(jax.random.fold_in(_rk, 612), (4, 256, 256), jnp.float32))
        return (x, itok_BxS_13_99985, ctx_2048)
    x, itok_BxS_13_99985, ctx_2048 = _rec_inputs()

    def _L0_attn_setup():
        import jax, jax.numpy as jnp
        import numpy as np
        DIM = 256
        HID = 512
        H = 64
        P = HID // H
        N = 128
        G = 1
        K = 4
        Q = 128
        CONV_DIM = HID + 2 * G * N
        D_IN = 2 * HID + 2 * G * N + H
        EPS = 1e-05

        def _causal_conv_silu(xBC, w):
            kern = w.T[:, None, :]
            y = jax.lax.conv_general_dilated(xBC, kern, window_strides=(1,), padding=[(K - 1, 0)], dimension_numbers=('NHC', 'HIO', 'NHC'), feature_group_count=xBC.shape[-1])
            return y * jax.nn.sigmoid(y)

        def _ssm(x, W_in, conv_w, dt_bias, A_log, D, norm_w, W_out):
            Bsz, L, _ = x.shape
            zxbcdt = x @ W_in.T
            z = zxbcdt[..., :HID]
            xBC = zxbcdt[..., HID:HID + CONV_DIM]
            dt_raw = zxbcdt[..., HID + CONV_DIM:]
            xBC = _causal_conv_silu(xBC, conv_w)
            xs = xBC[..., :HID].reshape(Bsz, L, H, P)
            rep = H // G
            Bh = jnp.repeat(xBC[..., HID:HID + G * N].reshape(Bsz, L, G, N), rep, axis=2)
            Ch = jnp.repeat(xBC[..., HID + G * N:].reshape(Bsz, L, G, N), rep, axis=2)
            dt = jax.nn.softplus(dt_raw + dt_bias)
            A = -jnp.exp(A_log)
            nc = L // Q
            a = (dt * A).reshape(Bsz, nc, Q, H)
            cum = jnp.cumsum(a, axis=2)
            xs_c = xs.reshape(Bsz, nc, Q, H, P)
            dtc = dt.reshape(Bsz, nc, Q, H)
            Bc = Bh.reshape(Bsz, nc, Q, H, N)
            Cc = Ch.reshape(Bsz, nc, Q, H, N)
            diff = cum[:, :, :, None, :] - cum[:, :, None, :, :]
            tril = jnp.tril(jnp.ones((Q, Q), bool))[None, None, :, :, None]
            Lmat = jnp.exp(jnp.where(tril, diff, -jnp.inf))
            CB = jnp.einsum('bcihn,bcjhn->bcijh', Cc, Bc)
            M = CB * Lmat * dtc[:, :, None, :, :]
            Yd = jnp.einsum('bcijh,bcjhp->bcihp', M, xs_c)
            wdec = jnp.exp(cum[:, :, -1:, :] - cum) * dtc
            states = jnp.einsum('bcqh,bcqhn,bcqhp->bchpn', wdec, Bc, xs_c)
            chunk_decay = jnp.exp(cum[:, :, -1, :])

            def step(S, inp):
                dec, st = inp
                return (S * dec[..., None, None] + st, S)
            S0 = jnp.zeros((Bsz, H, P, N), x.dtype)
            _, Sprev = jax.lax.scan(step, S0, (chunk_decay.transpose(1, 0, 2), states.transpose(1, 0, 2, 3, 4)))
            Sprev = Sprev.transpose(1, 0, 2, 3, 4)
            Yoff = jnp.einsum('bcqh,bcqhn,bchpn->bcqhp', jnp.exp(cum), Cc, Sprev)
            y = (Yd + Yoff).reshape(Bsz, L, H, P) + D[None, None, :, None] * xs
            y = y.reshape(Bsz, L, HID)
            yz = y * (z * jax.nn.sigmoid(z))
            yn = yz * jax.lax.rsqrt(jnp.mean(yz * yz, axis=-1, keepdims=True) + EPS) * norm_w
            return yn @ W_out.T
        key = jax.random.key(seed)
        k = jax.random.split(key, 6)
        return {'x': jax.random.normal(k[0], (2, 512, DIM), jnp.float32), 'W_in': jax.random.normal(k[1], (D_IN, DIM), jnp.float32) * DIM ** (-0.5), 'conv_w': jax.random.normal(k[2], (CONV_DIM, K), jnp.float32) * K ** (-0.5), 'dt_bias': jax.random.uniform(k[3], (H,), jnp.float32, minval=0.001, maxval=0.1), 'A_log': jnp.log(jax.random.uniform(k[4], (H,), jnp.float32, minval=1.0, maxval=16.0)), 'D': jnp.ones((H,), jnp.float32), 'norm_w': jnp.ones((HID,), jnp.float32), 'W_out': jax.random.normal(k[5], (DIM, HID), jnp.float32) * HID ** (-0.5)}
    _L0_attn_all = _L0_attn_setup()
    _L0_attn_in = {k: v for k, v in _L0_attn_all.items() if k in ('W_in', 'conv_w', 'dt_bias', 'A_log', 'D', 'norm_w', 'W_out')}
    del _L0_attn_all

    def _L0_xattn_setup():
        import jax, jax.numpy as jnp
        import numpy as np
        B, S, D = (4, 512, 256)
        E = 4
        F = 1024 // E
        VOCAB = 12500
        key = jax.random.key(seed)
        k1, k2, k3, k4, k5 = jax.random.split(key, 5)
        hidden_states = jax.random.normal(k1, (B, S, D), dtype=jnp.float32)
        token_ids = jax.random.randint(k2, (B, S), 0, VOCAB, dtype=jnp.int64)
        Wg = jax.random.normal(k3, (E, F, D), dtype=jnp.float32) * 0.02
        Wu = jax.random.normal(k4, (E, F, D), dtype=jnp.float32) * 0.02
        Wd = jax.random.normal(k5, (E, D, F), dtype=jnp.float32) * 0.02
        return {'hidden_states': hidden_states, 'token_ids': token_ids, 'Wg': Wg, 'Wu': Wu, 'Wd': Wd}
    _L0_xattn_all = _L0_xattn_setup()
    _L0_xattn_in = {k: v for k, v in _L0_xattn_all.items() if k in ()}
    del _L0_xattn_all

    def _L0_ffn_setup():
        import jax, jax.numpy as jnp
        import numpy as np
        L, B, D = (256, 1, 256)
        H = 16
        DK, DV = (D // 2, D)
        HDK, HDV = (DK // H, DV // H)
        RATIO = 2
        BASE = 10000.0
        EPS = 1e-05

        def _apply_rotary(x, cos, sin):
            d2 = x.shape[-1] // 2
            x1, x2 = (x[..., :d2], x[..., d2:])
            return jnp.concatenate([x1 * cos - x2 * sin, x2 * cos + x1 * sin], axis=-1)
        key = jax.random.key(seed)
        ks = jax.random.split(key, 8)
        s = 0.02
        return {'x': jax.random.normal(ks[0], (L, B, D), jnp.float32), 'conv_w': jax.random.normal(ks[1], (D, 2), jnp.float32) * 0.5, 'Wq': jax.random.normal(ks[2], (D, DK), jnp.float32) * s, 'Wk': jax.random.normal(ks[3], (D, DK), jnp.float32) * s, 'Wv': jax.random.normal(ks[4], (D, DV), jnp.float32) * s, 'Wg': jax.random.normal(ks[5], (D, DV), jnp.float32) * s, 'router_w': jax.random.normal(ks[6], (H, HDV, RATIO), jnp.float32) * s, 'Wout': jax.random.normal(ks[7], (DV, D), jnp.float32) * s}
    _L0_ffn_all = _L0_ffn_setup()
    _L0_ffn_in = {k: v for k, v in _L0_ffn_all.items() if k in ('conv_w', 'Wq', 'Wk', 'Wv', 'Wg', 'router_w', 'Wout')}
    del _L0_ffn_all
    return {'x': x, 'itok_BxS_13_99985': itok_BxS_13_99985, 'ctx_2048': ctx_2048, 'L0_attn_W_in': _L0_attn_in['W_in'], 'L0_attn_conv_w': _L0_attn_in['conv_w'], 'L0_attn_dt_bias': _L0_attn_in['dt_bias'], 'L0_attn_A_log': _L0_attn_in['A_log'], 'L0_attn_D': _L0_attn_in['D'], 'L0_attn_norm_w': _L0_attn_in['norm_w'], 'L0_attn_W_out': _L0_attn_in['W_out'], 'L0_ffn_conv_w': _L0_ffn_in['conv_w'], 'L0_ffn_Wq': _L0_ffn_in['Wq'], 'L0_ffn_Wk': _L0_ffn_in['Wk'], 'L0_ffn_Wv': _L0_ffn_in['Wv'], 'L0_ffn_Wg': _L0_ffn_in['Wg'], 'L0_ffn_router_w': _L0_ffn_in['router_w'], 'L0_ffn_Wout': _L0_ffn_in['Wout']}

def reference(x, itok_BxS_13_99985, ctx_2048, L0_attn_W_in, L0_attn_conv_w, L0_attn_dt_bias, L0_attn_A_log, L0_attn_D, L0_attn_norm_w, L0_attn_W_out, L0_ffn_conv_w, L0_ffn_Wq, L0_ffn_Wk, L0_ffn_Wv, L0_ffn_Wg, L0_ffn_router_w, L0_ffn_Wout):
    import jax
    import jax.numpy as jnp

    def _L0_attn_ref(x, W_in, conv_w, dt_bias, A_log, D, norm_w, W_out):
        import jax, jax.numpy as jnp
        import numpy as np
        DIM = 256
        HID = 512
        H = 64
        P = HID // H
        N = 128
        G = 1
        K = 4
        Q = 128
        CONV_DIM = HID + 2 * G * N
        D_IN = 2 * HID + 2 * G * N + H
        EPS = 1e-05

        def _causal_conv_silu(xBC, w):
            kern = w.T[:, None, :]
            y = jax.lax.conv_general_dilated(xBC, kern, window_strides=(1,), padding=[(K - 1, 0)], dimension_numbers=('NHC', 'HIO', 'NHC'), feature_group_count=xBC.shape[-1])
            return y * jax.nn.sigmoid(y)

        def _ssm(x, W_in, conv_w, dt_bias, A_log, D, norm_w, W_out):
            Bsz, L, _ = x.shape
            zxbcdt = x @ W_in.T
            z = zxbcdt[..., :HID]
            xBC = zxbcdt[..., HID:HID + CONV_DIM]
            dt_raw = zxbcdt[..., HID + CONV_DIM:]
            xBC = _causal_conv_silu(xBC, conv_w)
            xs = xBC[..., :HID].reshape(Bsz, L, H, P)
            rep = H // G
            Bh = jnp.repeat(xBC[..., HID:HID + G * N].reshape(Bsz, L, G, N), rep, axis=2)
            Ch = jnp.repeat(xBC[..., HID + G * N:].reshape(Bsz, L, G, N), rep, axis=2)
            dt = jax.nn.softplus(dt_raw + dt_bias)
            A = -jnp.exp(A_log)
            nc = L // Q
            a = (dt * A).reshape(Bsz, nc, Q, H)
            cum = jnp.cumsum(a, axis=2)
            xs_c = xs.reshape(Bsz, nc, Q, H, P)
            dtc = dt.reshape(Bsz, nc, Q, H)
            Bc = Bh.reshape(Bsz, nc, Q, H, N)
            Cc = Ch.reshape(Bsz, nc, Q, H, N)
            diff = cum[:, :, :, None, :] - cum[:, :, None, :, :]
            tril = jnp.tril(jnp.ones((Q, Q), bool))[None, None, :, :, None]
            Lmat = jnp.exp(jnp.where(tril, diff, -jnp.inf))
            CB = jnp.einsum('bcihn,bcjhn->bcijh', Cc, Bc)
            M = CB * Lmat * dtc[:, :, None, :, :]
            Yd = jnp.einsum('bcijh,bcjhp->bcihp', M, xs_c)
            wdec = jnp.exp(cum[:, :, -1:, :] - cum) * dtc
            states = jnp.einsum('bcqh,bcqhn,bcqhp->bchpn', wdec, Bc, xs_c)
            chunk_decay = jnp.exp(cum[:, :, -1, :])

            def step(S, inp):
                dec, st = inp
                return (S * dec[..., None, None] + st, S)
            S0 = jnp.zeros((Bsz, H, P, N), x.dtype)
            _, Sprev = jax.lax.scan(step, S0, (chunk_decay.transpose(1, 0, 2), states.transpose(1, 0, 2, 3, 4)))
            Sprev = Sprev.transpose(1, 0, 2, 3, 4)
            Yoff = jnp.einsum('bcqh,bcqhn,bchpn->bcqhp', jnp.exp(cum), Cc, Sprev)
            y = (Yd + Yoff).reshape(Bsz, L, H, P) + D[None, None, :, None] * xs
            y = y.reshape(Bsz, L, HID)
            yz = y * (z * jax.nn.sigmoid(z))
            yn = yz * jax.lax.rsqrt(jnp.mean(yz * yz, axis=-1, keepdims=True) + EPS) * norm_w
            return yn @ W_out.T
        return _ssm(x, W_in, conv_w, dt_bias, A_log, D, norm_w, W_out)

    def _L0_xattn_ref(hidden_states, token_ids, Wg, Wu, Wd):
        import jax, jax.numpy as jnp
        import numpy as np
        B, S, D = (4, 512, 256)
        E = 4
        F = 1024 // E
        VOCAB = 12500
        tokens_per_expert = VOCAB // E
        tid = jnp.clip(token_ids, 0, VOCAB - 1)
        expert_ids = jnp.minimum(tid // tokens_per_expert, E - 1)
        out = jnp.zeros_like(hidden_states)
        for e in range(E):
            g = jax.nn.silu(jnp.einsum('bsd,fd->bsf', hidden_states, Wg[e]))
            u = jnp.einsum('bsd,fd->bsf', hidden_states, Wu[e])
            y = jnp.einsum('bsf,df->bsd', g * u, Wd[e])
            out = jnp.where((expert_ids == e)[..., None], y, out)
        return out

    def _L0_ffn_ref(x, conv_w, Wq, Wk, Wv, Wg, router_w, Wout):
        import jax, jax.numpy as jnp
        import numpy as np
        L, B, D = (256, 1, 256)
        H = 16
        DK, DV = (D // 2, D)
        HDK, HDV = (DK // H, DV // H)
        RATIO = 2
        BASE = 10000.0
        EPS = 1e-05

        def _apply_rotary(x, cos, sin):
            d2 = x.shape[-1] // 2
            x1, x2 = (x[..., :d2], x[..., d2:])
            return jnp.concatenate([x1 * cos - x2 * sin, x2 * cos + x1 * sin], axis=-1)
        x = jnp.transpose(x, (1, 0, 2))
        b, l, d = x.shape
        x_prev = jnp.pad(x, ((0, 0), (1, 0), (0, 0)))[:, :l]
        x = jax.nn.silu(x_prev * conv_w[:, 0] + x * conv_w[:, 1])
        q = jax.nn.silu(x @ Wq)
        k = x @ Wk
        v = x @ Wv
        g = x @ Wg
        q = q.reshape(b, l, H, HDK).transpose(0, 2, 1, 3)
        k = k.reshape(b, l, H, HDK).transpose(0, 2, 1, 3)
        v = v.reshape(b, l, H, HDV).transpose(0, 2, 1, 3)
        inv_freq = 1.0 / BASE ** (jnp.arange(0, HDK, 2, dtype=jnp.float32) / HDK)
        freqs = jnp.arange(l, dtype=jnp.float32)[:, None] * inv_freq[None, :]
        cos, sin = (jnp.cos(freqs), jnp.sin(freqs))
        q = _apply_rotary(q, cos, sin)
        k = _apply_rotary(k, cos, sin)
        logits = jnp.einsum('bhld,hdr->bhlr', v, router_w)
        scores = jax.nn.softmax(logits, axis=-1)
        onehot = jax.nn.one_hot(jnp.argmax(scores, axis=-1), RATIO, dtype=scores.dtype)
        masked_scores = scores * onehot
        masked_ind = onehot
        sum_ind = jnp.cumsum(masked_ind, axis=2)
        norm = jnp.where(sum_ind > 0, 1.0 / jnp.maximum(sum_ind, 1.0), 0.0)[..., None]
        q_exp = q[:, :, :, None, :] * masked_scores[..., None] * norm
        k_exp = k[:, :, :, None, :] * masked_ind[..., None]
        q_exp = q_exp.reshape(b, H, l, RATIO * HDK)
        k_exp = k_exp.reshape(b, H, l, RATIO * HDK)
        qk = jnp.einsum('bhld,bhmd->bhlm', q_exp, k_exp) * HDK ** (-0.5)
        mask = jnp.tril(jnp.ones((l, l), dtype=qk.dtype))
        qk = qk * mask
        o = jnp.einsum('bhlm,bhmd->bhld', qk, v)
        o = o.transpose(0, 2, 1, 3)
        mu = jnp.mean(o, axis=-1, keepdims=True)
        var = jnp.var(o, axis=-1, keepdims=True)
        o = (o - mu) / jnp.sqrt(var + EPS)
        out = jax.nn.silu(g) * o.reshape(b, l, d)
        out = out @ Wout
        return jnp.transpose(out, (1, 0, 2))
    x = x + _L0_attn_ref(_layernorm(x, axis=-1), L0_attn_W_in, L0_attn_conv_w, L0_attn_dt_bias, L0_attn_A_log, L0_attn_D, L0_attn_norm_w, L0_attn_W_out)
    x = x + _L0_xattn_ref(_layernorm(x, axis=-1), itok_BxS_13_99985, ctx_2048, ctx_2048, ctx_2048)
    x = x + _L0_ffn_ref(_layernorm(x, axis=-1), L0_ffn_conv_w, L0_ffn_Wq, L0_ffn_Wk, L0_ffn_Wv, L0_ffn_Wg, L0_ffn_router_w, L0_ffn_Wout)
    return x

_drawn_inputs = setup_inputs


def setup_inputs(seed=0):
    import zlib

    import numpy as np

    out = dict(_drawn_inputs(seed))
    spreads = {'L0_attn_D': (1.0, 0.2), 'L0_attn_norm_w': (1.0, 0.2)}
    factors = {'L0_attn_dt_bias': 5.518,
     'L0_ffn_conv_w': 8.0,
     'L0_ffn_Wq': 8.0,
     'L0_ffn_Wk': 8.0,
     'L0_ffn_Wv': 8.0,
     'L0_ffn_Wg': 8.0,
     'L0_ffn_router_w': 8.0,
     'L0_ffn_Wout': 8.0}
    for name, (base, spread) in spreads.items():
        noise = np.random.default_rng([zlib.crc32(name.encode()), seed]).standard_normal(out[name].shape)
        drawn = base * np.exp(spread * noise) if base else spread * noise
        out[name] = jnp.asarray(drawn.astype(out[name].dtype))
    for name, factor in factors.items():
        out[name] = (out[name] * factor).astype(out[name].dtype)
    return out
```

```python
from contextlib import ExitStack

import concourse.bass as bass
from concourse import mybir

ALU = mybir.AluOpType
ACT = mybir.ActivationFunctionType
F32 = mybir.dt.float32
I32 = mybir.dt.int32
BF16 = mybir.dt.bfloat16
AX_X = mybir.AxisListType.X

P = 128
B, L, D = 4, 256, 256
C = L // P
KD = D // P
HID, H, PH, N = 512, 64, 8, 128
MZ = HID // P
MX = (HID + 2 * N) // P
WIN = HID + MX * P + P
E = 4
VOCAB = 12500
EPS = 1e-5
QH, QK, QV = 16, 8, 16
DK, DV = 128, 256

LEVELS = [(128, 32), (32, 8), (8, 4), (4, 2), (2, 1)]
NL = len(LEVELS)
SRC = [(lv, i) for lv, (par, blk) in enumerate(LEVELS[:-1]) for i in range(1, par // blk)]
NS = len(SRC)
SEAM = NS + NL
NSLOT = SEAM + 1
CBM = [(0, 0)] + [x for x in SRC if x[0] > 0] + [(NL - 1, 1)]
NM = len(CBM)
USES = [NL, NL + 1]
NU = sum(USES)


def shape_constants():
    import numpy as np
    t = np.arange(P)
    k, j = t[:, None], t[None, :]
    decay = np.zeros((P, NSLOT + 1, P), np.float32)
    for s, (lv, i) in enumerate(SRC):
        par, blk = LEVELS[lv]
        start = (j // par) * par + i * blk
        decay[:, s] = (k // par == j // par) & (k > j) & (k < start)
    for lv, (par, blk) in enumerate(LEVELS):
        decay[:, NS + lv] = (k // blk == j // blk) & (k <= j)
    decay[:, SEAM] = k > j
    decay[:, SEAM + 1] = k <= j
    cb = np.zeros((P, NM, P), np.float32)
    src, tgt = t[:, None], t[None, :]
    cb[:, 0] = src < (tgt // LEVELS[0][1]) * LEVELS[0][1]
    for m, (lv, i) in enumerate(CBM):
        if m:
            par, blk = LEVELS[lv]
            cb[:, m] = (src // par == tgt // par) & ((tgt % par) // blk == i) & (src % par < i * blk)
    ident = np.eye(P, dtype=np.float32)
    inv_freq = (1.0 / np.float32(10000.0) ** (np.arange(0, QK, 2, dtype=np.float32) / np.float32(QK))).astype(np.float32)
    ang = np.arange(B, dtype=np.float32)[:, None] * inv_freq[None, :]
    cos, sin = np.cos(ang), np.sin(ang)
    rot = np.zeros((P, B, 2, QK), np.float32)
    rot[:, :, 0] = np.concatenate([cos, cos], 1)[None]
    rot[:, :, 1] = np.concatenate([-sin, sin], 1)[None]
    sign = np.ones((P, 1), np.float32)
    sign[P // 2:] = -1.0
    return {"decay_masks": decay.reshape(P, -1), "cb_masks": cb.reshape(P, -1), "ident": ident,
            "rot": rot.reshape(P, -1), "sign": sign}


def decoder_layer(nc, t, out):
    ctx = ExitStack()
    with ctx:
        def sb(name, shape, dt=F32):
            return ctx.enter_context(nc.sbuf_tensor(name, shape, dt))

        def sem(name):
            return ctx.enter_context(nc.semaphore(name))

        PS = ctx.enter_context(nc.psum_tensor("PS", [P, 8, 512], F32))

        x_all = sb("x_all", [P, B * C, D])
        w_in = sb("w_in", [P, KD, WIN])
        w_out = sb("w_out", [P, MZ, D])
        conv_w = sb("conv_w", [P, MX, 4])
        norm_w = sb("norm_w", [P, MZ])
        d_bc = sb("d_bc", [P, H])
        dt_bias = sb("dt_bias", [P, 1])
        a_log = sb("a_log", [P, 1])
        sign = sb("sign", [P, 1])
        ident = sb("ident_sb", [P, P])
        decay_m = sb("decay_m", [P, NSLOT + 1, P])
        cb_m = sb("cb_m", [P, NM, P])
        ctxw = sb("ctxw", [P, E, KD, D])
        w3 = sb("w3", [P, KD, 2 * DK + 2 * DV])
        conv3_w = sb("conv3_w", [P, KD, 2])
        rw = sb("rw", [P, QH, QV, 2])
        w_out3 = sb("w_out3", [P, KD, D])
        rot = sb("rot_sb", [P, B, 2, QK])

        mask = sb("mask", [P, E, B * L], BF16)

        st = sb("st", [P, B * C, 6])
        mv = sb("mv", [P, B * C, 2])
        ve = sb("ve", [P, B * C])
        rs = sb("rs", [P, B * C])
        mhalf = sb("mhalf", [P, B * C])
        ones = sb("ones", [P, 1])
        avec = sb("avec", [P, 1])
        h_sb = sb("h_sb", [P, C, D])
        zT_all = sb("zT_all", [P, MZ, B * L])
        xs_all = sb("xs_all", [P, B * C, HID])
        cb_all = sb("cb_all", [P, B, C + 1, P])
        dtok_all = sb("dtok_all", [P, B * C, P])

        ARENA = 23936
        arena = sb("arena", [P, ARENA])

        def places(at, *shapes):
            views = []
            for shape in shapes:
                size = 1
                for n in shape:
                    size *= n
                assert at + size <= ARENA
                v = arena[:, at:at + size]
                names = "abcde"[:len(shape)]
                if len(shape) > 1:
                    v = v.rearrange(f"p ({' '.join(names)}) -> p {' '.join(names)}",
                                    **dict(zip(names[1:], shape[1:])))
                views.append(v)
                at += size
            return views

        hT_all, acc, xc, dt_raw, sp1, sp2 = places(
            0, (KD, B * L), (MX, L), (MX, L), (B * L,), (B * L,), (B * L,))
        ex_all, src = places(0, (B, NSLOT, C, H), (C, NS, HID))
        CHUNKS = B * NSLOT * C * H + C * NS * HID
        cbm, xsd, srcx, coefd, term, y, yzT, sq, junk, cbd, ms, rms = places(
            CHUNKS, (C, NM + 1, P), (C, HID), (HID,), (C, H), (2, HID), (C, HID), (C, MZ, P), (C, MZ, P),
            (P,), (C,), (C,), (C,))
        ids_f, ge_f = places(CHUNKS, (B * L,), (3, B * L // 2))
        ids = ids_f.bitcast(I32)
        ge = ge_f.bitcast(BF16)

        (h2, hm, sg, p, pm, h3, h3T_all, cacc, xc3, qk, q_rot, k_all, v_all, g_sb, ra, rb, vr,
         prod, pv, o, oc, osq, og, ogT, rwd, st2, mv2, ve2, rs2, delta, th, ind_all, cnt1, cnt0,
         sc, wl, eq, mu, var, rsh, nwt) = places(
            0, (C, D), (E, KD, L), (KD, L), (KD, L), (E, KD, L), (C, D), (B + 1, KD, L), (KD, L), (KD, L),
            (C, 2 * DK), (C, DK), (C, B, DK), (C, B, DV), (C, DV), (C, 2 * DK), (C, 2 * DK), (C, DV),
            (C, B, DK), (C, B, DV), (C, DV), (C, DV), (C, DV), (C, DV), (KD, L), (DV,),
            (C, 6), (C, 2), (C,), (C,), (C, QH), (C, QH), (C, B, QH), (C, QH), (C, QH),
            (C, QH), (C, B, QH), (C, B, QH), (C * QH,), (C * QH,), (C * QH,), (C * QH,))

        def after(b, per, k):
            return per * (b + 1) + k

        def before(b, per, k):
            return per * b + k

        sems = {}

        def counted(name, per):
            sems[name] = (sem(name), per)
            return sems[name][0]

        in_x, in_w1, in_small, in_const, in_ids, in_late = (sem(n) for n in
            ("in_x", "in_w1", "in_small", "in_const", "in_ids", "in_late"))
        v_setup = sem("v_setup")
        pool_setup = sem("pool_setup")
        w_out_ready = sem("w_out_ready")
        var_ready, rstd_ready = sem("var_ready"), sem("rstd_ready")
        h_ready = counted("h_ready", 1)
        hT_ps = counted("hT_ps", 1)
        hT_sb = counted("hT_sb", 1)
        xbc_ps = counted("xbc_ps", 3)
        z_ps = counted("z_ps", 1)
        dt_ps = counted("dt_ps", 1)
        tap3 = counted("tap3", 3)
        taps = counted("taps", 18)
        z_sb = counted("z_sb", 1)
        dt_sb = counted("dt_sb", 1)
        xc_ready = counted("xc_ready", 3)
        tok_ps = counted("tok_ps", 3)
        tok_sb = counted("tok_sb", 3)
        sp_act = sem("sp_act")
        sp_dve = sem("sp_dve")
        dtT_ready = sem("dtT_ready")
        dtok_ps, dtok_sb = sem("dtok_ps"), sem("dtok_sb")
        ex_ps = counted("ex_ps", 2)
        ex_sb = counted("ex_sb", 2)
        cbm_ready = counted("cbm_ready", 2)
        xsd_ready = counted("xsd_ready", 2)
        src0_ready = counted("src0_ready", 2)
        src1_ready = counted("src1_ready", 2)
        srcx_ready = counted("srcx_ready", 1)
        p_ps = counted("p_ps", NU)
        p_taken = counted("p_taken", NU)
        diag = counted("diag", 8)
        summed = counted("summed", NU)
        yT_ps = counted("yT_ps", 2)
        yz_ready = counted("yz_ready", 2)
        sq_ready = counted("sq_ready", 2)
        o1_ps = counted("o1_ps", 2)
        ms_ready = counted("ms_ready", 2)
        rms_ready = counted("rms_ready", 2)
        x1_ready = counted("x1_ready", 2)
        masks_ready = sem("masks_ready")
        ln2 = counted("ln2", 5)
        rs2_ready = counted("rs2_ready", 1)
        h2_ready = counted("h2_ready", 1)
        h2T_ps = counted("h2T_ps", 1)
        hm_ready = counted("hm_ready", 1)
        s_ps = counted("s_ps", 1)
        sg_ready = counted("sg_ready", 1)
        p_ready = counted("p_ready", 1)
        pm_ready = counted("pm_ready", 1)
        y2_ps = counted("y2_ps", 1)
        x2_ready = counted("x2_ready", 1)
        N3 = 31
        set3 = sem("set3")
        ln3 = counted("ln3", 5)
        rs3_ready = counted("rs3_ready", 1)
        h3_ready = counted("h3_ready", 1)
        h3T_ps = counted("h3T_ps", 1)
        h3T_sb = counted("h3T_sb", 1)
        conv3 = counted("conv3", 2)
        xc3_ready = counted("xc3_ready", 1)
        pr_ps = counted("pr_ps", 2)
        pr_sb = counted("pr_sb", 1)
        th_ready = counted("th_ready", 1)
        dl_ready = counted("dl_ready", 1)
        chain3 = counted("chain3", N3)
        osq_ready = counted("osq_ready", 1)
        hv_ready = counted("hv_ready", 1)
        og_ready = counted("og_ready", 1)
        ogT_ps = counted("ogT_ps", 1)
        ogT_sb = counted("ogT_sb", 1)
        o3_ps = counted("o3_ps", 1)
        out_ready = counted("out_ready", 1)
        stored = sem("stored")

        def tok(ap, b):
            return ap[..., bass.ts(b, L)]

        def heads(ap):
            return ap.rearrange("p (h d) -> p h d", d=PH)

        def over_head(ap):
            return ap.unsqueeze(2).broadcast_to([P, H, PH])

        block = ctx.enter_context(nc.Block())

        @block.sync
        def _(sp):
            sp.dma_start(x_all[:, :, :], t["x"].rearrange("b (c p) d -> p (b c) d", p=P)).then_inc(in_x, 16)
            sp.dma_start(ident[:, :], t["ident"]).then_inc(in_x, 16)
            sp.dma_start(w_in[:, :, :], t["w_in"].rearrange("(k p) n -> p k n", p=P)).then_inc(in_w1, 16)
            sp.dma_start(conv_w[:, :, :], t["conv_w"].rearrange("(m p) k -> p m k", p=P)).then_inc(in_w1, 16)
            sp.dma_start(dt_bias[:, :], t["dt_bias"]).then_inc(in_small, 16)
            sp.dma_start(a_log[:, :], t["a_log"]).then_inc(in_small, 16)
            sp.dma_start(sign[:, :], t["sign"]).then_inc(in_small, 16)
            sp.dma_start(norm_w[:, :], t["norm_w"].rearrange("(m p) -> p m", p=P), allow_slow_non_contiguous=True).then_inc(in_small, 16)
            sp.dma_start(d_bc[:, :], t["d"].partition_broadcast(P)).then_inc(in_small, 16)
            sp.dma_start(w_out[:, :, :], t["w_out"].rearrange("(m p) n -> p m n", p=P)).then_inc(in_small, 16)
            sp.dma_start(decay_m[:, :, :], t["decay_masks"].rearrange("p (s j) -> p s j", j=P)).then_inc(in_const, 16)
            sp.dma_start(cb_m[:, :, :], t["cb_masks"].rearrange("p (s j) -> p s j", j=P)).then_inc(in_const, 16)
            sp.dma_start(ids, t["ids"].rearrange("b l -> (b l)").partition_broadcast(P)).then_inc(in_ids, 16)
            sp.dma_start(ctxw[:, :, :, :], t["ctxT"].rearrange("e (k p) n -> p e k n", p=P)).then_inc(in_late, 16)
            sp.dma_start(w3[:, :, :], t["w3"].rearrange("(k p) n -> p k n", p=P)).then_inc(in_late, 16)
            sp.dma_start(conv3_w[:, :, :], t["conv3_w"].rearrange("(k p) w -> p k w", p=P)).then_inc(in_late, 16)
            sp.dma_start(rw[:, :, :, :], t["router_w"].partition_broadcast(P)).then_inc(in_late, 16)
            sp.dma_start(w_out3[:, :, :], t["w_out3"].rearrange("(k p) n -> p k n", p=P)).then_inc(in_late, 16)
            sp.dma_start(rot[:, :, :, :], t["rot"].rearrange("p (b s d) -> p b s d", b=B, s=2)).then_inc(in_late, 16)
            with sp.Fori(0, B) as b:
                sp.wait_ge(out_ready, after(b, 1, 1))
                sp.dma_start(out[bass.ds(b, 1)].rearrange("b (c p) d -> p (b c) d", p=P),
                             x_all[:, bass.ts(b, C), :]).then_inc(stored, 16)
            sp.wait_ge(stored, 16 * B)

        @block.tensor
        def _(pe):
            for name in ("hT_ps", "xbc_ps", "z_ps", "dt_ps", "tok_ps", "ex_ps", "p_ps", "yT_ps", "o1_ps",
                         "h2T_ps", "s_ps", "y2_ps", "h3T_ps", "pr_ps", "ogT_ps", "o3_ps"):
                pe.sem_inc(*sems[name])
            pe.wait_ge(in_x, 32)
            pe.wait_ge(in_w1, 32)
            with pe.Fori(0, B) as b:
                pe.wait_ge(tok_sb, before(b, 3, 3))
                pe.wait_ge(h_ready, after(b, 1, 1))
                for c in range(C):
                    for k in range(KD):
                        mm = pe.transpose(PS[:, 6, k * L + c * P:k * L + (c + 1) * P],
                                          h_sb[:, c, k * P:(k + 1) * P], ident[:, :])
                mm.then_inc(hT_ps, 1)
                pe.wait_ge(hT_sb, after(b, 1, 1))
                for q in range(MX // 2):
                    pe.wait_ge(taps, before(b, 18, 6 * q + 6))
                    for m in range(2):
                        for k in range(KD):
                            col = HID + (2 * q + m) * P
                            mm = pe.matmul(PS[:, 2 + q, m * L:(m + 1) * L], w_in[:, k, col:col + P],
                                           hT_all[:, k, bass.ts(b, L)], start=(k == 0), stop=(k == KD - 1))
                    mm.then_inc(xbc_ps, 1)
                pe.wait_ge(z_sb, before(b, 1, 1))
                for m in range(MZ):
                    for k in range(KD):
                        mm = pe.matmul(PS[:, m // 2, (m % 2) * L:(m % 2 + 1) * L], w_in[:, k, m * P:(m + 1) * P],
                                       hT_all[:, k, bass.ts(b, L)], start=(k == 0), stop=(k == KD - 1))
                mm.then_inc(z_ps, 1)
                for k in range(KD):
                    mm = pe.matmul(PS[:, 5, 0:L], w_in[:, k, WIN - P:WIN], hT_all[:, k, bass.ts(b, L)],
                                   start=(k == 0), stop=(k == KD - 1))
                mm.then_inc(dt_ps, 1)
                for c in range(C):
                    pe.wait_ge(xc_ready, after(b, 3, 2 + c))
                    for m in range(MZ):
                        mm = pe.transpose(PS[:, 7 - c, m * P:(m + 1) * P], xc[:, m, c * P:(c + 1) * P], ident[:, :])
                    mm.then_inc(tok_ps, 1)
                pe.wait_ge(dt_sb, after(b, 1, 1))
                for s, (cj, ci) in enumerate(((0, 0), (1, 1), (0, 1))):
                    mm = pe.matmul(PS[:, 5, s * P:(s + 1) * P], xc[:, MZ, cj * P:(cj + 1) * P],
                                   xc[:, MZ + 1, ci * P:(ci + 1) * P], start=True, stop=True)
                mm.then_inc(tok_ps, 1)

            pe.wait_ge(tok_sb, after(B - 1, 3, 3))
            pe.wait_ge(dtT_ready, 1)
            for i in range(B * C):
                mm = pe.transpose(PS[:, 6 + i // 4, (i % 4) * P:(i % 4 + 1) * P],
                                  dt_raw[:, i * P:(i + 1) * P], ident[:, :])
            mm.then_inc(dtok_ps, 1)
            pe.wait_ge(dtok_sb, 1)
            pe.wait_ge(in_const, 32)
            pe.wait_ge(w_out_ready, 1)
            pe.wait_ge(z_sb, after(B - 1, 1, 1))
            pe.wait_ge(taps, after(B - 1, 18, 18))

            def products(b, c, u0, levels):
                for u, lv in enumerate(levels, u0):
                    if u < 2:
                        pe.wait_ge(p_taken, before(b, NU, NU))
                    else:
                        pe.wait_ge(p_taken, after(b, NU, u - 1))
                    bank = PS[:, 4 + u % 2, :]
                    if lv == "seam":
                        pe.wait_ge(srcx_ready, after(b, 1, 1))
                        mm = pe.matmul(bank, cbm[:, 1, NM, :], srcx[:, :], start=True, stop=True)
                    elif lv == 0:
                        blk = LEVELS[0][1]
                        pe.wait_ge(src0_ready, after(b, C, c + 1))
                        for i in range(P // blk):
                            mm = pe.matmul(PS[i * blk:(i + 1) * blk, 4 + u % 2, :],
                                           cbm[:, c, 0, i * blk:(i + 1) * blk], src[:, c, max(i, 1) - 1, :],
                                           start=True, stop=True)
                    elif lv == NL - 1:
                        mm = pe.matmul(bank, cbm[:, c, NM - 1, :], xsd[:, c, :], start=True, stop=True)
                    else:
                        pe.wait_ge(src1_ready, after(b, C, c + 1))
                        slots = [s for s, (l, _) in enumerate(SRC) if l == lv]
                        for s in slots:
                            mm = pe.matmul(bank, cbm[:, c, CBM.index(SRC[s]), :], src[:, c, s, :],
                                           start=(s == slots[0]), stop=(s == slots[-1]))
                    mm.then_inc(p_ps, 1)

            with pe.Fori(0, B) as b:
                pe.wait_ge(ex_sb, before(b, 2, 2))
                EX = PS[:, 0:4, :].rearrange("p a (s c h) -> p (a s) c h", c=C, h=H)
                for s in range(SEAM):
                    mm = pe.matmul(EX[:, s], decay_m[:, s, :], dtok_all[:, bass.ts(b, C), H:2 * H],
                                   start=True, stop=True)
                    if s == NS - 1:
                        mm.then_inc(ex_ps, 1)
                for c in range(C):
                    mm = pe.matmul(EX[:, SEAM, c], decay_m[:, SEAM + c, :], dtok_all[:, b * C + c, H:2 * H],
                                   start=True, stop=True)
                mm.then_inc(ex_ps, 1)
                pe.wait_ge(cbm_ready, after(b, C, 1))
                pe.wait_ge(xsd_ready, after(b, C, 1))
                products(b, 0, 0, range(NL))
                pe.wait_ge(cbm_ready, after(b, C, 2))
                pe.wait_ge(xsd_ready, after(b, C, 2))
                products(b, 1, USES[0], ["seam", *range(NL)])
                for c in range(C):
                    pe.wait_ge(summed, after(b, NU, sum(USES[:c + 1])))
                    if c:
                        pe.wait_ge(yz_ready, after(b, C, c))
                    else:
                        pe.wait_ge(yz_ready, before(b, C, C))
                    for m in range(MZ):
                        mm = pe.transpose(PS[:, 6, m * P:(m + 1) * P], y[:, c, m * P:(m + 1) * P], ident[:, :])
                    mm.then_inc(yT_ps, 1)
                    pe.wait_ge(yz_ready, after(b, C, c + 1))
                    if c:
                        pe.wait_ge(x1_ready, after(b, C, c))
                    else:
                        pe.wait_ge(x1_ready, before(b, C, C))
                    for m in range(MZ):
                        pe.matmul(PS[:, 7, 0:D], yzT[:, c, m, :], w_out[:, m, :], start=(m == 0), stop=(m == MZ - 1))
                    pe.wait_ge(sq_ready, after(b, C, c + 1))
                    for m in range(MZ):
                        mm = pe.matmul(PS[:, 7, D:D + 1], sq[:, c, m, :], ones[:, :], start=(m == 0), stop=(m == MZ - 1))
                    mm.then_inc(o1_ps, 1)

            pe.wait_ge(in_late, 96)
            pe.wait_ge(ex_sb, after(B - 1, 2, 2))
            with pe.Fori(0, B) as b:
                pe.wait_ge(hm_ready, before(b, 1, 1))
                pe.wait_ge(h2_ready, after(b, 1, 1))
                for c in range(C):
                    for k in range(KD):
                        mm = pe.transpose(PS[:, 0, k * L + c * P:k * L + (c + 1) * P],
                                          h2[:, c, k * P:(k + 1) * P], ident[:, :])
                mm.then_inc(h2T_ps, 1)
                pe.wait_ge(hm_ready, after(b, 1, 1))
                pe.wait_ge(p_ready, before(b, 1, 1))
                for m in range(KD):
                    for e in range(E):
                        for k in range(KD):
                            mm = pe.matmul(PS[:, 1, m * L:(m + 1) * L], ctxw[:, e, k, m * P:(m + 1) * P],
                                           hm[:, e, k, :], start=(e == 0 and k == 0), stop=(e == E - 1 and k == KD - 1))
                mm.then_inc(s_ps, 1)
                pe.wait_ge(pm_ready, after(b, 1, 1))
                pe.wait_ge(x2_ready, before(b, 1, 1))
                for c in range(C):
                    for e in range(E):
                        for k in range(KD):
                            mm = pe.matmul(PS[:, 2, c * D:(c + 1) * D], pm[:, e, k, c * P:(c + 1) * P],
                                           ctxw[:, e, k, :], start=(e == 0 and k == 0), stop=(e == E - 1 and k == KD - 1))
                mm.then_inc(y2_ps, 1)

            pe.wait_ge(p_taken, after(B - 1, NU, NU))
            pe.wait_ge(yz_ready, after(B - 1, C, C))
            pe.wait_ge(x1_ready, after(B - 1, C, C))
            pe.wait_ge(hm_ready, after(B - 1, 1, 1))
            with pe.Fori(0, B) as b:
                pe.wait_ge(h3T_sb, before(b, 1, 1))
                pe.wait_ge(h3_ready, after(b, 1, 1))
                for c in range(C):
                    for k in range(KD):
                        mm = pe.transpose(PS[:, 3, k * L + c * P:k * L + (c + 1) * P],
                                          h3[:, c, k * P:(k + 1) * P], ident[:, :])
                mm.then_inc(h3T_ps, 1)
                pe.wait_ge(xc3_ready, after(b, 1, 1))
                pe.wait_ge(pr_sb, before(b, 1, 1))
                for c in range(C):
                    for k in range(KD):
                        pe.matmul(PS[:, 4 + c, :], xc3[:, k, c * P:(c + 1) * P], w3[:, k, 0:2 * DK + DV],
                                  start=(k == 0), stop=(k == KD - 1))
                    for k in range(KD):
                        mm = pe.matmul(PS[:, 6, c * DV:(c + 1) * DV], xc3[:, k, c * P:(c + 1) * P],
                                       w3[:, k, 2 * DK + DV:], start=(k == 0), stop=(k == KD - 1))
                    mm.then_inc(pr_ps, 1)
                pe.wait_ge(og_ready, after(b, 1, 1))
                pe.wait_ge(ogT_sb, before(b, 1, 1))
                for c in range(C):
                    for k in range(KD):
                        mm = pe.transpose(PS[:, 7, k * L + c * P:k * L + (c + 1) * P],
                                          og[:, c, k * P:(k + 1) * P], ident[:, :])
                mm.then_inc(ogT_ps, 1)
                pe.wait_ge(ogT_sb, after(b, 1, 1))
                pe.wait_ge(out_ready, before(b, 1, 1))
                for c in range(C):
                    for k in range(KD):
                        mm = pe.matmul(PS[:, 0, c * D:(c + 1) * D], ogT[:, k, c * P:(c + 1) * P], w_out3[:, k, :],
                                       start=(k == 0), stop=(k == KD - 1))
                mm.then_inc(o3_ps, 1)

        @block.scalar
        def _(act):
            for name in ("hT_sb", "tap3", "z_sb", "dt_sb", "xc_ready", "tok_sb", "ex_sb", "sq_ready",
                         "sg_ready", "h3T_sb", "xc3_ready", "pr_sb", "th_ready", "osq_ready", "ogT_sb"):
                act.sem_inc(*sems[name])
            act.wait_ge(in_w1, 32)
            act.wait_ge(in_small, 96)
            with act.Fori(0, B) as b:
                act.wait_ge(hT_ps, after(b, 1, 1))
                act.wait_ge(in_w1, 32)
                act.activation(tok(hT_all[:, :, :], b), PS[:, 6, :].rearrange("p (k t) -> p k t", k=KD), ACT.Copy)\
                   .then_inc(hT_sb, 1)
                for q in range(MX // 2):
                    act.wait_ge(xbc_ps, after(b, 3, q + 1))
                    act.wait_ge(xc_ready, before(b, 3, q + 1))
                    for m in range(2):
                        ins = act.activation(acc[:, 2 * q + m, :], PS[:, 2 + q, m * L:(m + 1) * L], ACT.Identity,
                                             scale=conv_w[:, 2 * q + m, 3:4])
                    ins.then_inc(tap3, 1)
                act.wait_ge(z_ps, after(b, 1, 1))
                act.wait_ge(in_w1, 32)
                act.activation(tok(zT_all[:, :, :], b), PS[:, 0:2, :].rearrange("p a (m t) -> p (a m) t", t=L),
                               ACT.Silu).then_inc(z_sb, 1)
                act.wait_ge(dt_ps, after(b, 1, 1))
                act.wait_ge(in_w1, 32)
                act.activation(tok(dt_raw[:, :], b), PS[:, 5, 0:L], ACT.Copy).then_inc(dt_sb, 1)
                act.wait_ge(tok_ps, before(b, 3, 3))
                for q in range(MX // 2):
                    act.wait_ge(taps, after(b, 18, 6 * q + 6))
                    act.activation(xc[:, 2 * q:2 * q + 2, :], acc[:, 2 * q:2 * q + 2, :], ACT.Silu)\
                       .then_inc(xc_ready, 1)
                for c in range(C):
                    act.wait_ge(tok_ps, after(b, 3, c + 1))
                    act.wait_ge(in_w1, 32)
                    act.activation(xs_all[:, b * C + c, :], PS[:, 7 - c, :], ACT.Copy).then_inc(tok_sb, 1)
                act.wait_ge(tok_ps, after(b, 3, 3))
                act.wait_ge(in_w1, 32)
                act.activation(cb_all[:, b, :, :], PS[:, 5, 0:3 * P].rearrange("p (s i) -> p s i", i=P), ACT.Copy)\
                   .then_inc(tok_sb, 1)

            act.wait_ge(dt_sb, after(B - 1, 1, 1))
            act.activation(sp1[:, :], dt_raw[:, :], ACT.Abs, bias=dt_bias[:, :]).then_inc(sp_act, 1)
            act.wait_ge(sp_act, 1)
            act.activation(sp2[:, :], sp1[:, :], ACT.Exp, scale=-1.0).then_inc(sp_act, 1)
            act.activation(avec[:, :], a_log[:, :], ACT.Exp).then_inc(sp_act, 1)
            act.wait_ge(sp_act, 2)
            act.activation(sp1[:, :], sp2[:, :], ACT.Ln, bias=1.0).then_inc(sp_act, 1)
            act.wait_ge(dtok_ps, 1)
            act.activation(dtok_all[:, :, :], PS[:, 6:8, :].rearrange("p a (s h) -> p (a s) h", h=P), ACT.Copy)\
               .then_inc(dtok_sb, 1)

            EX = PS[:, 0:4, :].rearrange("p a (s c h) -> p (a s) (c h)", c=C, h=H)
            with act.Fori(0, B) as b:
                ex = ex_all[:, b, :, :, :].rearrange("p s c h -> p s (c h)")
                act.wait_ge(ex_ps, after(b, 2, 1))
                act.wait_ge(in_w1, 32)
                act.activation(ex[:, 0:NS], EX[:, 0:NS], ACT.Exp).then_inc(ex_sb, 1)
                act.wait_ge(ex_ps, after(b, 2, 2))
                act.wait_ge(in_w1, 32)
                act.activation(ex[:, NS:NSLOT], EX[:, NS:NSLOT], ACT.Exp).then_inc(ex_sb, 1)
                for c in range(C):
                    act.wait_ge(o1_ps, before(b, C, C))
                    act.wait_ge(yz_ready, after(b, C, c + 1))
                    act.activation(sq[:, c, :, :], yzT[:, c, :, :], ACT.Square).then_inc(sq_ready, 1)

            with act.Fori(0, B) as b:
                act.wait_ge(p_ready, before(b, 1, 1))
                act.wait_ge(s_ps, after(b, 1, 1))
                act.activation(sg[:, :, :], PS[:, 1, :].rearrange("p (k t) -> p k t", k=KD), ACT.Silu)\
                   .then_inc(sg_ready, 1)

            with act.Fori(0, B) as b:
                act.wait_ge(h3T_ps, after(b, 1, 1))
                act.wait_ge(set3, 1)
                act.activation(h3T_all[:, b + 1, :, :], PS[:, 3, :].rearrange("p (k t) -> p k t", k=KD), ACT.Copy)\
                   .then_inc(h3T_sb, 1)
                act.wait_ge(pr_ps, before(b, C, C))
                act.wait_ge(conv3, after(b, 2, 2))
                act.activation(xc3[:, :, :], cacc[:, :, :], ACT.Silu).then_inc(xc3_ready, 1)
                act.wait_ge(og_ready, before(b, 1, 1))
                act.wait_ge(pr_ps, after(b, C, C))
                act.activation(qk[:, :, 0:DK], PS[:, 4:6, 0:DK], ACT.Silu)
                act.activation(qk[:, :, DK:2 * DK], PS[:, 4:6, DK:2 * DK], ACT.Copy)
                act.activation(g_sb[:, :, :], PS[:, 6, :].rearrange("p (c n) -> p c n", c=C), ACT.Silu)
                act.activation(v_all[:, :, b, :], PS[:, 4:6, 2 * DK:2 * DK + DV], ACT.Copy).then_inc(pr_sb, 1)
                act.wait_ge(dl_ready, after(b, 1, 1))
                act.activation(th[:, :, :], delta[:, :, :], ACT.Tanh, scale=0.5).then_inc(th_ready, 1)
                act.wait_ge(hv_ready, after(b, 1, 1))
                act.activation(osq[:, :, :], oc[:, :, :], ACT.Square).then_inc(osq_ready, 1)
                act.wait_ge(o3_ps, before(b, 1, 1))
                act.wait_ge(ogT_ps, after(b, 1, 1))
                act.activation(ogT[:, :, :], PS[:, 7, :].rearrange("p (k t) -> p k t", k=KD), ACT.Copy)\
                   .then_inc(ogT_sb, 1)

        @block.gpsimd
        def _(pool):
            for name in ("cbm_ready", "src0_ready", "rms_ready", "rs2_ready", "rs3_ready"):
                pool.sem_inc(*sems[name])
            pool.memset(mhalf[:, :], -0.5).then_inc(pool_setup, 1)
            pool.wait_ge(var_ready, 1)
            pool.wait_ge(pool_setup, 1)
            pool.tensor_tensor(rs[:, :], ve[:, :], mhalf[:, :], ALU.pow).then_inc(rstd_ready, 1)
            pool.wait_ge(in_ids, 16)
            per = VOCAB // E
            for i in range(E - 1):
                pool.tensor_scalar(ge[:, i, :], ids, float(per * (i + 1)), None, ALU.is_ge).then_inc(pool_setup, 1)
            pool.wait_ge(pool_setup, E)
            pool.tensor_scalar(mask[:, 0, :], ge[:, 0, :], -1.0, 1.0, ALU.mult, ALU.add)
            for i in range(1, E - 1):
                pool.tensor_tensor(mask[:, i, :], ge[:, i - 1, :], ge[:, i, :], ALU.subtract)
            pool.tensor_copy(mask[:, E - 1, :], ge[:, E - 2, :]).then_inc(masks_ready, 1)

            pool.wait_ge(masks_ready, 1)
            pool.wait_ge(in_const, 32)
            pool.wait_ge(tok_sb, after(B - 1, 3, 3))
            with pool.Fori(0, B) as b:
                for c in range(C):
                    pool.wait_ge(yT_ps, before(b, C, c + 1))
                    pool.wait_ge(in_const, 32)
                    if c:
                        pool.tensor_copy(cbm[:, 1, NM, :], cb_all[:, b, C, :])
                    pool.tensor_tensor(cbm[:, c, 0:NM, :], cb_m[:, :, :],
                                       cb_all[:, b, c, :].unsqueeze(1).broadcast_to([P, NM, P]), ALU.mult)\
                        .then_inc(cbm_ready, 1)
                    pool.wait_ge(ex_sb, after(b, 2, 1))
                    pool.wait_ge(xsd_ready, after(b, C, c + 1))
                    pool.wait_ge(in_const, 32)
                    n0 = sum(lv == 0 for lv, _ in SRC)
                    for s in range(n0):
                        ins = pool.tensor_tensor(heads(src[:, c, s, :]), heads(xsd[:, c, :]),
                                                 over_head(ex_all[:, b, s, c, :]), ALU.mult)
                    ins.then_inc(src0_ready, 1)
                for c in range(C):
                    pool.wait_ge(ms_ready, after(b, C, c + 1))
                    pool.tensor_tensor(rms[:, c:c + 1], ms[:, c:c + 1], mhalf[:, 0:1], ALU.pow).then_inc(rms_ready, 1)

            with pool.Fori(0, B) as b:
                pool.wait_ge(ln2, after(b, 5, 5))
                pool.tensor_tensor(rs2[:, :], ve2[:, :], mhalf[:, 0:C], ALU.pow).then_inc(rs2_ready, 1)
            with pool.Fori(0, B) as b:
                pool.wait_ge(ln3, after(b, 5, 5))
                pool.tensor_tensor(rs2[:, :], ve2[:, :], mhalf[:, 0:C], ALU.pow).then_inc(rs3_ready, 1)

        @block.vector
        def _(dve):
            for name in ("h_ready", "taps", "xsd_ready", "src1_ready", "srcx_ready", "diag", "p_taken", "summed",
                         "yz_ready", "ms_ready", "x1_ready", "ln2", "h2_ready", "hm_ready", "p_ready", "pm_ready",
                         "x2_ready", "ln3", "h3_ready", "conv3", "dl_ready", "chain3", "hv_ready",
                         "og_ready", "out_ready"):
                dve.sem_inc(*sems[name])
            dve.memset(ones[:, :], 1.0)
            dve.wait_ge(in_x, 32)
            for i in range(B * C):
                dve.bn_stats(st[:, i, :], x_all[:, i, :]).then_inc(v_setup, 1)
            for i in range(B * C):
                dve.wait_ge(v_setup, i + 1)
                ins = dve.bn_aggr(mv[:, i, :], st[:, i, :])
            ins.then_inc(v_setup, 1)
            dve.wait_ge(v_setup, B * C + 1)
            dve.tensor_scalar(ve[:, :], mv[:, :, 1], EPS, None, ALU.add).then_inc(var_ready, 1)
            dve.wait_ge(rstd_ready, 1)
            dve.wait_ge(in_w1, 32)
            with dve.Fori(0, B) as b:
                dve.wait_ge(hT_ps, before(b, 1, 1))
                for c in range(C):
                    i = b * C + c
                    ins = dve.tensor_scalar(h_sb[:, c, :], x_all[:, i, :], mv[:, i, 0:1], rs[:, bass.ds(i, 1)],
                                            ALU.subtract, ALU.mult)
                ins.then_inc(h_ready, 1)
                for q in range(MX // 2):
                    dve.wait_ge(tap3, after(b, 3, q + 1))
                    for tap in range(1, 4):
                        for m in range(2):
                            n = 6 * q + 2 * (tap - 1) + m
                            if tap > 1:
                                dve.wait_ge(taps, after(b, 18, n - 1))
                            dve.scalar_tensor_tensor(acc[:, 2 * q + m, tap:], PS[:, 2 + q, m * L:(m + 1) * L - tap],
                                                     conv_w[:, 2 * q + m, 3 - tap:4 - tap], acc[:, 2 * q + m, tap:],
                                                     ALU.mult, ALU.add).then_inc(taps, 1)

            dve.wait_ge(sp_act, 1)
            dve.wait_ge(dt_sb, after(B - 1, 1, 1))
            dve.tensor_scalar(dt_raw[:, :], dt_raw[:, :], dt_bias[:, :], 0.0, ALU.add, ALU.max).then_inc(v_setup, 1)
            dve.wait_ge(sp_act, 4)
            dve.tensor_tensor(avec[:, :], avec[:, :], sign[:, :], ALU.mult).then_inc(v_setup, 1)
            dve.wait_ge(v_setup, B * C + 3)
            dve.tensor_tensor(dt_raw[:, :], dt_raw[:, :], sp1[:, :], ALU.add).then_inc(v_setup, 1)
            dve.wait_ge(v_setup, B * C + 4)
            dve.tensor_scalar(dt_raw[:, :], dt_raw[:, :], avec[:, :], None, ALU.mult).then_inc(dtT_ready, 1)
            for m in range(MZ):
                ins = dve.tensor_scalar(w_out[:, m, :], w_out[:, m, :], norm_w[:, m:m + 1], None, ALU.mult)
            ins.then_inc(w_out_ready, 1)

            dve.wait_ge(masks_ready, 1)
            dve.wait_ge(dtok_sb, 1)

            def take(b, c, u0, levels):
                for u, lv in enumerate(levels, u0):
                    slot = SEAM if lv == "seam" else NS + lv
                    dve.wait_ge(p_ps, after(b, NU, u + 1))
                    if u >= 2:
                        dve.wait_ge(summed, after(b, NU, u - 1))
                    dve.tensor_tensor(heads(term[:, u % 2, :]), heads(PS[:, 4 + u % 2, :]),
                                      over_head(ex_all[:, b, slot, c, :]), ALU.mult).then_inc(p_taken, 1)
                    dve.wait_ge(p_taken, after(b, NU, u + 1))
                    if u > u0:
                        dve.wait_ge(summed, after(b, NU, u))
                    dve.tensor_tensor(y[:, c, :], y[:, c, :], term[:, u % 2, :], ALU.add).then_inc(summed, 1)

            with dve.Fori(0, B) as b:
                for c in range(C):
                    i = b * C + c
                    dve.wait_ge(yT_ps, before(b, C, c + 1))
                    dve.tensor_tensor(heads(xsd[:, c, :]), heads(xs_all[:, i, :]), over_head(dtok_all[:, i, 0:H]),
                                      ALU.mult).then_inc(xsd_ready, 1)
                    dve.tensor_tensor(junk, cb_all[:, b, c, :], ident[:, :], ALU.mult).then_inc(diag, 1)
                    dve.wait_ge(diag, after(b, 8, 4 * c + 1))
                    dve.tensor_reduce(cbd[:, c:c + 1], junk, AX_X, ALU.add).then_inc(diag, 1)
                    dve.wait_ge(diag, after(b, 8, 4 * c + 2))
                    dve.scalar_tensor_tensor(coefd[:, c, :], dtok_all[:, i, 0:H], cbd[:, c:c + 1], d_bc[:, :],
                                             ALU.mult, ALU.add).then_inc(diag, 1)
                    dve.wait_ge(diag, after(b, 8, 4 * c + 3))
                    dve.tensor_tensor(heads(y[:, c, :]), heads(xs_all[:, i, :]), over_head(coefd[:, c, :]),
                                      ALU.mult).then_inc(diag, 1)
                    dve.wait_ge(xsd_ready, after(b, C, c + 1))
                    n0 = sum(lv == 0 for lv, _ in SRC)
                    dve.wait_ge(ex_sb, after(b, 2, 1))
                    for s in range(n0, NS):
                        ins = dve.tensor_tensor(heads(src[:, c, s, :]), heads(xsd[:, c, :]),
                                                over_head(ex_all[:, b, s, c, :]), ALU.mult)
                    ins.then_inc(src1_ready, 1)
                    if c == 0:
                        dve.wait_ge(ex_sb, after(b, 2, 2))
                        dve.tensor_tensor(heads(srcx), heads(xsd[:, 0, :]), over_head(ex_all[:, b, SEAM, 0, :]),
                                          ALU.mult).then_inc(srcx_ready, 1)
                dve.wait_ge(diag, after(b, 8, 8))
                take(b, 0, 0, range(NL))
                take(b, 1, USES[0], ["seam", *range(NL)])
                for c in range(C):
                    i = b * C + c
                    dve.wait_ge(yT_ps, after(b, C, c + 1))
                    dve.tensor_tensor(yzT[:, c, :, :], PS[:, 6, :].rearrange("p (m t) -> p m t", m=MZ),
                                      zT_all[:, :, bass.ds(i * P, P)], ALU.mult).then_inc(yz_ready, 1)
                    dve.wait_ge(o1_ps, after(b, C, c + 1))
                    dve.tensor_scalar(ms[:, c:c + 1], PS[:, 7, D:D + 1], 1.0 / HID, EPS, ALU.mult, ALU.add)\
                        .then_inc(ms_ready, 1)
                    dve.wait_ge(rms_ready, after(b, C, c + 1))
                    dve.scalar_tensor_tensor(x_all[:, i, :], PS[:, 7, 0:D], rms[:, c:c + 1], x_all[:, i, :],
                                             ALU.mult, ALU.add).then_inc(x1_ready, 1)

            def layer_norm(b, chain, rstd, done, dst):
                for c in range(C):
                    dve.bn_stats(st2[:, c, :], x_all[:, b * C + c, :]).then_inc(chain, 1)
                dve.wait_ge(chain, after(b, 5, 2))
                dve.memset(ve2[:, :], EPS)
                for c in range(C):
                    dve.bn_aggr(mv2[:, c, :], st2[:, c, :]).then_inc(chain, 1)
                dve.wait_ge(chain, after(b, 5, 4))
                dve.tensor_tensor(ve2[:, :], mv2[:, :, 1], ve2[:, :], ALU.add).then_inc(chain, 1)
                dve.wait_ge(rstd, after(b, 1, 1))
                for c in range(C):
                    ins = dve.tensor_scalar(dst[:, c, :], x_all[:, b * C + c, :], mv2[:, c, 0:1], rs2[:, c:c + 1],
                                            ALU.subtract, ALU.mult)
                ins.then_inc(done, 1)

            dve.wait_ge(x1_ready, after(B - 1, C, C))
            with dve.Fori(0, B) as b:
                layer_norm(b, ln2, rs2_ready, h2_ready, h2)
                dve.wait_ge(h2T_ps, after(b, 1, 1))
                for e in range(E):
                    ins = dve.tensor_tensor(hm[:, e, :, :], PS[:, 0, :].rearrange("p (k t) -> p k t", k=KD),
                                            mask[:, e, bass.ts(b, L)].unsqueeze(1).broadcast_to([P, KD, L]), ALU.mult)
                ins.then_inc(hm_ready, 1)
                dve.wait_ge(sg_ready, after(b, 1, 1))
                dve.tensor_tensor(p[:, :, :], PS[:, 1, :].rearrange("p (k t) -> p k t", k=KD), sg[:, :, :],
                                  ALU.mult).then_inc(p_ready, 1)
                dve.wait_ge(p_ready, after(b, 1, 1))
                for e in range(E):
                    ins = dve.tensor_tensor(pm[:, e, :, :], p[:, :, :],
                                            mask[:, e, bass.ts(b, L)].unsqueeze(1).broadcast_to([P, KD, L]), ALU.mult)
                ins.then_inc(pm_ready, 1)
                dve.wait_ge(y2_ps, after(b, 1, 1))
                dve.tensor_tensor(x_all[:, bass.ts(b, C), :], PS[:, 2, :].rearrange("p (c n) -> p c n", c=C),
                                  x_all[:, bass.ts(b, C), :], ALU.add).then_inc(x2_ready, 1)

            dve.wait_ge(x2_ready, after(B - 1, 1, 1))
            dve.wait_ge(in_late, 96)
            for z in (h3T_all[:, 0, :, :], k_all, v_all, ind_all, cnt1, cnt0):
                dve.memset(z, 0.0)
            dve.tensor_tensor(rwd.rearrange("p (h d) -> p h d", h=QH), rw[:, :, :, 1], rw[:, :, :, 0],
                              ALU.subtract).then_inc(set3, 1)
            dve.wait_ge(set3, 1)
            with dve.Fori(0, B) as b:
                n = [0]

                def link(ins):
                    n[0] += 1
                    ins.then_inc(chain3, 1)
                    dve.wait_ge(chain3, after(b, N3, n[0]))

                layer_norm(b, ln3, rs3_ready, h3_ready, h3)
                dve.wait_ge(h3T_sb, after(b, 1, 1))
                for k in range(KD):
                    ins = dve.tensor_scalar(cacc[:, k, :], h3T_all[:, b, k, :], conv3_w[:, k, 0:1], None, ALU.mult)
                ins.then_inc(conv3, 1)
                dve.wait_ge(conv3, after(b, 2, 1))
                for k in range(KD):
                    ins = dve.scalar_tensor_tensor(cacc[:, k, :], h3T_all[:, b + 1, k, :], conv3_w[:, k, 1:2],
                                                   cacc[:, k, :], ALU.mult, ALU.add)
                ins.then_inc(conv3, 1)
                dve.wait_ge(pr_sb, after(b, 1, 1))
                link(dve.tensor_tensor(vr[:, :, :], v_all[:, :, b, :], rwd.unsqueeze(1).broadcast_to([P, C, DV]),
                                       ALU.mult))
                dve.tensor_reduce(delta[:, :, :], vr.rearrange("p c (h d) -> p c h d", d=QV), AX_X, ALU.add)\
                    .then_inc(dl_ready, 1)
                half = QK // 2
                qkh = qk.rearrange("p c (h d) -> p (c h) d", d=QK)
                rbh = rb.rearrange("p c (h d) -> p (c h) d", d=QK)
                rah = ra.rearrange("p c (h d) -> p (c h) d", d=QK)
                n_heads = C * 2 * QH
                dve.tensor_tensor(rah, qkh, rot[:, b, 0, :].unsqueeze(1).broadcast_to([P, n_heads, QK]), ALU.mult)
                dve.tensor_tensor(rbh[:, :, 0:half], qkh[:, :, half:QK],
                                  rot[:, b, 1, 0:half].unsqueeze(1).broadcast_to([P, n_heads, half]), ALU.mult)
                link(dve.tensor_tensor(rbh[:, :, half:QK], qkh[:, :, 0:half],
                                       rot[:, b, 1, half:QK].unsqueeze(1).broadcast_to([P, n_heads, half]), ALU.mult))
                dve.tensor_tensor(q_rot[:, :, :], ra[:, :, 0:DK], rb[:, :, 0:DK], ALU.add)
                dve.tensor_tensor(k_all[:, :, b, :], ra[:, :, DK:2 * DK], rb[:, :, DK:2 * DK], ALU.add)
                link(dve.tensor_scalar(ind_all[:, :, b, :], delta[:, :, :], 0.0, None, ALU.is_gt))
                dve.tensor_tensor(cnt1[:, :, :], cnt1[:, :, :], ind_all[:, :, b, :], ALU.add)
                link(dve.scalar_tensor_tensor(cnt0[:, :, :], cnt0[:, :, :], 1.0, ind_all[:, :, b, :],
                                              ALU.add, ALU.subtract))
                link(dve.tensor_tensor(sc[:, :, :], cnt1[:, :, :], cnt0[:, :, :], ALU.subtract))
                link(dve.tensor_tensor(sc[:, :, :], sc[:, :, :], ind_all[:, :, b, :], ALU.mult))
                link(dve.tensor_tensor(sc[:, :, :], sc[:, :, :], cnt0[:, :, :], ALU.add))
                link(dve.reciprocal(sc[:, :, :], sc[:, :, :]))
                dve.wait_ge(th_ready, after(b, 1, 1))
                link(dve.scalar_tensor_tensor(delta[:, :, :], th[:, :, :], -1.0, th[:, :, :], ALU.mult, ALU.max))
                scale = float(QK) ** -0.5
                link(dve.tensor_scalar(delta[:, :, :], delta[:, :, :], 0.5 * scale, 0.5 * scale, ALU.mult, ALU.add))
                link(dve.tensor_tensor(sc[:, :, :], sc[:, :, :], delta[:, :, :], ALU.mult))
                dve.tensor_tensor(eq[:, :, :, :], ind_all[:, :, :, :],
                                  ind_all[:, :, b, :].unsqueeze(2).broadcast_to([P, C, B, QH]), ALU.is_equal)
                link(dve.tensor_tensor(prod[:, :, :, :], k_all[:, :, :, :],
                                       q_rot.unsqueeze(2).broadcast_to([P, C, B, DK]), ALU.mult))
                link(dve.tensor_reduce(wl.rearrange("p c m h -> p (c m h)"),
                                       prod.rearrange("p c m (h d) -> p (c m h) d", d=QK), AX_X, ALU.add))
                link(dve.tensor_tensor(wl[:, :, :, :], wl[:, :, :, :], eq[:, :, :, :], ALU.mult))
                link(dve.tensor_tensor(wl[:, :, :, :], wl[:, :, :, :],
                                       sc.unsqueeze(2).broadcast_to([P, C, B, QH]), ALU.mult))
                link(dve.tensor_tensor(pv.rearrange("p c m (h d) -> p (c m h) d", d=QV),
                                       v_all.rearrange("p c m (h d) -> p (c m h) d", d=QV),
                                       wl.rearrange("p c m h -> p (c m h)").unsqueeze(2)
                                         .broadcast_to([P, C * B * QH, QV]), ALU.mult))
                link(dve.tensor_reduce(o[:, :, :], pv.rearrange("p c m n -> p c n m"), AX_X, ALU.add))
                oh = o.rearrange("p c (h d) -> p (c h) d", d=QV)
                och = oc.rearrange("p c (h d) -> p (c h) d", d=QV)

                def over_value(ap):
                    return ap.unsqueeze(2).broadcast_to([P, C * QH, QV])

                link(dve.tensor_reduce(mu, oh, AX_X, ALU.add))
                dve.scalar_tensor_tensor(och, over_value(mu), -1.0 / QV, oh, ALU.mult, ALU.add).then_inc(hv_ready, 1)
                dve.wait_ge(osq_ready, after(b, 1, 1))
                link(dve.tensor_reduce(var, osq.rearrange("p c (h d) -> p (c h) d", d=QV), AX_X, ALU.add))
                link(dve.tensor_scalar(var, var, 1.0 / QV, EPS, ALU.mult, ALU.add))
                link(dve.tensor_scalar(rsh.bitcast(I32), var.bitcast(I32), -0.5, float(0x5F3759DF),
                                       ALU.mult, ALU.add))
                for _ in range(3):
                    link(dve.scalar_tensor_tensor(nwt, rsh, -0.5, rsh, ALU.mult, ALU.mult))
                    link(dve.tensor_tensor(nwt, nwt, var, ALU.mult))
                    link(dve.scalar_tensor_tensor(rsh, nwt, 1.5, rsh, ALU.add, ALU.mult))
                link(dve.tensor_tensor(och, och, over_value(rsh), ALU.mult))
                assert n[0] == N3, n
                dve.tensor_tensor(og[:, :, :], oc[:, :, :], g_sb[:, :, :], ALU.mult).then_inc(og_ready, 1)
                dve.wait_ge(o3_ps, after(b, 1, 1))
                dve.tensor_tensor(x_all[:, bass.ts(b, C), :], PS[:, 0, :].rearrange("p (c n) -> p c n", c=C),
                                  x_all[:, bass.ts(b, C), :], ALU.add).then_inc(out_ready, 1)


_INS = {
    "x": (B, L, D), "w_in": (D, WIN), "conv_w": (MX * P, 4), "dt_bias": (P, 1), "a_log": (P, 1), "d": (H,),
    "norm_w": (HID,), "w_out": (HID, D), "ids": (B, L), "ctxT": (E, D, D), "w3": (D, 2 * DK + 2 * DV),
    "conv3_w": (D, 2), "router_w": (QH, QV, 2), "w_out3": (D, D),
}


def kernel(x, itok_BxS_13_99985, ctx_2048, L0_attn_W_in, L0_attn_conv_w, L0_attn_dt_bias, L0_attn_A_log, L0_attn_D,
           L0_attn_norm_w, L0_attn_W_out, L0_ffn_conv_w, L0_ffn_Wq, L0_ffn_Wk, L0_ffn_Wv, L0_ffn_Wg,
           L0_ffn_router_w, L0_ffn_Wout):
    import numpy as np
    import concourse.bacc as bacc
    from concourse.bass_utils import run_bass_kernel_spmd

    w_in = np.asarray(L0_attn_W_in).T
    dt_bias = np.asarray(L0_attn_dt_bias)
    a_log = np.asarray(L0_attn_A_log)
    arrays = {
        "x": x, "w_in": np.concatenate([w_in, w_in[:, -H:]], 1), "conv_w": L0_attn_conv_w,
        "dt_bias": np.concatenate([dt_bias, dt_bias])[:, None],
        "a_log": np.concatenate([np.zeros_like(a_log), a_log])[:, None],
        "d": L0_attn_D, "norm_w": L0_attn_norm_w, "w_out": np.asarray(L0_attn_W_out).T, "ids": itok_BxS_13_99985,
        "ctxT": np.asarray(ctx_2048).transpose(0, 2, 1),
        "w3": np.concatenate([np.asarray(w) for w in (L0_ffn_Wq, L0_ffn_Wk, L0_ffn_Wv, L0_ffn_Wg)], 1),
        "conv3_w": L0_ffn_conv_w, "router_w": L0_ffn_router_w, "w_out3": L0_ffn_Wout,
    }
    arrays = {k: np.ascontiguousarray(v) for k, v in arrays.items()}
    assert all(arrays[k].shape == s for k, s in _INS.items())
    arrays |= shape_constants()
    nc = bacc.Bacc("TRN2", target_bir_lowering=False, num_devices=1)
    t = {k: nc.dram_tensor(f"in_{k}", a.shape, mybir.dt.from_np(a.dtype), kind="ExternalInput").ap()
         for k, a in arrays.items()}
    out = nc.dram_tensor("out", (B, L, D), F32, kind="ExternalOutput").ap()
    decoder_layer(nc, t, out)
    r = run_bass_kernel_spmd(nc, [{f"in_{k}": a for k, a in arrays.items()}], core_ids=[0])
    return r.results[0]["out"]
```

```python
from contextlib import ExitStack

import concourse.bass as bass
from concourse import mybir

ALU = mybir.AluOpType
ACT = mybir.ActivationFunctionType
F32 = mybir.dt.float32
I32 = mybir.dt.int32
BF16 = mybir.dt.bfloat16
AX_X = mybir.AxisListType.X

P = 128
B, L, D = 4, 256, 256
C = L // P
KD = D // P
HID, H, PH, N = 512, 64, 8, 128
MZ = HID // P
MX = (HID + 2 * N) // P
WIN = HID + MX * P + P
E = 4
VOCAB = 12500
EPS = 1e-5
QH, QK, QV = 16, 8, 16
DK, DV = 128, 256
PAIR_AT = [sum(B - d for d in range(lag)) for lag in range(B)]
NPAIR = sum(B - d for d in range(B))

LEVELS = [(128, 32), (32, 8), (8, 4), (4, 2), (2, 1)]
NL = len(LEVELS)
SRC = [(lv, i) for lv, (par, blk) in enumerate(LEVELS[:-1]) for i in range(1, par // blk)]
NS = len(SRC)
SEAM = NS + NL
NSLOT = SEAM + 1
CBM = [(0, 0)] + [x for x in SRC if x[0] > 0] + [(NL - 1, 1)]
NM = len(CBM)
USES = [NL, NL + 1]
NU = sum(USES)
NTERM = NU + C


def shape_constants():
    import numpy as np
    t = np.arange(P)
    k, j = t[:, None], t[None, :]
    decay = np.zeros((P, NSLOT + 1, P), np.float32)
    for s, (lv, i) in enumerate(SRC):
        par, blk = LEVELS[lv]
        start = (j // par) * par + i * blk
        decay[:, s] = (k // par == j // par) & (k > j) & (k < start)
    for lv, (par, blk) in enumerate(LEVELS):
        decay[:, NS + lv] = (k // blk == j // blk) & (k <= j)
    decay[:, SEAM] = k > j
    decay[:, SEAM + 1] = k <= j
    cb = np.zeros((P, NM, P), np.float32)
    src, tgt = t[:, None], t[None, :]
    cb[:, 0] = src < (tgt // LEVELS[0][1]) * LEVELS[0][1]
    for m, (lv, i) in enumerate(CBM):
        if m:
            par, blk = LEVELS[lv]
            cb[:, m] = (src // par == tgt // par) & ((tgt % par) // blk == i) & (src % par < i * blk)
    ident = np.eye(P, dtype=np.float32)
    inv_freq = (1.0 / np.float32(10000.0) ** (np.arange(0, QK, 2, dtype=np.float32) / np.float32(QK))).astype(np.float32)
    ang = np.arange(B, dtype=np.float32)[:, None] * inv_freq[None, :]
    cos, sin = np.cos(ang), np.sin(ang)
    rot = np.zeros((P, B, 2, QK), np.float32)
    rot[:, :, 0] = np.concatenate([cos, cos], 1)[None]
    rot[:, :, 1] = np.concatenate([-sin, sin], 1)[None]
    sign = np.ones((P, 1), np.float32)
    sign[P // 2:] = -1.0
    return {"decay_masks": decay.reshape(P, -1), "cb_masks": cb.reshape(P, -1), "ident": ident,
            "rot": rot.reshape(P, -1), "sign": sign}


def decoder_layer(nc, t, out):
    ctx = ExitStack()
    with ctx:
        def sb(name, shape, dt=F32):
            return ctx.enter_context(nc.sbuf_tensor(name, shape, dt))

        def sem(name):
            return ctx.enter_context(nc.semaphore(name))

        PS = ctx.enter_context(nc.psum_tensor("PS", [P, 8, 512], F32))

        x_all = sb("x_all", [P, B * C, D])
        w_out = sb("w_out", [P, MZ, D])
        conv_w = sb("conv_w", [P, MX, 4])
        norm_w = sb("norm_w", [P, MZ])
        d_bc = sb("d_bc", [P, H])
        dt_bias = sb("dt_bias", [P, 1])
        a_log = sb("a_log", [P, 1])
        sign = sb("sign", [P, 1])
        ident = sb("ident_sb", [P, P])
        decay_m = sb("decay_m", [P, NSLOT + 1, P])
        cb_m = sb("cb_m", [P, NM, P])
        ctxw = sb("ctxw", [P, E, KD, D])
        w3 = sb("w3", [P, KD, 2 * DK + 2 * DV])
        conv3_w = sb("conv3_w", [P, KD, 2])
        rw = sb("rw", [P, QH, QV, 2])
        w_out3 = sb("w_out3", [P, KD, D])
        rot = sb("rot_sb", [P, B, 2, QK])

        mask = sb("mask", [P, E, B * L], BF16)

        st = sb("st", [P, B * C, 6])
        mv = sb("mv", [P, B * C, 2])
        ve = sb("ve", [P, B * C])
        rs = sb("rs", [P, B * C])
        mhalf = sb("mhalf", [P, B * C])
        ones = sb("ones", [P, 1])
        avec = sb("avec", [P, 1])
        zT_all = sb("zT_all", [P, MZ, B * L])
        xs_all = sb("xs_all", [P, B * C, HID])
        cb_all = sb("cb_all", [P, B, C + 1, P])
        dtok_all = sb("dtok_all", [P, B * C, P])

        ARENA = 28100
        arena = sb("arena", [P, ARENA])

        def places(at, *shapes):
            views = []
            for shape in shapes:
                size = 1
                for n in shape:
                    size *= n
                assert at + size <= ARENA
                v = arena[:, at:at + size]
                names = "abcde"[:len(shape)]
                if len(shape) > 1:
                    v = v.rearrange(f"p ({' '.join(names)}) -> p {' '.join(names)}",
                                    **dict(zip(names[1:], shape[1:])))
                views.append(v)
                at += size
            return views

        hT_all, acc, xc, dt_raw, sp1, sp2 = places(
            0, (KD, B * L), (MX, L), (MX, L), (B * L,), (B * L,), (B * L,))
        ex_all, src = places(0, (B, NSLOT, C, H), (C, NS, HID))
        CHUNKS = B * NSLOT * C * H + C * NS * HID
        cbm, xsd, srcx, coefd, yzT, sq, junk, cbd, ms, rms, term = places(
            CHUNKS, (C, NM + 1, P), (C, HID), (HID,), (C, H), (C, MZ, P), (C, MZ, P),
            (P,), (C,), (C,), (C,), (NTERM, HID))
        h_sb, ids_f, ge_f, w_in = places(CHUNKS, (C, D), (B * L,), (3, B * L // 2), (KD, WIN))
        ids = ids_f.bitcast(I32)
        ge = ge_f.bitcast(BF16)

        q_all, k_all, v_all, g_all, delta, rwd = places(
            0, (C, B * DK), (C, B * DK), (C, B * DV), (C, B * DV), (C, B * QH), (DV,))
        KEPT = 2 * C * B * (DK + DV) + C * B * QH + DV
        (h2, h3, hm, sg, p, pm, h3T_all, cacc, xc3, qk, ra, rb, vr, st2, mv2, ve2, rs2, st3, mv3, ve3, rs3) = places(
            KEPT, (C, D), (C, D), (E, KD, L), (KD, L), (KD, L), (E, KD, L), (B + 1, KD, L), (KD, L), (KD, L),
            (C, 2 * DK), (C, 2 * DK), (C, 2 * DK), (C, DV),
            (C, 6), (C, 2), (C,), (C,), (C, 6), (C, 2), (C,), (C,))
        (prod, pv, wl, eq, ind, th, cnt, sc, oc, osq, og, mu, var, rsh, nwt, ogT) = places(
            KEPT, (C, NPAIR * DK), (C, NPAIR * DV), (C, NPAIR * QH), (C, NPAIR * QH), (C, B * QH), (C, B * QH),
            (C, B * QH), (C, B * QH), (C, B * DV), (C, B * DV), (C, B * DV), (C, B * QH), (C, B * QH),
            (C, B * QH), (C, B * QH), (C, B, KD, P))

        def after(b, per, k):
            return per * (b + 1) + k

        def before(b, per, k):
            return per * b + k

        sems = {}

        def counted(name, per):
            sems[name] = (sem(name), per)
            return sems[name][0]

        in_x, in_w1, in_small, in_const, in_ids, in_late = (sem(n) for n in
            ("in_x", "in_w1", "in_small", "in_const", "in_ids", "in_late"))
        v_setup = sem("v_setup")
        pool_setup = sem("pool_setup")
        w_out_ready = sem("w_out_ready")
        var_ready, rstd_ready = sem("var_ready"), sem("rstd_ready")
        h_ready = counted("h_ready", 1)
        hT_ps = counted("hT_ps", 1)
        hT_sb = counted("hT_sb", 1)
        xbc_ps = counted("xbc_ps", 3)
        z_ps = counted("z_ps", 1)
        dt_ps = counted("dt_ps", 1)
        tap3 = counted("tap3", 3)
        taps = counted("taps", 18)
        z_sb = counted("z_sb", 1)
        dt_sb = counted("dt_sb", 1)
        xc_ready = counted("xc_ready", 3)
        tok_ps = counted("tok_ps", 3)
        tok_sb = counted("tok_sb", 3)
        sp_act = sem("sp_act")
        sp_dve = sem("sp_dve")
        dtT_ready = sem("dtT_ready")
        dtok_ps, dtok_sb = sem("dtok_ps"), sem("dtok_sb")
        ex_ps = counted("ex_ps", 2)
        ex_sb = counted("ex_sb", 2)
        cbm_ready = counted("cbm_ready", 2)
        xsd_ready = counted("xsd_ready", 2)
        src0_ready = counted("src0_ready", 2)
        src1_ready = counted("src1_ready", 2)
        srcx_ready = counted("srcx_ready", 1)
        p_ps = counted("p_ps", NU)
        p_taken = counted("p_taken", NU)
        diag = counted("diag", 8)
        yT_ps = counted("yT_ps", 2)
        yz_ready = counted("yz_ready", 2)
        sq_ready = counted("sq_ready", 2)
        o1_ps = counted("o1_ps", 2)
        ms_ready = counted("ms_ready", 2)
        rms_ready = counted("rms_ready", 2)
        x1_ready = counted("x1_ready", 2)
        masks_ready = sem("masks_ready")
        ln2 = counted("ln2", 5)
        rs2_ready = counted("rs2_ready", 1)
        h2_ready = counted("h2_ready", 1)
        h2T_ps = counted("h2T_ps", 1)
        hm_ready = counted("hm_ready", 1)
        s_ps = counted("s_ps", 1)
        sg_ready = counted("sg_ready", 1)
        p_ready = counted("p_ready", 1)
        pm_ready = counted("pm_ready", 1)
        y2_ps = counted("y2_ps", 1)
        x2_ready = counted("x2_ready", 1)
        set3 = sem("set3")
        ln3 = counted("ln3", 5)
        rs3_ready = counted("rs3_ready", 1)
        h3_ready = counted("h3_ready", 1)
        h3T_ps = counted("h3T_ps", 1)
        h3T_sb = counted("h3T_sb", 1)
        conv3 = counted("conv3", 2)
        xc3_ready = counted("xc3_ready", 1)
        pr_ps = counted("pr_ps", 2)
        pr_sb = counted("pr_sb", 1)
        rot_parts = counted("rot_parts", 3)
        rot_ready = counted("rot_ready", 2)
        dl_ready = counted("dl_ready", 2)
        th_ready, prod0_ready, wl_ready, pv_pool, pv_far = (sem(n) for n in
            ("th_ready", "prod0_ready", "wl_ready", "pv_pool", "pv_far"))
        chain3 = sem("chain3")
        oc_ready, osq_ready, ocg_ready, og_ready = (sem(n) for n in
            ("oc_ready", "osq_ready", "ocg_ready", "og_ready"))
        ogT_ps, ogT_sb, o3_ps, out_ready = (sem(n) for n in ("ogT_ps", "ogT_sb", "o3_ps", "out_ready"))
        stored = sem("stored")

        x_bc = x_all.rearrange("p (b c) d -> p b c d", c=C)

        def passes(eng, body):
            body(0, first=True, last=False)
            with eng.Fori(1, B - 1) as b:
                body(b, first=False, last=False)
            body(B - 1, first=False, last=True)

        def tok(ap, b):
            return ap[..., bass.ts(b, L)]

        def heads(ap):
            return ap.rearrange("p (h d) -> p h d", d=PH)

        def over_head(ap):
            return ap.unsqueeze(2).broadcast_to([P, H, PH])

        def levels_of(c):
            return [*range(NL)] if c == 0 else ["seam", *range(NL)]

        def terms(c):
            at = sum(USES[:c]) + c
            return [*range(at, at + USES[c] + 1)]

        block = ctx.enter_context(nc.Block())

        @block.sync
        def _(sp):
            sp.dma_start(x_all[:, :, :], t["x"].rearrange("b (c p) d -> p (b c) d", p=P)).then_inc(in_x, 16)
            sp.dma_start(ident[:, :], t["ident"]).then_inc(in_x, 16)
            sp.dma_start(w_in[:, :, :], t["w_in"].rearrange("(k p) n -> p k n", p=P)).then_inc(in_w1, 16)
            sp.dma_start(conv_w[:, :, :], t["conv_w"].rearrange("(m p) k -> p m k", p=P)).then_inc(in_w1, 16)
            sp.dma_start(dt_bias[:, :], t["dt_bias"]).then_inc(in_small, 16)
            sp.dma_start(a_log[:, :], t["a_log"]).then_inc(in_small, 16)
            sp.dma_start(sign[:, :], t["sign"]).then_inc(in_small, 16)
            sp.dma_start(norm_w[:, :], t["norm_w"].rearrange("(m p) -> p m", p=P), allow_slow_non_contiguous=True).then_inc(in_small, 16)
            sp.dma_start(d_bc[:, :], t["d"].partition_broadcast(P)).then_inc(in_small, 16)
            sp.dma_start(w_out[:, :, :], t["w_out"].rearrange("(m p) n -> p m n", p=P)).then_inc(in_small, 16)
            sp.dma_start(decay_m[:, :, :], t["decay_masks"].rearrange("p (s j) -> p s j", j=P)).then_inc(in_const, 16)
            sp.dma_start(cb_m[:, :, :], t["cb_masks"].rearrange("p (s j) -> p s j", j=P)).then_inc(in_const, 16)
            sp.dma_start(ids, t["ids"].rearrange("b l -> (b l)").partition_broadcast(P)).then_inc(in_ids, 16)
            sp.dma_start(ctxw[:, :, :, :], t["ctxT"].rearrange("e (k p) n -> p e k n", p=P)).then_inc(in_late, 16)
            sp.dma_start(w3[:, :, :], t["w3"].rearrange("(k p) n -> p k n", p=P)).then_inc(in_late, 16)
            sp.dma_start(conv3_w[:, :, :], t["conv3_w"].rearrange("(k p) w -> p k w", p=P)).then_inc(in_late, 16)
            sp.dma_start(rw[:, :, :, :], t["router_w"].partition_broadcast(P)).then_inc(in_late, 16)
            sp.dma_start(w_out3[:, :, :], t["w_out3"].rearrange("(k p) n -> p k n", p=P)).then_inc(in_late, 16)
            sp.dma_start(rot[:, :, :, :], t["rot"].rearrange("p (b s d) -> p b s d", b=B, s=2)).then_inc(in_late, 16)
            for c in range(C):
                for i in range(2):
                    sp.wait_ge(out_ready, 2 * c + i + 1)
                    half = slice(i * B // 2, (i + 1) * B // 2)
                    sp.dma_start(out[half, c * P:(c + 1) * P, :].rearrange("b p d -> p b d"),
                                 x_bc[:, half, c, :]).then_inc(stored, 16)
            sp.wait_ge(stored, 16 * 2 * C)

        @block.tensor
        def _(pe):
            for name in ("hT_ps", "xbc_ps", "z_ps", "dt_ps", "tok_ps", "ex_ps", "p_ps", "yT_ps", "o1_ps",
                         "h2T_ps", "s_ps", "y2_ps", "h3T_ps", "pr_ps"):
                pe.sem_inc(*sems[name])
            pe.wait_ge(in_x, 32)
            with pe.Fori(0, B) as b:
                pe.wait_ge(hT_sb, before(b, 1, 1))
                pe.wait_ge(h_ready, after(b, 1, 1))
                for c in range(C):
                    for k in range(KD):
                        mm = pe.transpose(PS[:, 6, k * L + c * P:k * L + (c + 1) * P],
                                          h_sb[:, c, k * P:(k + 1) * P], ident[:, :])
                mm.then_inc(hT_ps, 1)
            pe.wait_ge(hT_sb, after(B - 1, 1, 1))
            pe.wait_ge(in_w1, 32)

            def xbc_product(b):
                for q in range(MX // 2):
                    pe.wait_ge(taps, before(b, 18, 6 * q + 6))
                    for m in range(2):
                        for k in range(KD):
                            col = HID + (2 * q + m) * P
                            mm = pe.matmul(PS[:, 2 + q, m * L:(m + 1) * L], w_in[:, k, col:col + P],
                                           hT_all[:, k, bass.ts(b, L)], start=(k == 0), stop=(k == KD - 1))
                    mm.then_inc(xbc_ps, 1)

            def z_dt_product(b):
                pe.wait_ge(z_sb, before(b, 1, 1))
                for m in range(MZ):
                    for k in range(KD):
                        mm = pe.matmul(PS[:, m // 2, (m % 2) * L:(m % 2 + 1) * L], w_in[:, k, m * P:(m + 1) * P],
                                       hT_all[:, k, bass.ts(b, L)], start=(k == 0), stop=(k == KD - 1))
                mm.then_inc(z_ps, 1)
                pe.wait_ge(tok_sb, before(b, 3, 3))
                for k in range(KD):
                    mm = pe.matmul(PS[:, 5, 0:L], w_in[:, k, WIN - P:WIN], hT_all[:, k, bass.ts(b, L)],
                                   start=(k == 0), stop=(k == KD - 1))
                mm.then_inc(dt_ps, 1)

            def by_token(b):
                pe.wait_ge(tok_sb, before(b, 3, 3))
                for c in range(C):
                    pe.wait_ge(xc_ready, after(b, 3, 2 + c))
                    for m in range(MZ):
                        mm = pe.transpose(PS[:, 7 - c, m * P:(m + 1) * P], xc[:, m, c * P:(c + 1) * P], ident[:, :])
                    mm.then_inc(tok_ps, 1)
                pe.wait_ge(dt_sb, after(b, 1, 1))
                for s, (cj, ci) in enumerate(((0, 0), (1, 1), (0, 1))):
                    mm = pe.matmul(PS[:, 5, s * P:(s + 1) * P], xc[:, MZ, cj * P:(cj + 1) * P],
                                   xc[:, MZ + 1, ci * P:(ci + 1) * P], start=True, stop=True)
                mm.then_inc(tok_ps, 1)

            def in_projection(b, first, last):
                xbc_product(b)
                if not first:
                    by_token(b - 1)
                z_dt_product(b)

            passes(pe, in_projection)
            by_token(B - 1)

            pe.wait_ge(tok_sb, after(B - 1, 3, 3))
            pe.wait_ge(dtT_ready, 1)
            for i in range(B * C):
                mm = pe.transpose(PS[:, 6 + i // 4, (i % 4) * P:(i % 4 + 1) * P],
                                  dt_raw[:, i * P:(i + 1) * P], ident[:, :])
            mm.then_inc(dtok_ps, 1)
            pe.wait_ge(dtok_sb, 1)
            pe.wait_ge(in_const, 32)
            pe.wait_ge(w_out_ready, 1)
            pe.wait_ge(z_sb, after(B - 1, 1, 1))
            pe.wait_ge(taps, after(B - 1, 18, 18))

            def exponents(b):
                pe.wait_ge(ex_sb, before(b, 2, 2))
                EX = PS[:, 0:4, :].rearrange("p a (s c h) -> p (a s) c h", c=C, h=H)
                for s in range(SEAM):
                    mm = pe.matmul(EX[:, s], decay_m[:, s, :], dtok_all[:, bass.ts(b, C), H:2 * H],
                                   start=True, stop=True)
                    if s == NS - 1:
                        mm.then_inc(ex_ps, 1)
                for c in range(C):
                    mm = pe.matmul(EX[:, SEAM, c], decay_m[:, SEAM + c, :], dtok_all[:, b * C + c, H:2 * H],
                                   start=True, stop=True)
                mm.then_inc(ex_ps, 1)

            def product(b, c, u, lv):
                if u < 2:
                    pe.wait_ge(p_taken, before(b, NU, NU))
                else:
                    pe.wait_ge(p_taken, after(b, NU, u - 1))
                bank = PS[:, 4 + u % 2, :]
                if lv == "seam":
                    pe.wait_ge(srcx_ready, after(b, 1, 1))
                    mm = pe.matmul(bank, cbm[:, 1, NM, :], srcx[:, :], start=True, stop=True)
                elif lv == 0:
                    blk = LEVELS[0][1]
                    pe.wait_ge(src0_ready, after(b, C, c + 1))
                    for i in range(P // blk):
                        mm = pe.matmul(PS[i * blk:(i + 1) * blk, 4 + u % 2, :],
                                       cbm[:, c, 0, i * blk:(i + 1) * blk], src[:, c, max(i, 1) - 1, :],
                                       start=True, stop=True)
                elif lv == NL - 1:
                    mm = pe.matmul(bank, cbm[:, c, NM - 1, :], xsd[:, c, :], start=True, stop=True)
                else:
                    pe.wait_ge(src1_ready, after(b, C, c + 1))
                    slots = [s for s, (l, _) in enumerate(SRC) if l == lv]
                    for s in slots:
                        mm = pe.matmul(bank, cbm[:, c, CBM.index(SRC[s]), :], src[:, c, s, :],
                                       start=(s == slots[0]), stop=(s == slots[-1]))
                mm.then_inc(p_ps, 1)

            def sum_terms(b, c):
                pe.wait_ge(p_taken, after(b, NU, sum(USES[:c + 1])))
                pe.wait_ge(diag, after(b, 8, 4 * c + 4))
                pe.wait_ge(yz_ready, after(b, C, c) if c else before(b, C, C))
                mine = terms(c)
                for m in range(MZ):
                    for j in mine:
                        mm = pe.matmul(PS[:, 6, m * P:(m + 1) * P], term[:, j, m * P:(m + 1) * P], ident[:, :],
                                       is_transpose=True, start=(j == mine[0]), stop=(j == mine[-1]))
                mm.then_inc(yT_ps, 1)

            def project(b, c):
                pe.wait_ge(yz_ready, after(b, C, c + 1))
                pe.wait_ge(x1_ready, after(b, C, c) if c else before(b, C, C))
                for m in range(MZ):
                    pe.matmul(PS[:, 7, 0:D], yzT[:, c, m, :], w_out[:, m, :], start=(m == 0), stop=(m == MZ - 1))

            def square_sum(b, c):
                pe.wait_ge(sq_ready, after(b, C, c + 1))
                for m in range(MZ):
                    mm = pe.matmul(PS[:, 7, D:D + 1], sq[:, c, m, :], ones[:, :], start=(m == 0), stop=(m == MZ - 1))
                mm.then_inc(o1_ps, 1)

            def chunks(b, first, last):
                for c in range(C):
                    gate = (b, 0) if c else (b - 1, 1)
                    pe.wait_ge(cbm_ready, after(b, C, c + 1))
                    pe.wait_ge(xsd_ready, after(b, C, c + 1))
                    for j, lv in enumerate(levels_of(c)):
                        product(b, c, sum(USES[:c]) + j, lv)
                        if c == 0 and j == 1 and not last:
                            exponents(b + 1)
                        if not (first and c == 0):
                            if j == 0:
                                sum_terms(*gate)
                            if j == 2:
                                project(*gate)
                            if j == 3:
                                square_sum(*gate)

            exponents(0)
            passes(pe, chunks)
            sum_terms(B - 1, 1)
            project(B - 1, 1)
            square_sum(B - 1, 1)

            pe.wait_ge(in_late, 96)
            pe.wait_ge(ex_sb, after(B - 1, 2, 2))
            pe.wait_ge(p_taken, after(B - 1, NU, NU))
            pe.wait_ge(yz_ready, after(B - 1, C, C))
            pe.wait_ge(x1_ready, after(B - 1, C, C))

            def expert_transpose(b):
                pe.wait_ge(hm_ready, before(b, 1, 1))
                pe.wait_ge(h2_ready, after(b, 1, 1))
                for c in range(C):
                    for k in range(KD):
                        mm = pe.transpose(PS[:, 0, k * L + c * P:k * L + (c + 1) * P],
                                          h2[:, c, k * P:(k + 1) * P], ident[:, :])
                mm.then_inc(h2T_ps, 1)

            def up(b, m):
                pe.wait_ge(hm_ready, after(b, 1, 1))
                pe.wait_ge(p_ready, before(b, 1, 1))
                for e in range(E):
                    for k in range(KD):
                        mm = pe.matmul(PS[:, 1, m * L:(m + 1) * L], ctxw[:, e, k, m * P:(m + 1) * P],
                                       hm[:, e, k, :], start=(e == 0 and k == 0), stop=(e == E - 1 and k == KD - 1))
                if m == KD - 1:
                    mm.then_inc(s_ps, 1)

            def down(b):
                pe.wait_ge(pm_ready, after(b, 1, 1))
                pe.wait_ge(x2_ready, before(b, 1, 1))
                for c in range(C):
                    for e in range(E):
                        for k in range(KD):
                            mm = pe.matmul(PS[:, 2, c * D:(c + 1) * D], pm[:, e, k, c * P:(c + 1) * P],
                                           ctxw[:, e, k, :], start=(e == 0 and k == 0), stop=(e == E - 1 and k == KD - 1))
                mm.then_inc(y2_ps, 1)

            def retention_transpose(b):
                pe.wait_ge(h3T_sb, before(b, 1, 1))
                pe.wait_ge(h3_ready, after(b, 1, 1))
                for c in range(C):
                    for k in range(KD):
                        mm = pe.transpose(PS[:, 3, k * L + c * P:k * L + (c + 1) * P],
                                          h3[:, c, k * P:(k + 1) * P], ident[:, :])
                mm.then_inc(h3T_ps, 1)

            def retention_project(b):
                pe.wait_ge(xc3_ready, after(b, 1, 1))
                pe.wait_ge(pr_sb, before(b, 1, 1))
                for c in range(C):
                    for k in range(KD):
                        pe.matmul(PS[:, 4 + c, :], xc3[:, k, c * P:(c + 1) * P], w3[:, k, 0:2 * DK + DV],
                                  start=(k == 0), stop=(k == KD - 1))
                    for k in range(KD):
                        mm = pe.matmul(PS[:, 6, c * DV:(c + 1) * DV], xc3[:, k, c * P:(c + 1) * P],
                                       w3[:, k, 2 * DK + DV:], start=(k == 0), stop=(k == KD - 1))
                    mm.then_inc(pr_ps, 1)

            def experts(b, first, last):
                up(b, 0)
                if not first:
                    retention_transpose(b - 1)
                up(b, 1)
                if not first:
                    retention_project(b - 1)
                if not last:
                    expert_transpose(b + 1)
                down(b)

            expert_transpose(0)
            passes(pe, experts)
            retention_transpose(B - 1)
            retention_project(B - 1)

            pe.wait_ge(x2_ready, after(B - 1, 1, 1))
            pe.wait_ge(pr_sb, after(B - 1, 1, 1))
            for c in range(C):
                pe.wait_ge(og_ready, c + 1)
                for b in range(B):
                    for k in range(KD):
                        mm = pe.transpose(PS[:, 2 * c + b // 2, (b % 2) * D + k * P:(b % 2) * D + (k + 1) * P],
                                          og[:, c, b * DV + k * P:b * DV + (k + 1) * P], ident[:, :])
                mm.then_inc(ogT_ps, 1)
            for c in range(C):
                pe.wait_ge(ogT_sb, c + 1)
                for b in range(B):
                    for k in range(KD):
                        mm = pe.matmul(PS[:, 4 + 2 * c + b // 2, (b % 2) * D:(b % 2 + 1) * D], ogT[:, c, b, k, :],
                                       w_out3[:, k, :], start=(k == 0), stop=(k == KD - 1))
                    if b % 2:
                        mm.then_inc(o3_ps, 1)

        @block.scalar
        def _(act):
            for name in ("hT_sb", "tap3", "z_sb", "dt_sb", "xc_ready", "tok_sb", "ex_sb", "sq_ready",
                         "sg_ready", "h3T_sb", "xc3_ready", "pr_sb"):
                act.sem_inc(*sems[name])
            act.preload_act_table_set("silu_and_others")
            act.wait_ge(in_x, 32)
            with act.Fori(0, B) as b:
                act.wait_ge(hT_ps, after(b, 1, 1))
                act.wait_ge(in_x, 32)
                act.activation(tok(hT_all[:, :, :], b), PS[:, 6, :].rearrange("p (k t) -> p k t", k=KD), ACT.Copy)\
                   .then_inc(hT_sb, 1)
            act.wait_ge(in_w1, 32)
            act.wait_ge(in_small, 96)

            def copy_by_token(b):
                for c in range(C):
                    act.wait_ge(tok_ps, after(b, 3, c + 1))
                    act.wait_ge(in_w1, 32)
                    act.activation(xs_all[:, b * C + c, :], PS[:, 7 - c, :], ACT.Copy).then_inc(tok_sb, 1)
                act.wait_ge(tok_ps, after(b, 3, 3))
                act.wait_ge(in_w1, 32)
                act.activation(cb_all[:, b, :, :], PS[:, 5, 0:3 * P].rearrange("p (s i) -> p s i", i=P), ACT.Copy)\
                   .then_inc(tok_sb, 1)

            def in_projection(b, first, last):
                for q in range(MX // 2):
                    act.wait_ge(xbc_ps, after(b, 3, q + 1))
                    act.wait_ge(xc_ready, before(b, 3, q + 1))
                    for m in range(2):
                        ins = act.activation(acc[:, 2 * q + m, :], PS[:, 2 + q, m * L:(m + 1) * L], ACT.Identity,
                                             scale=conv_w[:, 2 * q + m, 3:4])
                    ins.then_inc(tap3, 1)
                if not first:
                    copy_by_token(b - 1)
                act.wait_ge(z_ps, after(b, 1, 1))
                act.wait_ge(in_w1, 32)
                act.activation(tok(zT_all[:, :, :], b), PS[:, 0:2, :].rearrange("p a (m t) -> p (a m) t", t=L),
                               ACT.Silu).then_inc(z_sb, 1)
                act.wait_ge(dt_ps, after(b, 1, 1))
                act.wait_ge(in_w1, 32)
                act.activation(tok(dt_raw[:, :], b), PS[:, 5, 0:L], ACT.Copy).then_inc(dt_sb, 1)
                act.wait_ge(tok_ps, before(b, 3, 3))
                for q in range(MX // 2):
                    act.wait_ge(taps, after(b, 18, 6 * q + 6))
                    act.activation(xc[:, 2 * q:2 * q + 2, :], acc[:, 2 * q:2 * q + 2, :], ACT.Silu)\
                       .then_inc(xc_ready, 1)

            passes(act, in_projection)
            copy_by_token(B - 1)
            act.preload_act_table_set("natural_log_exp_and_others")

            act.wait_ge(dt_sb, after(B - 1, 1, 1))
            act.activation(sp1[:, :], dt_raw[:, :], ACT.Abs, bias=dt_bias[:, :]).then_inc(sp_act, 1)
            act.wait_ge(sp_act, 1)
            act.activation(sp2[:, :], sp1[:, :], ACT.Exp, scale=-1.0).then_inc(sp_act, 1)
            act.activation(avec[:, :], a_log[:, :], ACT.Exp).then_inc(sp_act, 1)
            act.wait_ge(sp_act, 2)
            act.activation(sp1[:, :], sp2[:, :], ACT.Ln, bias=1.0).then_inc(sp_act, 1)
            act.wait_ge(dtok_ps, 1)
            act.activation(dtok_all[:, :, :], PS[:, 6:8, :].rearrange("p a (s h) -> p (a s) h", h=P), ACT.Copy)\
               .then_inc(dtok_sb, 1)

            EX = PS[:, 0:4, :].rearrange("p a (s c h) -> p (a s) (c h)", c=C, h=H)

            def decays(b):
                ex = ex_all[:, b, :, :, :].rearrange("p s c h -> p s (c h)")
                act.wait_ge(ex_ps, after(b, 2, 1))
                act.wait_ge(in_w1, 32)
                act.activation(ex[:, 0:NS], EX[:, 0:NS], ACT.Exp).then_inc(ex_sb, 1)
                act.wait_ge(ex_ps, after(b, 2, 2))
                act.wait_ge(in_w1, 32)
                act.activation(ex[:, NS:NSLOT], EX[:, NS:NSLOT], ACT.Exp).then_inc(ex_sb, 1)

            def squares(b, c):
                act.wait_ge(o1_ps, before(b, C, c + 1))
                act.wait_ge(yz_ready, after(b, C, c + 1))
                act.activation(sq[:, c, :, :], yzT[:, c, :, :], ACT.Square).then_inc(sq_ready, 1)

            def chunks(b, first, last):
                if not first:
                    squares(b - 1, 1)
                if not last:
                    decays(b + 1)
                squares(b, 0)

            decays(0)
            passes(act, chunks)
            squares(B - 1, 1)

            act.preload_act_table_set("silu_and_others")

            def expert_silu(b):
                act.wait_ge(p_ready, before(b, 1, 1))
                act.wait_ge(s_ps, after(b, 1, 1))
                act.activation(sg[:, :, :], PS[:, 1, :].rearrange("p (k t) -> p k t", k=KD), ACT.Silu)\
                   .then_inc(sg_ready, 1)

            def retention_in(b):
                act.wait_ge(h3T_ps, after(b, 1, 1))
                act.wait_ge(set3, 1)
                act.activation(h3T_all[:, b + 1, :, :], PS[:, 3, :].rearrange("p (k t) -> p k t", k=KD), ACT.Copy)\
                   .then_inc(h3T_sb, 1)
                act.wait_ge(pr_ps, before(b, C, C))
                act.wait_ge(conv3, after(b, 2, 2))
                act.activation(xc3[:, :, :], cacc[:, :, :], ACT.Silu).then_inc(xc3_ready, 1)

            def retention_parts(b):
                act.wait_ge(rot_ready, before(b, 2, 2))
                act.wait_ge(pr_ps, after(b, C, C))
                act.activation(qk[:, :, 0:DK], PS[:, 4:6, 0:DK], ACT.Silu)
                act.activation(qk[:, :, DK:2 * DK], PS[:, 4:6, DK:2 * DK], ACT.Copy)
                act.activation(g_all[:, :, bass.ts(b, DV)], PS[:, 6, :].rearrange("p (c n) -> p c n", c=C), ACT.Silu)
                act.activation(v_all[:, :, bass.ts(b, DV)], PS[:, 4:6, 2 * DK:2 * DK + DV], ACT.Copy)\
                   .then_inc(pr_sb, 1)

            def experts(b, first, last):
                if not first:
                    retention_in(b - 1)
                expert_silu(b)
                if not first:
                    retention_parts(b - 1)

            passes(act, experts)
            retention_in(B - 1)
            retention_parts(B - 1)

            act.wait_ge(dl_ready, after(B - 1, 2, 2))
            act.activation(th[:, :, :], delta[:, :, :], ACT.Tanh, scale=0.5).then_inc(th_ready, 1)
            for c in range(C):
                act.wait_ge(oc_ready, c + 1)
                act.activation(osq[:, c, :], oc[:, c, :], ACT.Square).then_inc(osq_ready, 1)
            for c in range(C):
                act.wait_ge(ogT_ps, c + 1)
                act.activation(ogT[:, c, :, :, :].rearrange("p b k t -> p (b k t)"),
                               PS[:, 2 * c:2 * c + 2, :].rearrange("p a n -> p (a n)"), ACT.Copy)\
                   .then_inc(ogT_sb, 1)

        @block.gpsimd
        def _(pool):
            for name in ("cbm_ready", "src0_ready", "rms_ready", "rs2_ready", "rs3_ready", "pm_ready",
                         "rot_parts", "rot_ready"):
                pool.sem_inc(*sems[name])
            pool.memset(mhalf[:, :], -0.5).then_inc(pool_setup, 1)
            pool.wait_ge(var_ready, 1)
            pool.wait_ge(pool_setup, 1)
            pool.tensor_tensor(rs[:, :], ve[:, :], mhalf[:, :], ALU.pow).then_inc(rstd_ready, 1)
            pool.wait_ge(in_ids, 16)
            per = VOCAB // E
            for i in range(E - 1):
                pool.tensor_scalar(ge[:, i, :], ids, float(per * (i + 1)), None, ALU.is_ge).then_inc(pool_setup, 1)
            pool.wait_ge(pool_setup, E)
            pool.tensor_scalar(mask[:, 0, :], ge[:, 0, :], -1.0, 1.0, ALU.mult, ALU.add)
            for i in range(1, E - 1):
                pool.tensor_tensor(mask[:, i, :], ge[:, i - 1, :], ge[:, i, :], ALU.subtract)
            pool.tensor_copy(mask[:, E - 1, :], ge[:, E - 2, :]).then_inc(masks_ready, 1)

            pool.wait_ge(masks_ready, 1)
            pool.wait_ge(in_const, 32)
            pool.wait_ge(tok_sb, after(B - 1, 3, 3))

            def prepare(b, c):
                pool.wait_ge(p_taken, before(b, NU, sum(USES[:c + 1])))
                pool.wait_ge(in_const, 32)
                if c:
                    pool.tensor_copy(cbm[:, 1, NM, :], cb_all[:, b, C, :])
                pool.tensor_tensor(cbm[:, c, 0:NM, :], cb_m[:, :, :],
                                   cb_all[:, b, c, :].unsqueeze(1).broadcast_to([P, NM, P]), ALU.mult)\
                    .then_inc(cbm_ready, 1)
                pool.wait_ge(ex_sb, after(b, 2, 1))
                pool.wait_ge(xsd_ready, after(b, C, c + 1))
                pool.wait_ge(in_const, 32)
                n0 = sum(lv == 0 for lv, _ in SRC)
                for s in range(n0):
                    ins = pool.tensor_tensor(heads(src[:, c, s, :]), heads(xsd[:, c, :]),
                                             over_head(ex_all[:, b, s, c, :]), ALU.mult)
                ins.then_inc(src0_ready, 1)

            def inverse_rms(b, c):
                pool.wait_ge(ms_ready, after(b, C, c + 1))
                pool.tensor_tensor(rms[:, c:c + 1], ms[:, c:c + 1], mhalf[:, 0:1], ALU.pow).then_inc(rms_ready, 1)

            def chunks(b, first, last):
                prepare(b, 1)
                if not first:
                    inverse_rms(b - 1, 1)
                if not last:
                    prepare(b + 1, 0)
                inverse_rms(b, 0)

            prepare(0, 0)
            passes(pool, chunks)
            inverse_rms(B - 1, 1)

            def expert_rstd(b):
                pool.wait_ge(ln2, after(b, 5, 5))
                pool.tensor_tensor(rs2[:, :], ve2[:, :], mhalf[:, 0:C], ALU.pow).then_inc(rs2_ready, 1)

            def retention_rstd(b):
                pool.wait_ge(ln3, after(b, 5, 5))
                pool.tensor_tensor(rs3[:, :], ve3[:, :], mhalf[:, 0:C], ALU.pow).then_inc(rs3_ready, 1)

            def mask_products(b):
                pool.wait_ge(y2_ps, before(b, 1, 1))
                pool.wait_ge(p_ready, after(b, 1, 1))
                pool.wait_ge(in_const, 32)
                for e in range(E):
                    ins = pool.tensor_tensor(pm[:, e, :, :], p[:, :, :],
                                             mask[:, e, bass.ts(b, L)].unsqueeze(1).broadcast_to([P, KD, L]), ALU.mult)
                ins.then_inc(pm_ready, 1)

            def rotate(b):
                half, n_heads = QK // 2, C * 2 * QH
                qkh, rah, rbh = (z.rearrange("p c (h d) -> p (c h) d", d=QK) for z in (qk, ra, rb))

                def over_heads(ap, n):
                    return ap.unsqueeze(1).broadcast_to([P, n_heads, n])

                pool.wait_ge(pr_sb, after(b, 1, 1))
                pool.wait_ge(in_const, 32)
                pool.tensor_tensor(rah, qkh, over_heads(rot[:, b, 0, :], QK), ALU.mult).then_inc(rot_parts, 1)
                pool.tensor_tensor(rbh[:, :, 0:half], qkh[:, :, half:QK], over_heads(rot[:, b, 1, 0:half], half),
                                   ALU.mult).then_inc(rot_parts, 1)
                pool.tensor_tensor(rbh[:, :, half:QK], qkh[:, :, 0:half], over_heads(rot[:, b, 1, half:QK], half),
                                   ALU.mult).then_inc(rot_parts, 1)
                pool.wait_ge(rot_parts, after(b, 3, 3))
                pool.wait_ge(in_const, 32)
                pool.tensor_tensor(q_all[:, :, bass.ts(b, DK)], ra[:, :, 0:DK], rb[:, :, 0:DK], ALU.add)\
                    .then_inc(rot_ready, 1)
                pool.tensor_tensor(k_all[:, :, bass.ts(b, DK)], ra[:, :, DK:2 * DK], rb[:, :, DK:2 * DK], ALU.add)\
                    .then_inc(rot_ready, 1)

            def experts(b, first, last):
                if not first:
                    retention_rstd(b - 1)
                if not last:
                    expert_rstd(b + 1)
                mask_products(b)
                if not first:
                    rotate(b - 1)

            expert_rstd(0)
            passes(pool, experts)
            retention_rstd(B - 1)
            rotate(B - 1)

            pool.wait_ge(dl_ready, after(B - 1, 2, 2))
            pool.wait_ge(rot_ready, after(B - 1, 2, 2))
            pool.tensor_tensor(prod[:, :, 0:B * DK], q_all[:, :, :], k_all[:, :, :], ALU.mult).then_inc(prod0_ready, 1)
            pool.wait_ge(wl_ready, 1)
            for lag in (B - 1, B - 2):
                at, n = PAIR_AT[lag], B - lag
                for c in range(C):
                    pool.tensor_tensor(pv[:, c, at * DV:(at + n) * DV].rearrange("p (h d) -> p h d", d=QV),
                                       v_all[:, c, 0:n * DV].rearrange("p (h d) -> p h d", d=QV),
                                       wl[:, c, at * QH:(at + n) * QH].unsqueeze(2).broadcast_to([P, n * QH, QV]),
                                       ALU.mult).then_inc(pv_pool, 1)
            pool.wait_ge(pv_pool, 2 * C)
            far, near = PAIR_AT[B - 1] * DV, (PAIR_AT[B - 2] + 1) * DV
            pool.tensor_tensor(pv[:, :, near:near + DV], pv[:, :, near:near + DV], pv[:, :, far:far + DV], ALU.add)\
                .then_inc(pv_far, 1)
            for c in range(C):
                pool.wait_ge(oc_ready, c + 1)
                pool.tensor_tensor(og[:, c, :], oc[:, c, :], g_all[:, c, :], ALU.mult).then_inc(ocg_ready, 1)

        @block.vector
        def _(dve):
            for name in ("h_ready", "taps", "xsd_ready", "src1_ready", "srcx_ready", "diag", "p_taken",
                         "yz_ready", "ms_ready", "x1_ready", "ln2", "h2_ready", "hm_ready", "p_ready",
                         "x2_ready", "ln3", "h3_ready", "conv3", "dl_ready"):
                dve.sem_inc(*sems[name])
            dve.memset(ones[:, :], 1.0)
            dve.wait_ge(in_x, 32)
            for i in range(B * C):
                dve.bn_stats(st[:, i, :], x_all[:, i, :]).then_inc(v_setup, 1)
            for i in range(B * C):
                dve.wait_ge(v_setup, i + 1)
                ins = dve.bn_aggr(mv[:, i, :], st[:, i, :])
            ins.then_inc(v_setup, 1)
            dve.wait_ge(v_setup, B * C + 1)
            dve.tensor_scalar(ve[:, :], mv[:, :, 1], EPS, None, ALU.add).then_inc(var_ready, 1)
            dve.wait_ge(rstd_ready, 1)
            with dve.Fori(0, B) as b:
                dve.wait_ge(hT_ps, before(b, 1, 1))
                for c in range(C):
                    i = b * C + c
                    ins = dve.tensor_scalar(h_sb[:, c, :], x_all[:, i, :], mv[:, i, 0:1], rs[:, bass.ds(i, 1)],
                                            ALU.subtract, ALU.mult)
                ins.then_inc(h_ready, 1)
            dve.wait_ge(in_w1, 32)
            with dve.Fori(0, B) as b:
                for q in range(MX // 2):
                    dve.wait_ge(tap3, after(b, 3, q + 1))
                    for tap in range(1, 4):
                        for m in range(2):
                            n = 6 * q + 2 * (tap - 1) + m
                            if tap > 1:
                                dve.wait_ge(taps, after(b, 18, n - 1))
                            dve.scalar_tensor_tensor(acc[:, 2 * q + m, tap:], PS[:, 2 + q, m * L:(m + 1) * L - tap],
                                                     conv_w[:, 2 * q + m, 3 - tap:4 - tap], acc[:, 2 * q + m, tap:],
                                                     ALU.mult, ALU.add).then_inc(taps, 1)

            dve.wait_ge(sp_act, 1)
            dve.wait_ge(dt_sb, after(B - 1, 1, 1))
            dve.tensor_scalar(dt_raw[:, :], dt_raw[:, :], dt_bias[:, :], 0.0, ALU.add, ALU.max).then_inc(v_setup, 1)
            dve.wait_ge(sp_act, 4)
            dve.tensor_tensor(avec[:, :], avec[:, :], sign[:, :], ALU.mult).then_inc(v_setup, 1)
            dve.wait_ge(v_setup, B * C + 3)
            dve.tensor_tensor(dt_raw[:, :], dt_raw[:, :], sp1[:, :], ALU.add).then_inc(v_setup, 1)
            dve.wait_ge(v_setup, B * C + 4)
            dve.tensor_scalar(dt_raw[:, :], dt_raw[:, :], avec[:, :], None, ALU.mult).then_inc(dtT_ready, 1)
            for m in range(MZ):
                ins = dve.tensor_scalar(w_out[:, m, :], w_out[:, m, :], norm_w[:, m:m + 1], None, ALU.mult)
            ins.then_inc(w_out_ready, 1)

            dve.wait_ge(masks_ready, 1)
            dve.wait_ge(dtok_sb, 1)

            FIRST_LEVEL = sum(lv == 0 for lv, _ in SRC)

            def dt_xs(b, c):
                i = b * C + c
                dve.wait_ge(src0_ready, before(b, C, c + 1))
                dve.tensor_tensor(heads(xsd[:, c, :]), heads(xs_all[:, i, :]), over_head(dtok_all[:, i, 0:H]),
                                  ALU.mult).then_inc(xsd_ready, 1)

            def decayed(b, c, slots):
                dve.wait_ge(xsd_ready, after(b, C, c + 1))
                dve.wait_ge(ex_sb, after(b, 2, 1))
                for s in slots:
                    ins = dve.tensor_tensor(heads(src[:, c, s, :]), heads(xsd[:, c, :]),
                                            over_head(ex_all[:, b, s, c, :]), ALU.mult)
                    if s == NS - 1:
                        ins.then_inc(src1_ready, 1)

            def decayed_to_end(b):
                dve.wait_ge(xsd_ready, after(b, C, 1))
                dve.wait_ge(ex_sb, after(b, 2, 2))
                dve.tensor_tensor(heads(srcx), heads(xsd[:, 0, :]), over_head(ex_all[:, b, SEAM, 0, :]),
                                  ALU.mult).then_inc(srcx_ready, 1)

            def own_factor(b, c):
                dve.tensor_tensor(junk, cb_all[:, b, c, :], ident[:, :], ALU.mult).then_inc(diag, 1)
                dve.wait_ge(diag, after(b, 8, 4 * c + 1))
                dve.tensor_reduce(cbd[:, c:c + 1], junk, AX_X, ALU.add).then_inc(diag, 1)
                dve.wait_ge(diag, after(b, 8, 4 * c + 2))
                dve.scalar_tensor_tensor(coefd[:, c, :], dtok_all[:, b * C + c, 0:H], cbd[:, c:c + 1], d_bc[:, :],
                                         ALU.mult, ALU.add).then_inc(diag, 1)

            def own_term(b, c):
                dve.wait_ge(yT_ps, before(b, C, c + 1))
                dve.wait_ge(diag, after(b, 8, 4 * c + 3))
                dve.tensor_tensor(heads(term[:, terms(c)[0], :]), heads(xs_all[:, b * C + c, :]),
                                  over_head(coefd[:, c, :]), ALU.mult).then_inc(diag, 1)

            def take(b, c, j, lv):
                u = sum(USES[:c]) + j
                slot = SEAM if lv == "seam" else NS + lv
                dve.wait_ge(ex_sb, after(b, 2, 2))
                dve.wait_ge(p_ps, after(b, NU, u + 1))
                dve.tensor_tensor(heads(term[:, terms(c)[1 + j], :]), heads(PS[:, 4 + u % 2, :]),
                                  over_head(ex_all[:, b, slot, c, :]), ALU.mult).then_inc(p_taken, 1)

            def gate(b, c):
                dve.wait_ge(o1_ps, before(b, C, c + 1))
                dve.wait_ge(yT_ps, after(b, C, c + 1))
                dve.tensor_tensor(yzT[:, c, :, :], PS[:, 6, :].rearrange("p (m t) -> p m t", m=MZ),
                                  zT_all[:, :, bass.ds((b * C + c) * P, P)], ALU.mult).then_inc(yz_ready, 1)

            def mean_square(b, c):
                dve.wait_ge(o1_ps, after(b, C, c + 1))
                dve.tensor_scalar(ms[:, c:c + 1], PS[:, 7, D:D + 1], 1.0 / HID, EPS, ALU.mult, ALU.add)\
                    .then_inc(ms_ready, 1)

            def residual(b, c):
                i = b * C + c
                dve.wait_ge(rms_ready, after(b, C, c + 1))
                dve.scalar_tensor_tensor(x_all[:, i, :], PS[:, 7, 0:D], rms[:, c:c + 1], x_all[:, i, :],
                                         ALU.mult, ALU.add).then_inc(x1_ready, 1)

            def chunks(b, first, last):
                for c in range(C):
                    behind = (b, 0) if c else (b - 1, 1)
                    ahead = (b + 1, 0) if c else (b, 1)
                    steps = levels_of(c)
                    for j, lv in enumerate(steps):
                        take(b, c, j, lv)
                        if not (first and c == 0):
                            if j == 0:
                                gate(*behind)
                            if j == 3:
                                mean_square(*behind)
                            if j == 4:
                                residual(*behind)
                        if not (last and c):
                            if j == 0:
                                dt_xs(*ahead)
                                if c == 0:
                                    decayed_to_end(b)
                            if j == 1:
                                decayed(*ahead, range(FIRST_LEVEL, NS - 2))
                            if j == 2:
                                decayed(*ahead, range(NS - 2, NS))
                            if j == 3:
                                own_factor(*ahead)
                            if j == 4:
                                own_term(*ahead)

            dt_xs(0, 0)
            decayed(0, 0, range(FIRST_LEVEL, NS))
            own_factor(0, 0)
            own_term(0, 0)
            passes(dve, chunks)
            gate(B - 1, 1)
            mean_square(B - 1, 1)
            residual(B - 1, 1)

            def statistics(b, chain, stats, moments, v_eps):
                for c in range(C):
                    dve.bn_stats(stats[:, c, :], x_all[:, b * C + c, :]).then_inc(chain, 1)
                dve.wait_ge(chain, after(b, 5, 2))
                dve.memset(v_eps[:, :], EPS)
                for c in range(C):
                    dve.bn_aggr(moments[:, c, :], stats[:, c, :]).then_inc(chain, 1)
                dve.wait_ge(chain, after(b, 5, 4))
                dve.tensor_tensor(v_eps[:, :], moments[:, :, 1], v_eps[:, :], ALU.add).then_inc(chain, 1)

            def normalise(b, rstd_done, moments, rstd, done, dst):
                dve.wait_ge(rstd_done, after(b, 1, 1))
                for c in range(C):
                    ins = dve.tensor_scalar(dst[:, c, :], x_all[:, b * C + c, :], moments[:, c, 0:1], rstd[:, c:c + 1],
                                            ALU.subtract, ALU.mult)
                ins.then_inc(done, 1)

            def mask_tokens(b):
                dve.wait_ge(h2T_ps, after(b, 1, 1))
                for e in range(E):
                    ins = dve.tensor_tensor(hm[:, e, :, :], PS[:, 0, :].rearrange("p (k t) -> p k t", k=KD),
                                            mask[:, e, bass.ts(b, L)].unsqueeze(1).broadcast_to([P, KD, L]), ALU.mult)
                ins.then_inc(hm_ready, 1)

            def gate_up(b):
                dve.wait_ge(pm_ready, before(b, 1, 1))
                dve.wait_ge(sg_ready, after(b, 1, 1))
                dve.tensor_tensor(p[:, :, :], PS[:, 1, :].rearrange("p (k t) -> p k t", k=KD), sg[:, :, :],
                                  ALU.mult).then_inc(p_ready, 1)

            def expert_residual(b):
                dve.wait_ge(y2_ps, after(b, 1, 1))
                dve.tensor_tensor(x_all[:, bass.ts(b, C), :], PS[:, 2, :].rearrange("p (c n) -> p c n", c=C),
                                  x_all[:, bass.ts(b, C), :], ALU.add).then_inc(x2_ready, 1)

            def convolve(b):
                dve.wait_ge(h3T_sb, after(b, 1, 1))
                for k in range(KD):
                    ins = dve.tensor_scalar(cacc[:, k, :], h3T_all[:, b, k, :], conv3_w[:, k, 0:1], None, ALU.mult)
                ins.then_inc(conv3, 1)
                dve.wait_ge(conv3, after(b, 2, 1))
                for k in range(KD):
                    ins = dve.scalar_tensor_tensor(cacc[:, k, :], h3T_all[:, b + 1, k, :], conv3_w[:, k, 1:2],
                                                   cacc[:, k, :], ALU.mult, ALU.add)
                ins.then_inc(conv3, 1)

            def route(b):
                dve.wait_ge(pr_sb, after(b, 1, 1))
                dve.tensor_tensor(vr[:, :, :], v_all[:, :, bass.ts(b, DV)], rwd.unsqueeze(1).broadcast_to([P, C, DV]),
                                  ALU.mult).then_inc(dl_ready, 1)
                dve.wait_ge(dl_ready, after(b, 2, 1))
                dve.tensor_reduce(delta[:, :, bass.ts(b, QH)], vr.rearrange("p c (h d) -> p c h d", d=QV), AX_X,
                                  ALU.add).then_inc(dl_ready, 1)

            def experts(b, first, last):
                if not first:
                    dve.wait_ge(x2_ready, after(b - 1, 1, 1))
                    statistics(b - 1, ln3, st3, mv3, ve3)
                if not last:
                    statistics(b + 1, ln2, st2, mv2, ve2)
                if not first:
                    normalise(b - 1, rs3_ready, mv3, rs3, h3_ready, h3)
                if not last:
                    normalise(b + 1, rs2_ready, mv2, rs2, h2_ready, h2)
                if not first:
                    convolve(b - 1)
                gate_up(b)
                if not last:
                    mask_tokens(b + 1)
                if not first:
                    route(b - 1)
                expert_residual(b)

            dve.wait_ge(x1_ready, after(B - 1, C, C))
            statistics(0, ln2, st2, mv2, ve2)
            normalise(0, rs2_ready, mv2, rs2, h2_ready, h2)
            dve.wait_ge(in_late, 96)
            dve.memset(h3T_all[:, 0, :, :], 0.0)
            dve.tensor_tensor(rwd.rearrange("p (h d) -> p h d", h=QH), rw[:, :, :, 1], rw[:, :, :, 0],
                              ALU.subtract).then_inc(set3, 1)
            dve.wait_ge(set3, 1)
            mask_tokens(0)
            passes(dve, experts)
            dve.wait_ge(x2_ready, after(B - 1, 1, 1))
            statistics(B - 1, ln3, st3, mv3, ve3)
            normalise(B - 1, rs3_ready, mv3, rs3, h3_ready, h3)
            convolve(B - 1)
            route(B - 1)

            n_links = [0]

            def link(ins):
                n_links[0] += 1
                ins.then_inc(chain3, 1)
                dve.wait_ge(chain3, n_links[0])

            def over(ap, n, width):
                return ap.unsqueeze(2).broadcast_to([P, n, width])

            def by_head(ap, width):
                return ap.rearrange("p (h d) -> p h d", d=width)

            dve.wait_ge(dl_ready, after(B - 1, 2, 2))
            dve.wait_ge(rot_ready, after(B - 1, 2, 2))
            link(dve.tensor_scalar(ind[:, :, :], delta[:, :, :], 0.0, None, ALU.is_gt))
            for lag in range(1, B):
                at, n = PAIR_AT[lag], B - lag
                dve.tensor_tensor(eq[:, :, at * QH:(at + n) * QH], ind[:, :, lag * QH:], ind[:, :, 0:n * QH],
                                  ALU.is_equal)
                dve.tensor_tensor(prod[:, :, at * DK:(at + n) * DK], q_all[:, :, lag * DK:], k_all[:, :, 0:n * DK],
                                  ALU.mult)
            link(dve.memset(cnt[:, :, :], 1.0))
            for lag in range(1, B):
                at, n = PAIR_AT[lag], B - lag
                link(dve.tensor_tensor(cnt[:, :, lag * QH:], cnt[:, :, lag * QH:], eq[:, :, at * QH:(at + n) * QH],
                                       ALU.add))
            link(dve.reciprocal(sc[:, :, :], cnt[:, :, :]))
            scale = float(QK) ** -0.5
            dve.wait_ge(th_ready, 1)
            link(dve.scalar_tensor_tensor(th[:, :, :], th[:, :, :], -1.0, th[:, :, :], ALU.mult, ALU.max))
            link(dve.tensor_scalar(th[:, :, :], th[:, :, :], 0.5 * scale, 0.5 * scale, ALU.mult, ALU.add))
            link(dve.tensor_tensor(sc[:, :, :], sc[:, :, :], th[:, :, :], ALU.mult))
            own = B * QH
            for c in range(C):
                dve.tensor_reduce(wl[:, c, own:], by_head(prod[:, c, B * DK:], QK), AX_X, ALU.add)
            dve.wait_ge(prod0_ready, 1)
            for c in range(C):
                ins = dve.tensor_reduce(wl[:, c, 0:own], by_head(prod[:, c, 0:B * DK], QK), AX_X, ALU.add)
            link(ins)
            link(dve.tensor_tensor(wl[:, :, own:], wl[:, :, own:], eq[:, :, own:], ALU.mult))
            for lag in reversed(range(B)):
                at, n = PAIR_AT[lag], B - lag
                ins = dve.tensor_tensor(wl[:, :, at * QH:(at + n) * QH], wl[:, :, at * QH:(at + n) * QH],
                                        sc[:, :, lag * QH:], ALU.mult)
            ins.then_inc(wl_ready, 1)
            dve.wait_ge(wl_ready, 1)
            for lag in range(B - 2):
                at, n = PAIR_AT[lag], B - lag
                for c in range(C):
                    ins = dve.tensor_tensor(by_head(pv[:, c, at * DV:(at + n) * DV], QV),
                                            by_head(v_all[:, c, 0:n * DV], QV),
                                            over(wl[:, c, at * QH:(at + n) * QH], n * QH, QV), ALU.mult)
            link(ins)
            for lag in range(1, B - 1):
                at, n = PAIR_AT[lag], B - lag
                if lag == B - 2:
                    dve.wait_ge(pv_far, 1)
                link(dve.tensor_tensor(pv[:, :, lag * DV:B * DV], pv[:, :, lag * DV:B * DV],
                                       pv[:, :, at * DV:(at + n) * DV], ALU.add))
            heads_of = B * QH
            for c in range(C):
                o = by_head(pv[:, c, 0:B * DV], QV)
                link(dve.tensor_reduce(mu[:, c, :], o, AX_X, ALU.add))
                dve.scalar_tensor_tensor(by_head(oc[:, c, :], QV), over(mu[:, c, :], heads_of, QV), -1.0 / QV, o,
                                         ALU.mult, ALU.add).then_inc(oc_ready, 1)
            for c in range(C):
                dve.wait_ge(osq_ready, c + 1)
                ins = dve.tensor_reduce(var[:, c, :], by_head(osq[:, c, :], QV), AX_X, ALU.add)
            link(ins)
            link(dve.tensor_scalar(var[:, :, :], var[:, :, :], 1.0 / QV, EPS, ALU.mult, ALU.add))
            link(dve.tensor_scalar(rsh.bitcast(I32), var.bitcast(I32), -0.5, float(0x5F3759DF), ALU.mult, ALU.add))
            for _ in range(3):
                link(dve.scalar_tensor_tensor(nwt[:, :, :], rsh[:, :, :], -0.5, rsh[:, :, :], ALU.mult, ALU.mult))
                link(dve.tensor_tensor(nwt[:, :, :], nwt[:, :, :], var[:, :, :], ALU.mult))
                link(dve.scalar_tensor_tensor(rsh[:, :, :], nwt[:, :, :], 1.5, rsh[:, :, :], ALU.add, ALU.mult))
            for c in range(C):
                dve.wait_ge(ocg_ready, c + 1)
                dve.tensor_tensor(by_head(og[:, c, :], QV), by_head(og[:, c, :], QV), over(rsh[:, c, :], heads_of, QV),
                                  ALU.mult).then_inc(og_ready, 1)
            for c in range(C):
                for i in range(2):
                    dve.wait_ge(o3_ps, 2 * c + i + 1)
                    rows = x_bc[:, i * B // 2:(i + 1) * B // 2, c, :]
                    dve.tensor_tensor(rows, PS[:, 4 + 2 * c + i, :].rearrange("p (b n) -> p b n", n=D), rows,
                                      ALU.add).then_inc(out_ready, 1)


_INS = {
    "x": (B, L, D), "w_in": (D, WIN), "conv_w": (MX * P, 4), "dt_bias": (P, 1), "a_log": (P, 1), "d": (H,),
    "norm_w": (HID,), "w_out": (HID, D), "ids": (B, L), "ctxT": (E, D, D), "w3": (D, 2 * DK + 2 * DV),
    "conv3_w": (D, 2), "router_w": (QH, QV, 2), "w_out3": (D, D),
}


def kernel(x, itok_BxS_13_99985, ctx_2048, L0_attn_W_in, L0_attn_conv_w, L0_attn_dt_bias, L0_attn_A_log, L0_attn_D,
           L0_attn_norm_w, L0_attn_W_out, L0_ffn_conv_w, L0_ffn_Wq, L0_ffn_Wk, L0_ffn_Wv, L0_ffn_Wg,
           L0_ffn_router_w, L0_ffn_Wout):
    import numpy as np
    import concourse.bacc as bacc
    from concourse.bass_utils import run_bass_kernel_spmd

    w_in = np.asarray(L0_attn_W_in).T
    dt_bias = np.asarray(L0_attn_dt_bias)
    a_log = np.asarray(L0_attn_A_log)
    arrays = {
        "x": x, "w_in": np.concatenate([w_in, w_in[:, -H:]], 1), "conv_w": L0_attn_conv_w,
        "dt_bias": np.concatenate([dt_bias, dt_bias])[:, None],
        "a_log": np.concatenate([np.zeros_like(a_log), a_log])[:, None],
        "d": L0_attn_D, "norm_w": L0_attn_norm_w, "w_out": np.asarray(L0_attn_W_out).T, "ids": itok_BxS_13_99985,
        "ctxT": np.asarray(ctx_2048).transpose(0, 2, 1),
        "w3": np.concatenate([np.asarray(w) for w in (L0_ffn_Wq, L0_ffn_Wk, L0_ffn_Wv, L0_ffn_Wg)], 1),
        "conv3_w": L0_ffn_conv_w, "router_w": L0_ffn_router_w, "w_out3": L0_ffn_Wout,
    }
    arrays = {k: np.ascontiguousarray(v) for k, v in arrays.items()}
    assert all(arrays[k].shape == s for k, s in _INS.items())
    arrays |= shape_constants()
    nc = bacc.Bacc("TRN2", target_bir_lowering=False, num_devices=1)
    t = {k: nc.dram_tensor(f"in_{k}", a.shape, mybir.dt.from_np(a.dtype), kind="ExternalInput").ap()
         for k, a in arrays.items()}
    out = nc.dram_tensor("out", (B, L, D), F32, kind="ExternalOutput").ap()
    decoder_layer(nc, t, out)
    r = run_bass_kernel_spmd(nc, [{f"in_{k}": a for k, a in arrays.items()}], core_ids=[0])
    return r.results[0]["out"]
```

```python
from contextlib import ExitStack

import concourse.bass as bass
from concourse import mybir

ALU = mybir.AluOpType
ACT = mybir.ActivationFunctionType
F32 = mybir.dt.float32
I32 = mybir.dt.int32
BF16 = mybir.dt.bfloat16
AX_X = mybir.AxisListType.X

P = 128
B, L, D = 4, 256, 256
C = L // P
KD = D // P
HID, H, PH, N = 512, 64, 8, 128
MZ = HID // P
MX = (HID + 2 * N) // P
WIN = HID + MX * P + P
E = 4
VOCAB = 12500
EPS = 1e-5
QH, QK, QV = 16, 8, 16
DK, DV = 128, 256
PAIR_AT = [sum(B - d for d in range(lag)) for lag in range(B)]
NPAIR = sum(B - d for d in range(B))

LEVELS = [(128, 32), (32, 8), (8, 2), (2, 1)]
NL = len(LEVELS)
QUARTER = P // 4
SRC = [(lv, i) for lv in range(NL - 1) for i in range(1, 4)]
NS = len(SRC)
SEAM = NS + NL
NSLOT = SEAM + 1
EARLY = 8
BY_POOL = 4
USES = [NL, NL + 1]
NU = sum(USES)
SUMMED = [n - NL + 1 for n in USES]
NTERM = NU + C


def shape_constants():
    import numpy as np
    t = np.arange(P)
    k, j = t[:, None], t[None, :]
    decay = np.zeros((P, NSLOT + 1, P), np.float32)
    for s, (lv, i) in enumerate(SRC):
        par, blk = LEVELS[lv]
        start = (j // par) * par + i * blk
        decay[:, s] = (k // par == j // par) & (k > j) & (k < start)
    cb = np.zeros((P, NL, P), np.float32)
    for lv, (par, blk) in enumerate(LEVELS):
        tgt = j if lv == NL - 1 else t.reshape(P // par, 4, blk).transpose(1, 0, 2).reshape(1, P)
        decay[:, NS + lv] = (k // blk == tgt // blk) & (k <= tgt)
        cb[:, lv] = (k // par == tgt // par) & (k < tgt // blk * blk)
    decay[:, SEAM] = k > j
    decay[:, SEAM + 1] = k <= j
    ident = np.eye(P, dtype=np.float32)
    inv_freq = (1.0 / np.float32(10000.0) ** (np.arange(0, QK, 2, dtype=np.float32) / np.float32(QK))).astype(np.float32)
    ang = np.arange(B, dtype=np.float32)[:, None] * inv_freq[None, :]
    cos, sin = np.cos(ang), np.sin(ang)
    rot = np.zeros((P, C, B, 2, QK), np.float32)
    rot[:, :, :, 0] = np.concatenate([cos, cos], 1)
    rot[:, :, :, 1] = np.concatenate([-sin, sin], 1)
    sign = np.ones((P, 1), np.float32)
    sign[P // 2:] = -1.0
    return {"decay_masks": decay.reshape(P, -1), "cb_masks": cb.reshape(P, -1), "ident": ident,
            "rot": rot.reshape(P, -1), "sign": sign}


def decoder_layer(nc, t, out):
    ctx = ExitStack()
    with ctx:
        def sb(name, shape, dt=F32):
            return ctx.enter_context(nc.sbuf_tensor(name, shape, dt))

        def sem(name):
            return ctx.enter_context(nc.semaphore(name))

        PS = ctx.enter_context(nc.psum_tensor("PS", [P, 8, 512], F32))

        x_all = sb("x_all", [P, C * B, D])
        w_out = sb("w_out", [P, MZ, D])
        conv_w = sb("conv_w", [P, MX, 4])
        norm_w = sb("norm_w", [P, MZ])
        d_bc = sb("d_bc", [P, H])
        dt_bias = sb("dt_bias", [P, 1])
        a_log = sb("a_log", [P, 1])
        sign = sb("sign", [P, 1])
        ident = sb("ident_sb", [P, P])
        decay_m = sb("decay_m", [P, NSLOT + 1, P], BF16)
        dta_parts = sb("dta_parts", [P, 3, B * C, H], BF16)
        cb_m = sb("cb_m", [P, NL, P])
        ctxw = sb("ctxw", [P, E, KD, D])
        w_qkr = sb("w_qkr", [P, KD, 2 * DK + QH])
        w_vg = sb("w_vg", [P, KD, 2 * DV])
        conv3_w = sb("conv3_w", [P, KD, 2])
        rw = sb("rw", [P, QH, QV, 2])
        w_out3 = sb("w_out3", [P, KD, D])
        rot = sb("rot_sb", [P, C * B, 2, QK])

        mask = sb("mask", [P, E, B * L], BF16)

        st = sb("st", [P, B * C, 6])
        mv = sb("mv", [P, B * C, 2])
        ve = sb("ve", [P, B * C])
        rs = sb("rs", [P, B * C])
        mhalf = sb("mhalf", [P, B * C])
        eps_col = sb("eps_col", [P, 1])
        ones = sb("ones", [P, 1])
        avec = sb("avec", [P, 1])
        zT_all = sb("zT_all", [P, MZ, B * L])
        xs_all = sb("xs_all", [P, B * C, HID])
        cb_all = sb("cb_all", [P, B, C + 1, P])
        dtok_all = sb("dtok_all", [P, B * C, P])

        ARENA = 28100
        arena = sb("arena", [P, ARENA])

        def places(region, at, *shapes):
            views = []
            for shape in shapes:
                size = 1
                for n in shape:
                    size *= n
                assert at + size <= region.shape[1]
                v = region[:, at:at + size]
                names = "abcde"[:len(shape)]
                if len(shape) > 1:
                    v = v.rearrange(f"p ({' '.join(names)}) -> p {' '.join(names)}",
                                    **dict(zip(names[1:], shape[1:])))
                views.append(v)
                at += size
            return views

        hT_all, acc, xc, dt_raw, sp1, sp2 = places(
            arena, 0, (KD, B * L), (MX, L), (MX, L), (B * L,), (B * L,), (B * L,))
        ex_all, src = places(arena, 0, (B, NSLOT, C, H), (C, NS, HID))
        CHUNKS = B * NSLOT * C * H + C * NS * HID
        decay_f, dta_rest = places(arena, (KD * B + 2 * MX + 3 * B) * L, (NSLOT + 1, P), (B * C, H))
        assert (KD * B + 2 * MX + 3 * B) * L + (NSLOT + 1) * P + B * C * H <= CHUNKS
        cbm, junk, xsd, srcx, coefd, yzT, sq, cbd, ms, rms, term = places(
            arena, CHUNKS, (C, NL + 1, P), (C, P), (C, HID), (HID,), (C, H), (C, MZ, P), (C, MZ, P),
            (C,), (C,), (C,), (NTERM, HID))
        h_sb, ids_f, ge_f, w_in = places(arena, CHUNKS, (2, C, D), (B * L,), (3, B * L // 2), (KD, WIN))
        ids = ids_f.bitcast(I32)
        ge = ge_f.bitcast(BF16)

        (h2, hm, st2, mv2, ve2, rs2, st3, mv3, ve3, rs3, q_all, k_all, v_all, g_all, delta, rwd, h3, sg, p,
         h3_prev, cacc, xc3, qkr, ra, rb, wv_part, wv_mean, prod, pv, wl, eq, ind, th, cnt, sc, var, rsh, dev,
         osq) = places(
            arena, 0, (2, D), (E, KD, L), (2, 6), (2, 2), (2,), (2,), (2, 6), (2, 2), (2,), (2,),
            (C * B, DK), (C * B, DK), (C * B, DV), (C * B, DV), (C * B, QH), (DV,), (2, D), (KD, L), (KD, L),
            (C * 3, KD, P), (2, KD, P), (2, KD, P), (2, 2 * DK + QH), (2, 2 * DK), (2, 2 * DK), (KD, DV), (KD, QH),
            (C, NPAIR * DK), (C, NPAIR * DV), (C, NPAIR * QH), (C, NPAIR * QH), (C, B * QH), (C, B * QH),
            (C, B * QH), (C, B * QH), (C, B * QH), (C, B * QH), (C, B * QH), (C, B * DV))
        assert 2 * D + E * KD * L + 64 <= 2 * NSLOT * C * H
        pm, ogT = places(zT_all.rearrange("p m t -> p (m t)"), 0, (E, KD, L), (C, B, KD, P))
        og, = places(xs_all.rearrange("p i n -> p (i n)"), 0, (C, B * DV))
        OUT_BANKS = ((2, 3), (4, 5))

        def after(b, per, k):
            return per * (b + 1) + k

        def before(b, per, k):
            return per * b + k

        sems = {}

        def counted(name, per):
            sems[name] = (sem(name), per)
            return sems[name][0]

        in_x = [sem(f"in_x{pair}") for pair in range(B // 2)]
        in_ident, in_dt, in_w1, in_small, in_const, in_ids, in_late = (sem(n) for n in
            ("in_ident", "in_dt", "in_w1", "in_small", "in_const", "in_ids", "in_late"))
        v_setup = sem("v_setup")
        pool_setup = sem("pool_setup")
        eps_set = sem("eps_set")
        split_ready = sem("split_ready")
        w_out_ready = sem("w_out_ready")
        var_ready = sem("var_ready")
        rstd_ready = counted("rstd_ready", 1)
        h_ready = counted("h_ready", 2)
        hT_ps = counted("hT_ps", 2)
        hT_sb = counted("hT_sb", 2)
        xbc_ps = counted("xbc_ps", 3)
        z_ps = counted("z_ps", 1)
        tap3 = counted("tap3", 3)
        taps = counted("taps", 18)
        z_sb = counted("z_sb", 1)
        xc_ready = counted("xc_ready", 3)
        tok_ps = counted("tok_ps", 3)
        tok_sb = counted("tok_sb", 3)
        sp_act = sem("sp_act")
        sp_dve = sem("sp_dve")
        dt_ps = sem("dt_ps")
        dtT_ready = sem("dtT_ready")
        dtok_ps, dtok_sb = sem("dtok_ps"), sem("dtok_sb")
        ex_ps = counted("ex_ps", 2)
        ex_sb = counted("ex_sb", 2)
        cbm_ready = counted("cbm_ready", 2)
        xsd_ready = counted("xsd_ready", 2)
        src0_ready = counted("src0_ready", 4)
        start_ready = sem("start_ready")
        src1_ready = counted("src1_ready", 2)
        srcx_ready = counted("srcx_ready", 1)
        p_ps = counted("p_ps", NU)
        p_taken = counted("p_taken", NU)
        diag_ready = counted("diag_ready", 2)
        diag_sum = counted("diag_sum", 2)
        coef_ready = counted("coef_ready", 2)
        own_ready = counted("own_ready", 2)
        seam_ready = counted("seam_ready", 1)
        summed = counted("summed", sum(SUMMED))
        yT_ps = counted("yT_ps", 2)
        yz_ready = counted("yz_ready", 2)
        sq_ready = counted("sq_ready", 2)
        o1_ps = counted("o1_ps", 2)
        ms_ready = counted("ms_ready", 2)
        rms_ready = counted("rms_ready", 2)
        x1_ready = counted("x1_ready", 2)
        masks_ready = sem("masks_ready")
        ln2 = counted("ln2", 5)
        rs2_ready = counted("rs2_ready", 1)
        h2_ready = counted("h2_ready", 1)
        h2T_ps = counted("h2T_ps", 1)
        hm_ready = counted("hm_ready", 1)
        s_ps = counted("s_ps", 1)
        sg_ready = counted("sg_ready", 1)
        p_ready = counted("p_ready", 1)
        pm_ready = counted("pm_ready", 1)
        y2_ps = counted("y2_ps", 1)
        x2_ready = counted("x2_ready", 1)
        set3 = sem("set3")
        ln3 = counted("ln3", 5)
        rs3_ready = counted("rs3_ready", 1)
        pm_far_ready = counted("pm_far_ready", 1)
        h3_ready = counted("h3_ready", 1)
        h3T_ps = counted("h3T_ps", 1)
        h3T_sb = counted("h3T_sb", 1)
        conv3 = counted("conv3", 3)
        xc3_ready = counted("xc3_ready", 2)
        pr_ps = counted("pr_ps", 2)
        pr_sb = counted("pr_sb", 3)
        rot_same = counted("rot_same", 1)
        rot_cross = counted("rot_cross", 1)
        rot_ready = counted("rot_ready", 2)
        dl_ready = counted("dl_ready", 1)
        th_ready, prod0_ready, wl_ready, pv_pool, pv_far = (sem(n) for n in
            ("th_ready", "prod0_ready", "wl_ready", "pv_pool", "pv_far"))
        chain3 = sem("chain3")
        oc_ready, osq_ready, ocg_ready, hvar_ready, dev_ready, inv_ready = (sem(n) for n in
            ("oc_ready", "osq_ready", "ocg_ready", "hvar_ready", "dev_ready", "inv_ready"))
        pairs_done = sem("pairs_done")
        og_ready = [sem(f"og_ready{c}") for c in range(C)]
        ogT_ps, ogT_sb, o3_ps, out_ready = (sem(n) for n in ("ogT_ps", "ogT_sb", "o3_ps", "out_ready"))
        stored = sem("stored")

        def prev_slot(j):
            return j + (j // 2 if isinstance(j, int) else 0)

        def by_rotated(ap):
            return ap.rearrange("p i (h d) -> p i h d", d=QK)

        def rotation(j, part, a, z):
            return rot[:, bass.ds(2 * j, 2), part, a:z].unsqueeze(2).broadcast_to([P, 2, 2 * QH, z - a])

        def two_positions(i):
            return slice(2 * i * DV, (2 * i + 2) * DV)

        def of_pair(ap, pair):
            return ap.rearrange("p (c b) -> p c b", c=C)[:, :, 2 * pair:2 * pair + 2]

        def passes(eng, body):
            body(0, first=True, last=False)
            with eng.Fori(1, B - 1) as b:
                body(b, first=False, last=False)
            body(B - 1, first=False, last=True)

        def tok(ap, b):
            return ap[..., bass.ts(b, L)]

        def heads(ap):
            return ap.rearrange("p (h d) -> p h d", d=PH)

        def over_head(ap):
            return ap.unsqueeze(2).broadcast_to([P, H, PH])

        def levels_of(c):
            return [*range(NL)] if c == 0 else ["seam", *range(NL)]

        def by_block(ap, lv):
            par, blk = LEVELS[lv]
            return ap.rearrange("p (q i r) -> p i q r", i=4, r=blk)

        def product_bank(u):
            return 4 + (u % 2 if u > 1 else 1 - u)

        def terms(c):
            at = sum(USES[:c]) + c
            return [*range(at, at + USES[c] + 1)]

        block = ctx.enter_context(nc.Block())

        @block.sync
        def _(sp):
            for pair in range(B // 2):
                for c in range(C):
                    s0 = c * B + 2 * pair
                    sp.dma_start(x_all[:, s0:s0 + 2, :],
                                 t["x"][2 * pair:2 * pair + 2, c * P:(c + 1) * P, :].rearrange("b p d -> p b d"))\
                        .then_inc(in_x[pair], 16)
            sp.dma_start(ident[:, :], t["ident"]).then_inc(in_ident, 16)
            w_in_dram = t["w_in"].rearrange("(k p) n -> p k n", p=P)
            sp.dma_start(w_in[:, :, WIN - P:], w_in_dram[:, :, WIN - P:]).then_inc(in_dt, 16)
            sp.dma_start(dt_bias[:, :], t["dt_bias"]).then_inc(in_dt, 16)
            sp.dma_start(a_log[:, :], t["a_log"]).then_inc(in_dt, 16)
            sp.dma_start(sign[:, :], t["sign"]).then_inc(in_dt, 16)
            sp.dma_start(w_in[:, :, 0:WIN - P], w_in_dram[:, :, 0:WIN - P]).then_inc(in_w1, 16)
            sp.dma_start(conv_w[:, :, :], t["conv_w"].rearrange("(m p) k -> p m k", p=P)).then_inc(in_w1, 16)
            sp.dma_start(norm_w[:, :], t["norm_w"].rearrange("(m p) -> p m", p=P),
                         allow_slow_non_contiguous=True).then_inc(in_small, 16)
            sp.dma_start(d_bc[:, :], t["d"].partition_broadcast(P)).then_inc(in_small, 16)
            sp.dma_start(w_out[:, :, :], t["w_out"].rearrange("(m p) n -> p m n", p=P)).then_inc(in_small, 16)
            sp.dma_start(decay_f[:, :, :], t["decay_masks"].rearrange("p (s j) -> p s j", j=P)).then_inc(in_const, 16)
            sp.dma_start(cb_m[:, :, :], t["cb_masks"].rearrange("p (s j) -> p s j", j=P)).then_inc(in_const, 16)
            for c in range(C):
                sp.dma_start(ids[:, c * B * P:(c + 1) * B * P].rearrange("p (b t) -> p b t", b=B),
                             t["ids"][:, c * P:(c + 1) * P].partition_broadcast(P)).then_inc(in_ids, 16)
            sp.dma_start(ctxw[:, :, :, :], t["ctxT"].rearrange("e (k p) n -> p e k n", p=P)).then_inc(in_late, 16)
            for dst, a, z in ((w_qkr[:, :, 0:2 * DK], 0, 2 * DK), (w_vg[:, :, :], 2 * DK, 2 * DK + 2 * DV)):
                sp.dma_start(dst, t["w3"][:, a:z].rearrange("(k p) n -> p k n", p=P)).then_inc(in_late, 16)
            sp.dma_start(conv3_w[:, :, :], t["conv3_w"].rearrange("(k p) w -> p k w", p=P)).then_inc(in_late, 16)
            sp.dma_start(rw[:, :, :, :], t["router_w"].partition_broadcast(P)).then_inc(in_late, 16)
            sp.dma_start(w_out3[:, :, :], t["w_out3"].rearrange("(k p) n -> p k n", p=P)).then_inc(in_late, 16)
            sp.dma_start(rot[:, :, :, :], t["rot"].rearrange("p (i s d) -> p i s d", i=C * B, s=2))\
                .then_inc(in_late, 16)
            for c in range(C):
                for i in range(2):
                    sp.wait_ge(out_ready, 2 * c + i + 1)
                    slots = slice(c * B + 2 * i, c * B + 2 * i + 2)
                    sp.dma_start(out[2 * i:2 * i + 2, c * P:(c + 1) * P, :].rearrange("b p d -> p b d"),
                                 x_all[:, slots, :]).then_inc(stored, 16)
            sp.wait_ge(stored, 16 * 2 * C)

        @block.tensor
        def _(pe):
            for name in ("hT_ps", "xbc_ps", "z_ps", "tok_ps", "ex_ps", "p_ps", "yT_ps", "o1_ps",
                         "h2T_ps", "s_ps", "y2_ps", "h3T_ps", "pr_ps"):
                pe.sem_inc(*sems[name])
            pe.wait_ge(in_ident, 16)
            with pe.Fori(0, B // 2) as pair:
                for i in range(2):
                    pe.wait_ge(hT_sb, before(pair, 2, i + 1))
                    pe.wait_ge(h_ready, after(pair, 2, i + 1))
                    for c in range(C):
                        for k in range(KD):
                            mm = pe.transpose(PS[:, 6 + i, k * L + c * P:k * L + (c + 1) * P],
                                              h_sb[:, i, c, k * P:(k + 1) * P], ident[:, :])
                    mm.then_inc(hT_ps, 1)
            pe.wait_ge(in_dt, 64)
            for i in range(2):
                pe.wait_ge(hT_sb, after(i, 2, 2))
                for k in range(KD):
                    mm = pe.matmul(PS[:, i, :], w_in[:, k, WIN - P:WIN], hT_all[:, k, i * 2 * L:(i + 1) * 2 * L],
                                   start=(k == 0), stop=(k == KD - 1))
                mm.then_inc(dt_ps, 1)
            pe.wait_ge(in_w1, 32)

            def xbc_product(b):
                for q in range(MX // 2):
                    pe.wait_ge(taps, before(b, 18, 6 * q + 6))
                    for m in range(2):
                        for k in range(KD):
                            col = HID + (2 * q + m) * P
                            mm = pe.matmul(PS[:, 2 + q, m * L:(m + 1) * L], w_in[:, k, col:col + P],
                                           hT_all[:, k, bass.ts(b, L)], start=(k == 0), stop=(k == KD - 1))
                    mm.then_inc(xbc_ps, 1)

            def z_product(b):
                pe.wait_ge(z_sb, before(b, 1, 1))
                for m in range(MZ):
                    for k in range(KD):
                        mm = pe.matmul(PS[:, m // 2, (m % 2) * L:(m % 2 + 1) * L], w_in[:, k, m * P:(m + 1) * P],
                                       hT_all[:, k, bass.ts(b, L)], start=(k == 0), stop=(k == KD - 1))
                mm.then_inc(z_ps, 1)

            def by_token(b):
                pe.wait_ge(tok_sb, before(b, 3, 3))
                pe.wait_ge(dtok_sb, 1)
                for c in range(C):
                    pe.wait_ge(xc_ready, after(b, 3, 2 + c))
                    for m in range(MZ):
                        mm = pe.transpose(PS[:, 7 - c, m * P:(m + 1) * P], xc[:, m, c * P:(c + 1) * P], ident[:, :])
                    mm.then_inc(tok_ps, 1)
                for s, (cj, ci) in enumerate(((0, 0), (1, 1), (0, 1))):
                    mm = pe.matmul(PS[:, 5, s * P:(s + 1) * P], xc[:, MZ, cj * P:(cj + 1) * P],
                                   xc[:, MZ + 1, ci * P:(ci + 1) * P], start=True, stop=True)
                mm.then_inc(tok_ps, 1)

            def in_projection(b, first, last):
                xbc_product(b)
                if not first:
                    by_token(b - 1)
                else:
                    pe.wait_ge(sp_act, 2)
                    pe.wait_ge(sp_dve, 2)
                z_product(b)
                if first:
                    pe.wait_ge(dtT_ready, 1)
                    for i in range(B * C):
                        mm = pe.transpose(PS[:, 6 + i // 4, (i % 4) * P:(i % 4 + 1) * P],
                                          dt_raw[:, i * P:(i + 1) * P], ident[:, :])
                    mm.then_inc(dtok_ps, 1)

            passes(pe, in_projection)

            def exponents(b):
                pe.wait_ge(ex_sb, before(b, 2, 2))
                EX = PS[:, 0:4, :].rearrange("p a (s c h) -> p (a s) c h", c=C, h=H)
                for s in range(SEAM):
                    for n in range(3):
                        mm = pe.matmul(EX[:, s], decay_m[:, s, :], dta_parts[:, n, bass.ts(b, C), :],
                                       start=(n == 0), stop=(n == 2))
                    if s == EARLY - 1:
                        mm.then_inc(ex_ps, 1)
                for c in range(C):
                    for n in range(3):
                        mm = pe.matmul(EX[:, SEAM, c], decay_m[:, SEAM + c, :], dta_parts[:, n, b * C + c, :],
                                       start=(n == 0), stop=(n == 2))
                mm.then_inc(ex_ps, 1)

            def product(b, c, u, lv):
                if u < 2:
                    pe.wait_ge(p_taken, before(b, NU, NU - 1 + u))
                else:
                    pe.wait_ge(p_taken, after(b, NU, max(u - 1, 2)))
                bank = PS[:, product_bank(u), :]
                if lv == "seam":
                    pe.wait_ge(seam_ready, after(b, 1, 1))
                    pe.wait_ge(srcx_ready, after(b, 1, 1))
                    mm = pe.matmul(bank, cbm[:, 1, NL, :], srcx[:, :], start=True, stop=True)
                elif lv == NL - 1:
                    mm = pe.matmul(bank, cbm[:, c, lv, :], xsd[:, c, :], start=True, stop=True)
                else:
                    pe.wait_ge(src0_ready, after(b, 4, 2 * c + (2 if lv else 1)))
                    if lv:
                        pe.wait_ge(src1_ready, after(b, C, c + 1))
                    for i in range(4):
                        rows = slice(i * QUARTER, (i + 1) * QUARTER)
                        mm = pe.matmul(PS[rows, product_bank(u), :], cbm[:, c, lv, rows],
                                       src[:, c, SRC.index((lv, max(i, 1))), :], start=True, stop=True)
                mm.then_inc(p_ps, 1)

            def sum_terms(b, c):
                pe.wait_ge(p_taken, after(b, NU, sum(USES[:c + 1])))
                pe.wait_ge(summed, after(b, sum(SUMMED), sum(SUMMED[:c + 1])))
                pe.wait_ge(yz_ready, after(b, C, c) if c else before(b, C, C))
                mine = [(terms(c)[0], "own")] + [(terms(c)[1 + j], levels_of(c)[j]) for j in range(SUMMED[c], USES[c])]
                for m in range(MZ):
                    for j, lv in mine:
                        out_t = PS[:, 6, m * P:(m + 1) * P]
                        if lv in range(1, NL - 1):
                            out_t = by_block(out_t, lv)
                        mm = pe.matmul(out_t, term[:, j, m * P:(m + 1) * P], ident[:, :],
                                       is_transpose=True, start=(j == mine[0][0]), stop=(j == mine[-1][0]))
                mm.then_inc(yT_ps, 1)

            def project(b, c):
                pe.wait_ge(yz_ready, after(b, C, c + 1))
                pe.wait_ge(x1_ready, after(b, C, c) if c else before(b, C, C))
                for m in range(MZ):
                    pe.matmul(PS[:, 7, 0:D], yzT[:, c, m, :], w_out[:, m, :], start=(m == 0), stop=(m == MZ - 1))

            def square_sum(b, c):
                pe.wait_ge(sq_ready, after(b, C, c + 1))
                for m in range(MZ):
                    mm = pe.matmul(PS[:, 7, D:D + 1], sq[:, c, m, :], ones[:, :], start=(m == 0), stop=(m == MZ - 1))
                mm.then_inc(o1_ps, 1)

            def expert_transpose(j):
                pe.wait_ge(hm_ready, before(j, 1, 1))
                pe.wait_ge(h2_ready, after(j, 1, 1))
                for c in range(C):
                    for k in range(KD):
                        mm = pe.transpose(PS[:, 0, k * L + c * P:k * L + (c + 1) * P],
                                          h2[:, c, k * P:(k + 1) * P], ident[:, :])
                mm.then_inc(h2T_ps, 1)

            def chunks(b, first, last):
                for c in range(C):
                    gate = (b, 0) if c else (b - 1, 1)
                    pe.wait_ge(cbm_ready, after(b, C, c + 1))
                    pe.wait_ge(xsd_ready, after(b, C, c + 1))
                    for j, lv in enumerate(levels_of(c)):
                        product(b, c, sum(USES[:c]) + j, lv)
                        if not (first and c == 0) and j == 1:
                            sum_terms(*gate)
                        if c == 0 and j == 1 and not last:
                            exponents(b + 1)
                        if not (first and c == 0):
                            if j == 2:
                                project(*gate)
                            if j == 3:
                                square_sum(*gate)
                        if last and c and j == 1:
                            pe.wait_ge(ex_sb, after(B - 1, 2, 2))
                            expert_transpose(0)

            pe.wait_ge(split_ready, 5)
            pe.wait_ge(z_sb, after(B - 1, 1, 1))
            pe.wait_ge(taps, after(B - 1, 18, 12))
            exponents(0)
            by_token(B - 1)
            pe.wait_ge(w_out_ready, 1)
            pe.wait_ge(taps, after(B - 1, 18, 18))
            pe.wait_ge(tok_sb, after(B - 1, 3, 3))
            pe.wait_ge(start_ready, 1)
            passes(pe, chunks)

            pe.wait_ge(in_late, 112)

            def up(b, m):
                pe.wait_ge(hm_ready, after(b, 1, 1))
                pe.wait_ge(p_ready, before(b, 1, 1))
                for e in range(E):
                    for k in range(KD):
                        mm = pe.matmul(PS[:, 1, m * L:(m + 1) * L], ctxw[:, e, k, m * P:(m + 1) * P],
                                       hm[:, e, k, :], start=(e == 0 and k == 0), stop=(e == E - 1 and k == KD - 1))
                if m == KD - 1:
                    mm.then_inc(s_ps, 1)

            def down(b):
                pe.wait_ge(pm_ready, after(b, 1, 1))
                pe.wait_ge(x2_ready, before(b, 1, 1))
                for c in range(C):
                    for e in range(E):
                        if c == 0 and e == E // 2:
                            pe.wait_ge(pm_far_ready, after(b, 1, 1))
                        for k in range(KD):
                            mm = pe.matmul(PS[:, 2, c * D:(c + 1) * D], pm[:, e, k, c * P:(c + 1) * P],
                                           ctxw[:, e, k, :], start=(e == 0 and k == 0),
                                           stop=(e == E - 1 and k == KD - 1))
                mm.then_inc(y2_ps, 1)

            def retention_transpose(b):
                pe.wait_ge(h3T_sb, before(b, 1, 1))
                pe.wait_ge(h3_ready, after(b, 1, 1))
                for c in range(2):
                    for k in range(KD):
                        mm = pe.transpose(PS[:, 3, (c * KD + k) * P:(c * KD + k + 1) * P],
                                          h3[:, c, k * P:(k + 1) * P], ident[:, :])
                mm.then_inc(h3T_ps, 1)

            def queries_keys(b):
                pe.wait_ge(pr_sb, before(b, 3, 3))
                pe.wait_ge(set3, 6)
                for c in range(2):
                    pe.wait_ge(xc3_ready, after(b, 2, c + 1))
                    for k in range(KD):
                        mm = pe.matmul(PS[:, 4 + c, 0:2 * DK + QH], xc3[:, c, k, :], w_qkr[:, k, :],
                                       start=(k == 0), stop=(k == KD - 1))
                mm.then_inc(pr_ps, 1)

            def values_gates(b, slots=(0, 1)):
                for c in slots:
                    for k in range(KD):
                        mm = pe.matmul(PS[:, 6 + c, :], xc3[:, c, k, :], w_vg[:, k, :],
                                       start=(k == 0), stop=(k == KD - 1))
                if slots[-1]:
                    mm.then_inc(pr_ps, 1)

            def experts(b, first, last):
                up(b, 0)
                if first:
                    sum_terms(B - 1, 1)
                else:
                    retention_transpose(b - 1)
                up(b, 1)
                if not first:
                    queries_keys(b - 1)
                    values_gates(b - 1, (0,) if last else (0, 1))
                if not last:
                    expert_transpose(b + 1)
                if first:
                    project(B - 1, 1)
                    square_sum(B - 1, 1)
                down(b)
                if last:
                    values_gates(b - 1, (1,))

            passes(pe, experts)
            retention_transpose(B - 1)
            queries_keys(B - 1)
            values_gates(B - 1)

            pe.wait_ge(x2_ready, after(B - 1, 1, 1))
            pe.wait_ge(h3T_sb, after(B - 1, 1, 1))
            for c in range(C):
                for i in range(2):
                    pe.wait_ge(og_ready[c], i + 1)
                    if c:
                        pe.wait_ge(ogT_sb, i + 1)
                    for b in range(2):
                        for k in range(KD):
                            col = (b * KD + k) * P
                            mm = pe.transpose(PS[:, i, col:col + P],
                                              og[:, c, 2 * i * DV + col:2 * i * DV + col + P], ident[:, :])
                    mm.then_inc(ogT_ps, 1)
                if c:
                    pe.wait_ge(pr_sb, after(B - 1, 3, 1))
                else:
                    pe.wait_ge(wl_ready, C)
                for i in range(2):
                    pe.wait_ge(ogT_sb, 2 * c + i + 1)
                    for b in range(2):
                        for k in range(KD):
                            mm = pe.matmul(PS[:, OUT_BANKS[c][i], b * D:(b + 1) * D], ogT[:, c, 2 * i + b, k, :],
                                           w_out3[:, k, :], start=(k == 0), stop=(k == KD - 1))
                    mm.then_inc(o3_ps, 1)

        @block.scalar
        def _(act):
            for name in ("hT_sb", "tap3", "z_sb", "xc_ready", "tok_sb", "ex_sb", "sq_ready", "diag_sum", "seam_ready",
                         "sg_ready", "h3T_sb", "xc3_ready", "pr_sb"):
                act.sem_inc(*sems[name])
            act.preload_act_table_set("natural_log_exp_and_others")
            act.wait_ge(in_ident, 16)
            with act.Fori(0, B // 2) as pair:
                for i in range(2):
                    act.wait_ge(hT_ps, after(pair, 2, i + 1))
                    act.wait_ge(in_ident, 16)
                    act.activation(hT_all[:, :, bass.ds((2 * pair + i) * L, L)],
                                   PS[:, 6 + i, :].rearrange("p (k t) -> p k t", k=KD), ACT.Copy).then_inc(hT_sb, 1)

            act.wait_ge(in_dt, 64)
            for i in range(2):
                act.wait_ge(dt_ps, i + 1)
                act.activation(sp1[:, i * 2 * L:(i + 1) * 2 * L], PS[:, i, :], ACT.Abs, bias=dt_bias[:, :])\
                    .then_inc(sp_act, 1)
            act.wait_ge(sp_act, 2)
            act.activation(sp2[:, :], sp1[:, :], ACT.Exp, scale=-1.0).then_inc(sp_act, 1)
            act.activation(avec[:, :], a_log[:, :], ACT.Exp).then_inc(sp_act, 1)
            act.wait_ge(sp_act, 3)
            act.activation(sp1[:, :], sp2[:, :], ACT.Ln, bias=1.0).then_inc(sp_act, 1)
            act.preload_act_table_set("silu_and_others")
            act.wait_ge(in_w1, 32)

            def copy_by_token(b):
                for c in range(C):
                    act.wait_ge(tok_ps, after(b, 3, c + 1))
                    act.wait_ge(in_w1, 32)
                    act.activation(xs_all[:, b * C + c, :], PS[:, 7 - c, :], ACT.Copy).then_inc(tok_sb, 1)
                act.wait_ge(tok_ps, after(b, 3, 3))
                act.wait_ge(in_w1, 32)
                act.activation(cb_all[:, b, :, :], PS[:, 5, 0:3 * P].rearrange("p (s i) -> p s i", i=P), ACT.Copy)\
                   .then_inc(tok_sb, 1)

            def in_projection(b, first, last):
                for q in range(MX // 2):
                    act.wait_ge(xbc_ps, after(b, 3, q + 1))
                    act.wait_ge(xc_ready, before(b, 3, q + 1))
                    for m in range(2):
                        ins = act.activation(acc[:, 2 * q + m, :], PS[:, 2 + q, m * L:(m + 1) * L], ACT.Identity,
                                             scale=conv_w[:, 2 * q + m, 3:4])
                    ins.then_inc(tap3, 1)
                if not first:
                    copy_by_token(b - 1)
                act.wait_ge(z_ps, after(b, 1, 1))
                act.wait_ge(in_w1, 32)
                act.activation(tok(zT_all[:, :, :], b), PS[:, 0:2, :].rearrange("p a (m t) -> p (a m) t", t=L),
                               ACT.Silu).then_inc(z_sb, 1)
                act.wait_ge(tok_ps, before(b, 3, 3))
                for q in range(MX // 2):
                    act.wait_ge(taps, after(b, 18, 6 * q + 6))
                    act.activation(xc[:, 2 * q:2 * q + 2, :], acc[:, 2 * q:2 * q + 2, :], ACT.Silu)\
                       .then_inc(xc_ready, 1)
                if first:
                    act.wait_ge(dtok_ps, 1)
                    act.activation(dtok_all[:, :, :], PS[:, 6:8, :].rearrange("p a (s h) -> p (a s) h", h=P), ACT.Copy)\
                       .then_inc(dtok_sb, 1)

            passes(act, in_projection)
            act.preload_act_table_set("natural_log_exp_and_others")

            EX = PS[:, 0:4, :].rearrange("p a (s c h) -> p (a s) (c h)", c=C, h=H)

            def decays(b):
                ex = ex_all[:, b, :, :, :].rearrange("p s c h -> p s (c h)")
                act.wait_ge(ex_ps, after(b, 2, 1))
                act.wait_ge(in_w1, 32)
                act.activation(ex[:, 0:EARLY], EX[:, 0:EARLY], ACT.Exp).then_inc(ex_sb, 1)
                act.wait_ge(ex_ps, after(b, 2, 2))
                act.wait_ge(in_w1, 32)
                act.activation(ex[:, EARLY:NSLOT], EX[:, EARLY:NSLOT], ACT.Exp).then_inc(ex_sb, 1)

            def squares(b, c):
                act.wait_ge(o1_ps, before(b, C, c + 1))
                act.wait_ge(yz_ready, after(b, C, c + 1))
                act.activation(sq[:, c, :, :], yzT[:, c, :, :], ACT.Square).then_inc(sq_ready, 1)

            def seam_copy(b):
                act.wait_ge(p_taken, before(b, NU, USES[0] + 1))
                act.wait_ge(in_w1, 32)
                act.activation(cbm[:, 1, NL, :], cb_all[:, b, C, :], ACT.Copy).then_inc(seam_ready, 1)

            def diagonal(b, c):
                act.wait_ge(coef_ready, before(b, C, c + 1))
                act.wait_ge(diag_ready, after(b, C, c + 1))
                act.activation(junk[:, c, :], junk[:, c, :], ACT.Copy, accum_out=cbd[:, c:c + 1]).then_inc(diag_sum, 1)

            def chunks(b, first, last):
                seam_copy(b)
                if not first:
                    squares(b - 1, 1)
                if not last:
                    decays(b + 1)
                diagonal(b, 1)
                squares(b, 0)
                if not last:
                    diagonal(b + 1, 0)

            decays(0)
            copy_by_token(B - 1)
            diagonal(0, 0)
            passes(act, chunks)
            act.preload_act_table_set("silu_and_others")
            squares(B - 1, 1)


            def expert_silu(b):
                act.wait_ge(p_ready, before(b, 1, 1))
                act.wait_ge(s_ps, after(b, 1, 1))
                act.activation(sg[:, :, :], PS[:, 1, :].rearrange("p (k t) -> p k t", k=KD), ACT.Silu)\
                   .then_inc(sg_ready, 1)

            def retention_silu(j):
                act.wait_ge(pr_ps, before(j, 2, 2))
                for i in range(2):
                    act.wait_ge(conv3, after(j, 3, i + 2))
                    act.activation(xc3[:, i, :, :], cacc[:, i, :, :], ACT.Silu).then_inc(xc3_ready, 1)
                act.wait_ge(in_late, 112)
                act.activation(h3_prev[:, prev_slot(j) + 1, :, :],
                               PS[:, 3, KD * P:].rearrange("p (k t) -> p k t", k=KD), ACT.Copy).then_inc(h3T_sb, 1)

            def queries_keys_parts(j):
                act.wait_ge(rot_ready, before(j, 2, 2))
                act.wait_ge(pr_ps, after(j, 2, 1))
                act.activation(qkr[:, :, 0:DK], PS[:, 4:6, 0:DK], ACT.Silu)
                act.activation(qkr[:, :, DK:], PS[:, 4:6, DK:2 * DK + QH], ACT.Copy).then_inc(pr_sb, 1)

            def values_gates_parts(j):
                act.wait_ge(pr_ps, after(j, 2, 2))
                act.activation(v_all[:, bass.ds(2 * j, 2), :], PS[:, 6:8, 0:DV], ACT.Copy).then_inc(pr_sb, 1)
                act.activation(g_all[:, bass.ds(2 * j, 2), :], PS[:, 6:8, DV:2 * DV], ACT.Silu)\
                   .then_inc(pr_sb, 1)

            def scores(c):
                act.wait_ge(dl_ready, after(2 * c + 1, 1, 1))
                act.activation(th[:, c, :], delta[:, c * B:(c + 1) * B, :].rearrange("p b h -> p (b h)"), ACT.Tanh,
                               scale=0.5).then_inc(th_ready, 1)

            def head_squares(c):
                for i in range(2):
                    act.wait_ge(oc_ready, 2 * c + i + 1)
                    act.activation(osq[:, c, two_positions(i)], pv[:, c, two_positions(i)], ACT.Square)\
                       .then_inc(osq_ready, 1)

            def copy_ogT(c):
                for i in range(2):
                    act.wait_ge(ogT_ps, 2 * c + i + 1)
                    act.activation(ogT[:, c, 2 * i:2 * i + 2, :, :].rearrange("p b k t -> p (b k t)"), PS[:, i, :],
                                   ACT.Copy).then_inc(ogT_sb, 1)

            def head_deviations(c):
                act.wait_ge(hvar_ready, c + 1)
                act.activation(dev[:, c, :], var[:, c, :], ACT.Sqrt, scale=1.0 / QV, bias=eps_col[:, :])\
                   .then_inc(dev_ready, 1)

            def experts(b, first, last):
                if not first:
                    retention_silu(b - 1)
                expert_silu(b)
                if last:
                    scores(0)
                if not first:
                    queries_keys_parts(b - 1)
                    values_gates_parts(b - 1)

            passes(act, experts)
            retention_silu(B - 1)
            act.wait_ge(eps_set, 1)
            head_squares(0)
            queries_keys_parts(B - 1)
            scores(1)
            values_gates_parts(B - 1)
            head_deviations(0)
            copy_ogT(0)
            head_squares(1)
            head_deviations(1)
            copy_ogT(1)

        @block.gpsimd
        def _(pool):
            for name in ("rstd_ready", "cbm_ready", "src0_ready", "summed", "diag_ready", "rms_ready", "rs2_ready",
                         "rs3_ready", "pm_far_ready", "rot_cross"):
                pool.sem_inc(*sems[name])
            pool.memset(mhalf[:, :], -0.5).then_inc(pool_setup, 1)
            pool.memset(eps_col[:, :], EPS).then_inc(eps_set, 1)
            pool.wait_ge(pool_setup, 1)
            for pair in range(B // 2):
                pool.wait_ge(var_ready, pair + 1)
                pool.tensor_tensor(of_pair(rs, pair), of_pair(ve, pair), of_pair(mhalf, pair), ALU.pow)\
                    .then_inc(rstd_ready, 1)
            pool.wait_ge(in_ids, 32)
            per = VOCAB // E
            for i in range(E - 1):
                pool.tensor_scalar(ge[:, i, :], ids, float(per * (i + 1)), None, ALU.is_ge).then_inc(pool_setup, 1)
            pool.wait_ge(pool_setup, E)
            pool.tensor_scalar(mask[:, 0, :], ge[:, 0, :], -1.0, 1.0, ALU.mult, ALU.add)
            for i in range(1, E - 1):
                pool.tensor_tensor(mask[:, i, :], ge[:, i - 1, :], ge[:, i, :], ALU.subtract)
            pool.tensor_copy(mask[:, E - 1, :], ge[:, E - 2, :]).then_inc(masks_ready, 1)

            pool.wait_ge(masks_ready, 1)
            pool.wait_ge(in_const, 32)
            pool.wait_ge(tok_sb, after(0, 3, 3))

            pool.wait_ge(in_const, 32)
            pool.tensor_copy(decay_m[:, :, :], decay_f[:, :, :]).then_inc(split_ready, 1)
            dta = dtok_all[:, :, H:2 * H]
            pool.wait_ge(dtok_sb, 1)
            pool.tensor_copy(dta_parts[:, 0, :, :], dta).then_inc(split_ready, 1)
            pool.wait_ge(split_ready, 2)
            pool.tensor_tensor(dta_rest[:, :, :], dta, dta_parts[:, 0, :, :], ALU.subtract).then_inc(split_ready, 1)
            pool.wait_ge(split_ready, 3)
            pool.tensor_copy(dta_parts[:, 1, :, :], dta_rest[:, :, :]).then_inc(split_ready, 1)
            pool.wait_ge(split_ready, 4)
            pool.tensor_tensor(dta_parts[:, 2, :, :], dta_rest[:, :, :], dta_parts[:, 1, :, :], ALU.subtract)\
                .then_inc(split_ready, 1)

            def masked_products(b, c):
                pool.wait_ge(p_taken, before(b, NU, sum(USES[:c + 1])))
                pool.wait_ge(diag_sum, before(b, C, c + 1))
                pool.wait_ge(in_const, 32)
                pool.tensor_tensor(cbm[:, c, 0:NL:NL - 1, :], cb_m[:, 0:NL:NL - 1, :],
                                   cb_all[:, b, c, :].unsqueeze(1).broadcast_to([P, 2, P]), ALU.mult)
                for lv in range(1, NL - 1):
                    four = dict(i=4, r=LEVELS[lv][1])
                    ins = pool.tensor_tensor(cbm[:, c, lv, :].rearrange("p (i q r) -> p i q r", **four),
                                             cb_m[:, lv, :].rearrange("p (i q r) -> p i q r", **four),
                                             by_block(cb_all[:, b, c, :], lv), ALU.mult)
                ins.then_inc(cbm_ready, 1)
                pool.tensor_tensor(junk[:, c, :], cb_all[:, b, c, :], ident[:, :], ALU.mult).then_inc(diag_ready, 1)

            def first_sources(b, c, slots=range(BY_POOL)):
                pool.wait_ge(ex_sb, after(b, 2, 1))
                pool.wait_ge(xsd_ready, after(b, C, c + 1))
                pool.wait_ge(in_const, 32)
                first_level = [s for s in slots if SRC[s][0] == 0]
                for s in slots:
                    ins = pool.tensor_tensor(heads(src[:, c, s, :]), heads(xsd[:, c, :]),
                                             over_head(ex_all[:, b, s, c, :]), ALU.mult)
                    if s in (first_level[-1], slots[-1]):
                        ins.then_inc(src0_ready, 1)

            def add_term(b, c, j):
                own, n = terms(c)[0], sum(SUMMED[:c]) + j
                if j:
                    pool.wait_ge(summed, after(b, sum(SUMMED), n))
                else:
                    pool.wait_ge(own_ready, after(b, C, c + 1))
                pool.wait_ge(p_taken, after(b, NU, sum(USES[:c]) + j + 1))
                pool.tensor_tensor(term[:, own, :], term[:, own, :], term[:, terms(c)[1 + j], :], ALU.add)\
                    .then_inc(summed, 1)

            def inverse_rms(b, c):
                pool.wait_ge(ms_ready, after(b, C, c + 1))
                pool.tensor_tensor(rms[:, c:c + 1], ms[:, c:c + 1], mhalf[:, 0:1], ALU.pow).then_inc(rms_ready, 1)

            def expert_rstd(b):
                pool.wait_ge(ln2, after(b, 5, 5))
                pool.tensor_tensor(rs2[:, :], ve2[:, :], mhalf[:, 0:2], ALU.pow).then_inc(rs2_ready, 1)

            def chunks(b, first, last):
                for c in range(C):
                    behind = (b, 0) if c else (b - 1, 1)
                    ahead = (b + 1, 0) if c else (b, 1)
                    if not (last and c):
                        masked_products(*ahead)
                    add_term(b, c, 0)
                    if not (last and c):
                        first_sources(*ahead)
                    if last and c == 0:
                        expert_rstd(0)
                    for j in range(1, SUMMED[0]):
                        add_term(b, c, j)
                    if not (first and c == 0):
                        inverse_rms(*behind)
                    for j in range(SUMMED[0], SUMMED[c]):
                        add_term(b, c, j)

            masked_products(0, 0)
            first_sources(0, 0, (0, 3))
            pool.wait_ge(tok_sb, after(B - 1, 3, 3))
            passes(pool, chunks)

            def retention_rstd(j):
                pool.wait_ge(ln3, after(j, 5, 5))
                pool.tensor_tensor(rs3[:, :], ve3[:, :], mhalf[:, 0:2], ALU.pow).then_inc(rs3_ready, 1)

            def mask_products(j):
                pool.wait_ge(y2_ps, before(j, 1, 1))
                pool.wait_ge(p_ready, after(j, 1, 1))
                pool.wait_ge(in_const, 32)
                for e in range(E // 2, E):
                    ins = pool.tensor_tensor(pm[:, e, :, :], p[:, :, :],
                                             mask[:, e, bass.ts(j, L)].unsqueeze(1).broadcast_to([P, KD, L]), ALU.mult)
                ins.then_inc(pm_far_ready, 1)

            def rotate_across(j):
                pool.wait_ge(pr_sb, after(j, 3, 1))
                pool.wait_ge(in_const, 32)
                source = by_rotated(qkr[:, :, 0:2 * DK])
                for a, z, other in ((0, QK // 2, QK // 2), (QK // 2, QK, 0)):
                    ins = pool.tensor_tensor(by_rotated(rb)[:, :, :, a:z], source[:, :, :, other:other + QK // 2],
                                             rotation(j, 1, a, z), ALU.mult)
                ins.then_inc(rot_cross, 1)

            def own_position(c):
                pool.wait_ge(rot_ready, after(2 * c + 1, 2, 2))
                pool.tensor_tensor(prod[:, c, 0:B * DK].rearrange("p (b n) -> p b n", b=B),
                                   q_all[:, c * B:(c + 1) * B, :], k_all[:, c * B:(c + 1) * B, :], ALU.mult)\
                    .then_inc(prod0_ready, 1)

            def far_values(c):
                pool.wait_ge(pr_sb, after(2 * c + 1, 3, 2))
                pool.wait_ge(wl_ready, c + 1)
                for lag in (B - 1, B - 2):
                    at, n = PAIR_AT[lag], B - lag
                    pool.tensor_tensor(pv[:, c, at * DV:(at + n) * DV].rearrange("p (h d) -> p h d", d=QV),
                                       v_all[:, c * B:c * B + n, :].rearrange("p b (h d) -> p (b h) d", d=QV),
                                       wl[:, c, at * QH:(at + n) * QH].unsqueeze(2).broadcast_to([P, n * QH, QV]),
                                       ALU.mult).then_inc(pv_pool, 1)
                pool.wait_ge(pv_pool, 2 * (c + 1))
                far, near = PAIR_AT[B - 1] * DV, (PAIR_AT[B - 2] + 1) * DV
                pool.tensor_tensor(pv[:, c, near:near + DV], pv[:, c, near:near + DV], pv[:, c, far:far + DV], ALU.add)\
                    .then_inc(pv_far, 1)

            def gated(c):
                pool.wait_ge(pr_sb, after(2 * c + 1, 3, 3))
                for i in range(2):
                    pool.wait_ge(oc_ready, 2 * c + i + 1)
                    pool.tensor_tensor(og[:, c, two_positions(i)], pv[:, c, two_positions(i)],
                                       g_all[:, c * B + 2 * i:c * B + 2 * i + 2, :].rearrange("p b n -> p (b n)"),
                                       ALU.mult).then_inc(ocg_ready, 1)

            def scale_first():
                pool.wait_ge(inv_ready, 1)
                pool.wait_ge(ocg_ready, 2)
                for i in range(2):
                    part = og[:, 0, two_positions(i)].rearrange("p (h d) -> p h d", d=QV)
                    inv_dev = rsh[:, 0, 2 * i * QH:(2 * i + 2) * QH]
                    pool.tensor_tensor(part, part, inv_dev.unsqueeze(2).broadcast_to([P, 2 * QH, QV]), ALU.mult)\
                        .then_inc(og_ready[0], 1)

            def experts(b, first, last):
                if not last:
                    expert_rstd(b + 1)
                if not first:
                    retention_rstd(b - 1)
                if last:
                    own_position(0)
                mask_products(b)
                if first:
                    inverse_rms(B - 1, 1)
                if last:
                    far_values(0)
                if last:
                    retention_rstd(B - 1)
                if not first:
                    rotate_across(b - 1)

            passes(pool, experts)
            rotate_across(B - 1)
            gated(0)
            own_position(1)
            scale_first()
            far_values(1)
            gated(1)

        @block.vector
        def _(dve):
            for name in ("h_ready", "taps", "xsd_ready", "src1_ready", "srcx_ready", "coef_ready", "own_ready", "p_taken",
                         "yz_ready", "ms_ready", "x1_ready", "ln2", "h2_ready", "hm_ready", "p_ready", "pm_ready",
                         "x2_ready", "ln3", "h3_ready", "conv3", "dl_ready", "rot_same", "rot_ready"):
                dve.sem_inc(*sems[name])
            dve.memset(ones[:, :], 1.0)
            for pair in range(B // 2):
                slots = [c * B + 2 * pair + i for c in range(C) for i in range(2)]
                done = pair * (len(slots) + 1)
                dve.wait_ge(in_x[pair], 32)
                for x in slots:
                    dve.bn_stats(st[:, x, :], x_all[:, x, :]).then_inc(v_setup, 1)
                for n, x in enumerate(slots):
                    dve.wait_ge(v_setup, done + n + 1)
                    ins = dve.bn_aggr(mv[:, x, :], st[:, x, :])
                ins.then_inc(v_setup, 1)
                dve.wait_ge(v_setup, done + len(slots) + 1)
                dve.tensor_scalar(of_pair(ve, pair), of_pair(mv[:, :, 1], pair), EPS, None, ALU.add)\
                   .then_inc(var_ready, 1)
            with dve.Fori(0, B // 2) as pair:
                for i in range(2):
                    dve.wait_ge(hT_ps, before(pair, 2, i + 1))
                    dve.wait_ge(rstd_ready, after(pair, 1, 1))
                    for c in range(C):
                        x = 2 * pair + (i + c * B)
                        ins = dve.tensor_scalar(h_sb[:, i, c, :], x_all[:, x, :], mv[:, x, 0:1], rs[:, bass.ds(x, 1)],
                                                ALU.subtract, ALU.mult)
                    ins.then_inc(h_ready, 1)

            dve.wait_ge(in_dt, 64)
            for i in range(2):
                dve.wait_ge(dt_ps, i + 1)
                dve.wait_ge(sp_act, i + 1)
                dve.tensor_scalar(dt_raw[:, i * 2 * L:(i + 1) * 2 * L], PS[:, i, :], dt_bias[:, :], 0.0,
                                  ALU.add, ALU.max).then_inc(sp_dve, 1)
            dve.wait_ge(sp_act, 5)
            dve.tensor_tensor(avec[:, :], avec[:, :], sign[:, :], ALU.mult).then_inc(sp_dve, 1)
            dve.wait_ge(sp_dve, 3)
            dve.tensor_tensor(dt_raw[:, :], dt_raw[:, :], sp1[:, :], ALU.add).then_inc(sp_dve, 1)
            dve.wait_ge(sp_dve, 4)
            dve.tensor_scalar(dt_raw[:, :], dt_raw[:, :], avec[:, :], None, ALU.mult).then_inc(dtT_ready, 1)

            dve.wait_ge(in_w1, 32)
            with dve.Fori(0, B) as b:
                for q in range(MX // 2):
                    dve.wait_ge(tap3, after(b, 3, q + 1))
                    for tap in range(1, 4):
                        for m in range(2):
                            n = 6 * q + 2 * (tap - 1) + m
                            if tap > 1:
                                dve.wait_ge(taps, after(b, 18, n - 1))
                            dve.scalar_tensor_tensor(acc[:, 2 * q + m, tap:], PS[:, 2 + q, m * L:(m + 1) * L - tap],
                                                     conv_w[:, 2 * q + m, 3 - tap:4 - tap], acc[:, 2 * q + m, tap:],
                                                     ALU.mult, ALU.add).then_inc(taps, 1)

            dve.wait_ge(in_small, 48)
            for m in range(MZ):
                ins = dve.tensor_scalar(w_out[:, m, :], w_out[:, m, :], norm_w[:, m:m + 1], None, ALU.mult)
            ins.then_inc(w_out_ready, 1)

            dve.wait_ge(masks_ready, 1)
            dve.wait_ge(dtok_sb, 1)

            def dt_xs(b, c):
                i = b * C + c
                dve.wait_ge(src0_ready, before(b, 4, 2 * c + 2))
                dve.tensor_tensor(heads(xsd[:, c, :]), heads(xs_all[:, i, :]), over_head(dtok_all[:, i, 0:H]),
                                  ALU.mult).then_inc(xsd_ready, 1)

            def decayed(b, c, slots):
                dve.wait_ge(xsd_ready, after(b, C, c + 1))
                dve.wait_ge(ex_sb, after(b, 2, 2 if slots[-1] >= EARLY else 1))
                for s in slots:
                    ins = dve.tensor_tensor(heads(src[:, c, s, :]), heads(xsd[:, c, :]),
                                            over_head(ex_all[:, b, s, c, :]), ALU.mult)
                    if s == NS - 1:
                        ins.then_inc(src1_ready, 1)
                if slots[-1] < BY_POOL:
                    ins.then_inc(start_ready, 1)

            def decayed_to_end(b):
                dve.wait_ge(xsd_ready, after(b, C, 1))
                dve.wait_ge(ex_sb, after(b, 2, 2))
                dve.tensor_tensor(heads(srcx), heads(xsd[:, 0, :]), over_head(ex_all[:, b, SEAM, 0, :]),
                                  ALU.mult).then_inc(srcx_ready, 1)

            def own_factor(b, c):
                dve.wait_ge(diag_sum, after(b, C, c + 1))
                dve.scalar_tensor_tensor(coefd[:, c, :], dtok_all[:, b * C + c, 0:H], cbd[:, c:c + 1], d_bc[:, :],
                                         ALU.mult, ALU.add).then_inc(coef_ready, 1)

            def own_term(b, c):
                dve.wait_ge(yT_ps, before(b, C, c + 1))
                dve.wait_ge(coef_ready, after(b, C, c + 1))
                dve.tensor_tensor(heads(term[:, terms(c)[0], :]), heads(xs_all[:, b * C + c, :]),
                                  over_head(coefd[:, c, :]), ALU.mult).then_inc(own_ready, 1)

            def take(b, c, j, lv):
                u = sum(USES[:c]) + j
                slot = SEAM if lv == "seam" else NS + lv
                dve.wait_ge(ex_sb, after(b, 2, 2))
                dve.wait_ge(p_ps, after(b, NU, u + 1))
                dve.tensor_tensor(heads(term[:, terms(c)[1 + j], :]), heads(PS[:, product_bank(u), :]),
                                  over_head(ex_all[:, b, slot, c, :]), ALU.mult).then_inc(p_taken, 1)

            def gate(b, c):
                dve.wait_ge(o1_ps, before(b, C, c + 1))
                dve.wait_ge(yT_ps, after(b, C, c + 1))
                dve.tensor_tensor(yzT[:, c, :, :], PS[:, 6, :].rearrange("p (m t) -> p m t", m=MZ),
                                  zT_all[:, :, bass.ds((b * C + c) * P, P)], ALU.mult).then_inc(yz_ready, 1)

            def mean_square(b, c):
                dve.wait_ge(o1_ps, after(b, C, c + 1))
                dve.tensor_scalar(ms[:, c:c + 1], PS[:, 7, D:D + 1], 1.0 / HID, EPS, ALU.mult, ALU.add)\
                    .then_inc(ms_ready, 1)

            def residual(b, c):
                i = b + c * B
                dve.wait_ge(rms_ready, after(b, C, c + 1))
                dve.scalar_tensor_tensor(x_all[:, i, :], PS[:, 7, 0:D], rms[:, c:c + 1], x_all[:, i, :],
                                         ALU.mult, ALU.add).then_inc(x1_ready, 1)

            def statistics(b, chain, stats, moments, v_eps):
                for c in range(C):
                    dve.bn_stats(stats[:, c, :], x_all[:, b * C + c, :]).then_inc(chain, 1)
                dve.wait_ge(chain, after(b, 5, 2))
                dve.memset(v_eps[:, :], EPS)
                for c in range(C):
                    dve.bn_aggr(moments[:, c, :], stats[:, c, :]).then_inc(chain, 1)
                dve.wait_ge(chain, after(b, 5, 4))
                dve.tensor_tensor(v_eps[:, :], moments[:, :, 1], v_eps[:, :], ALU.add).then_inc(chain, 1)

            def normalise(b, rstd_done, moments, rstd, done, dst):
                dve.wait_ge(rstd_done, after(b, 1, 1))
                for c in range(C):
                    ins = dve.tensor_scalar(dst[:, c, :], x_all[:, b * C + c, :], moments[:, c, 0:1], rstd[:, c:c + 1],
                                            ALU.subtract, ALU.mult)
                ins.then_inc(done, 1)

            def mask_tokens(b):
                dve.wait_ge(h2T_ps, after(b, 1, 1))
                for e in range(E):
                    ins = dve.tensor_tensor(hm[:, e, :, :], PS[:, 0, :].rearrange("p (k t) -> p k t", k=KD),
                                            mask[:, e, bass.ts(b, L)].unsqueeze(1).broadcast_to([P, KD, L]), ALU.mult)
                ins.then_inc(hm_ready, 1)

            def chunks(b, first, last):
                for c in range(C):
                    behind = (b, 0) if c else (b - 1, 1)
                    ahead = (b + 1, 0) if c else (b, 1)
                    steps = levels_of(c)
                    for j, lv in enumerate(steps):
                        take(b, c, j, lv)
                        if not (first and c == 0):
                            if j == 1:
                                gate(*behind)
                            if j == 3:
                                mean_square(*behind)
                        if not (last and c):
                            if j == 0:
                                dt_xs(*ahead)
                                if c == 0:
                                    decayed_to_end(b)
                            if j == 1:
                                decayed(*ahead, range(BY_POOL, EARLY - 1))
                            if j == 2:
                                decayed(*ahead, range(EARLY - 1, NS))
                            if j == 3:
                                own_factor(*ahead)
                                own_term(*ahead)
                        if not (first and c == 0) and j == 3:
                            residual(*behind)
                        if last:
                            if (c, j) == (0, 2):
                                dve.wait_ge(x1_ready, after(1, C, 1))
                                statistics(0, ln2, st2, mv2, ve2)
                            if (c, j) == (0, 3):
                                normalise(0, rs2_ready, mv2, rs2, h2_ready, h2)
                            if (c, j) == (1, 2):
                                mask_tokens(0)

            dt_xs(0, 0)
            decayed(0, 0, (1, 2))
            decayed(0, 0, range(BY_POOL, NS))
            own_factor(0, 0)
            own_term(0, 0)
            passes(dve, chunks)
            def gate_up(b):
                dve.wait_ge(pm_far_ready, before(b, 1, 1))
                dve.wait_ge(sg_ready, after(b, 1, 1))
                dve.tensor_tensor(p[:, :, :], PS[:, 1, :].rearrange("p (k t) -> p k t", k=KD), sg[:, :, :],
                                  ALU.mult).then_inc(p_ready, 1)
                dve.wait_ge(y2_ps, before(b, 1, 1))
                dve.wait_ge(p_ready, after(b, 1, 1))
                for e in range(E // 2):
                    ins = dve.tensor_tensor(pm[:, e, :, :], p[:, :, :],
                                            mask[:, e, bass.ts(b, L)].unsqueeze(1).broadcast_to([P, KD, L]), ALU.mult)
                ins.then_inc(pm_ready, 1)

            def expert_residual(b):
                dve.wait_ge(y2_ps, after(b, 1, 1))
                dve.tensor_tensor(x_all[:, bass.ts(b, C), :], PS[:, 2, :].rearrange("p (c n) -> p c n", c=C),
                                  x_all[:, bass.ts(b, C), :], ALU.add).then_inc(x2_ready, 1)

            def convolve(j):
                now = PS[:, 3, :].rearrange("p (i k t) -> p i k t", i=2, k=KD)
                dve.wait_ge(h3T_sb, before(j, 1, 1))
                dve.wait_ge(h3T_ps, after(j, 1, 1))
                for k in range(KD):
                    ins = dve.tensor_scalar(cacc[:, :, k, :], now[:, :, k, :], conv3_w[:, k, 1:2], None, ALU.mult)
                ins.then_inc(conv3, 1)
                dve.wait_ge(conv3, after(j, 3, 1))
                for i in range(2):
                    for k in range(KD):
                        prev = now[:, 0, k, :] if i else h3_prev[:, prev_slot(j), k, :]
                        ins = dve.scalar_tensor_tensor(cacc[:, i, k, :], prev, conv3_w[:, k, 0:1], cacc[:, i, k, :],
                                                       ALU.mult, ALU.add)
                    ins.then_inc(conv3, 1)

            def route(j):
                dve.wait_ge(pr_sb, after(j, 3, 1))
                dve.tensor_copy(delta[:, bass.ds(2 * j, 2), :], qkr[:, :, 2 * DK:2 * DK + QH])\
                   .then_inc(dl_ready, 1)

            def rotate_same(j):
                dve.wait_ge(pr_sb, after(j, 3, 1))
                dve.tensor_tensor(by_rotated(ra), by_rotated(qkr[:, :, 0:2 * DK]), rotation(j, 0, 0, QK), ALU.mult)\
                   .then_inc(rot_same, 1)

            def rotated(j):
                dve.wait_ge(rot_same, after(j, 1, 1))
                dve.wait_ge(rot_cross, after(j, 1, 1))
                for part, dst in enumerate((q_all, k_all)):
                    own = slice(part * DK, (part + 1) * DK)
                    dve.tensor_tensor(dst[:, bass.ds(2 * j, 2), :], ra[:, :, own], rb[:, :, own], ALU.add)\
                       .then_inc(rot_ready, 1)

            def router_and_values():
                wv = w_vg[:, :, 0:DV]
                dve.tensor_tensor(rwd.rearrange("p (h d) -> p h d", h=QH), rw[:, :, :, 1], rw[:, :, :, 0],
                                  ALU.subtract).then_inc(set3, 1)
                dve.wait_ge(set3, 1)
                dve.tensor_tensor(wv_part, wv, rwd.unsqueeze(1).broadcast_to([P, KD, DV]), ALU.mult).then_inc(set3, 1)
                for k in range(KD):
                    ins = dve.tensor_reduce(wv_mean[:, k, :], by_head(wv[:, k, :], QV), AX_X, ALU.add)
                ins.then_inc(set3, 1)
                dve.wait_ge(set3, 3)
                for k in range(KD):
                    ins = dve.tensor_reduce(w_qkr[:, k, 2 * DK:], by_head(wv_part[:, k, :], QV), AX_X, ALU.add)
                ins.then_inc(set3, 1)
                for k in range(KD):
                    dve.scalar_tensor_tensor(by_head(wv[:, k, :], QV), over(wv_mean[:, k, :], QH, QV), -1.0 / QV,
                                             by_head(wv[:, k, :], QV), ALU.mult, ALU.add).then_inc(set3, 1)

            n_links = [0]

            def link(ins):
                n_links[0] += 1
                ins.then_inc(chain3, 1)
                dve.wait_ge(chain3, n_links[0])

            def by_head(ap, width):
                return ap.rearrange("p (h d) -> p h d", d=width)

            def by_slot(ap, width):
                return ap.rearrange("p b (h d) -> p (b h) d", d=width)

            def over(ap, n, width):
                return ap.unsqueeze(2).broadcast_to([P, n, width])

            def choices(c):
                s0 = c * B
                dve.wait_ge(dl_ready, after(2 * c + 1, 1, 1))
                link(dve.tensor_scalar(ind[:, c, :], delta[:, s0:s0 + B, :].rearrange("p b h -> p (b h)"), 0.0, None,
                                       ALU.is_gt))
                for lag in range(1, B):
                    at, n = PAIR_AT[lag], B - lag
                    dve.tensor_tensor(eq[:, c, at * QH:(at + n) * QH], ind[:, c, lag * QH:], ind[:, c, 0:n * QH],
                                      ALU.is_equal)
                link(dve.memset(cnt[:, c, :], 1.0))
                for lag in range(1, B):
                    at, n = PAIR_AT[lag], B - lag
                    link(dve.tensor_tensor(cnt[:, c, lag * QH:], cnt[:, c, lag * QH:], eq[:, c, at * QH:(at + n) * QH],
                                           ALU.add))
                link(dve.reciprocal(sc[:, c, :], cnt[:, c, :]))
                scale = float(QK) ** -0.5
                dve.wait_ge(th_ready, c + 1)
                link(dve.scalar_tensor_tensor(th[:, c, :], th[:, c, :], -1.0, th[:, c, :], ALU.mult, ALU.max))
                link(dve.tensor_scalar(th[:, c, :], th[:, c, :], 0.5 * scale, 0.5 * scale, ALU.mult, ALU.add))
                link(dve.tensor_tensor(sc[:, c, :], sc[:, c, :], th[:, c, :], ALU.mult))

            def pair_products(c):
                s0 = c * B
                dve.wait_ge(rot_ready, after(2 * c + 1, 2, 2))
                for lag in range(1, B):
                    at, n = PAIR_AT[lag], B - lag
                    ins = dve.tensor_tensor(prod[:, c, at * DK:(at + n) * DK].rearrange("p (b n) -> p b n", b=n),
                                            q_all[:, s0 + lag:s0 + B, :], k_all[:, s0:s0 + n, :], ALU.mult)
                ins.then_inc(pairs_done, 1)

            def pair_weights(c):
                dve.wait_ge(pairs_done, c + 1)
                own = B * QH
                dve.tensor_reduce(wl[:, c, own:], by_head(prod[:, c, B * DK:], QK), AX_X, ALU.add)
                dve.wait_ge(prod0_ready, c + 1)
                link(dve.tensor_reduce(wl[:, c, 0:own], by_head(prod[:, c, 0:B * DK], QK), AX_X, ALU.add))
                link(dve.tensor_tensor(wl[:, c, own:], wl[:, c, own:], eq[:, c, own:], ALU.mult))
                for lag in reversed(range(B)):
                    at, n = PAIR_AT[lag], B - lag
                    ins = dve.tensor_tensor(wl[:, c, at * QH:(at + n) * QH], wl[:, c, at * QH:(at + n) * QH],
                                            sc[:, c, lag * QH:], ALU.mult)
                ins.then_inc(wl_ready, 1)
                dve.wait_ge(wl_ready, c + 1)

            def weigh(c, lag):
                s0, at, n = c * B, PAIR_AT[lag], B - lag
                dve.wait_ge(pr_sb, after(2 * c + 1, 3, 2))
                link(dve.tensor_tensor(by_head(pv[:, c, at * DV:(at + n) * DV], QV),
                                       by_slot(v_all[:, s0:s0 + n, :], QV),
                                       over(wl[:, c, at * QH:(at + n) * QH], n * QH, QV), ALU.mult))

            def sum_values(c, lag):
                assert B == 4
                at, n = PAIR_AT[lag], B - lag
                if lag == B - 2:
                    dve.wait_ge(pv_far, c + 1)
                dve.tensor_tensor(pv[:, c, lag * DV:B * DV], pv[:, c, lag * DV:B * DV],
                                  pv[:, c, at * DV:(at + n) * DV], ALU.add).then_inc(oc_ready, 1)
                dve.wait_ge(oc_ready, 2 * c + lag)

            def head_sums(c):
                for i in range(2):
                    dve.wait_ge(osq_ready, 2 * c + i + 1)
                    ins = dve.tensor_reduce(var[:, c, 2 * i * QH:(2 * i + 2) * QH],
                                            by_head(osq[:, c, two_positions(i)], QV), AX_X, ALU.add)
                ins.then_inc(hvar_ready, 1)

            def invert(c):
                dve.wait_ge(dev_ready, c + 1)
                dve.reciprocal(rsh[:, c, :], dev[:, c, :]).then_inc(inv_ready, 1)

            def scale_last():
                dve.wait_ge(inv_ready, 2)
                dve.wait_ge(ocg_ready, 4)
                for i in range(2):
                    part = by_head(og[:, 1, two_positions(i)], QV)
                    dve.tensor_tensor(part, part, over(rsh[:, 1, 2 * i * QH:(2 * i + 2) * QH], 2 * QH, QV), ALU.mult)\
                        .then_inc(og_ready[1], 1)

            def retention_residual(c):
                for i in range(2):
                    dve.wait_ge(o3_ps, 2 * c + i + 1)
                    rows = x_all[:, c * B + 2 * i:c * B + 2 * i + 2, :]
                    dve.tensor_tensor(rows, PS[:, OUT_BANKS[c][i], :].rearrange("p (b n) -> p b n", n=D), rows,
                                      ALU.add).then_inc(out_ready, 1)

            def experts(b, first, last):
                if first:
                    dve.wait_ge(x1_ready, after(B - 1, C, 1))
                if not last:
                    statistics(b + 1, ln2, st2, mv2, ve2)
                    normalise(b + 1, rs2_ready, mv2, rs2, h2_ready, h2)
                if not first:
                    expert_residual(b - 1)
                    dve.wait_ge(x2_ready, after(b - 1, 1, 1))
                    dve.memset(ve3[:, :], 0.0)
                    statistics(b - 1, ln3, st3, mv3, ve3)
                    normalise(b - 1, rs3_ready, mv3, rs3, h3_ready, h3)
                if not first:
                    convolve(b - 1)
                gate_up(b)
                if first:
                    mean_square(B - 1, 1)
                if last:
                    choices(0)
                    pair_products(0)
                    pair_weights(0)
                if not last:
                    mask_tokens(b + 1)
                if first:
                    residual(B - 1, 1)
                    for c in range(C):
                        dve.memset(h3_prev[:, 3 * c, :, :], 0.0)
                    dve.wait_ge(x1_ready, after(B - 1, C, C))
                elif last:
                    weigh(0, 0)
                else:
                    route(b - 1)
                    rotate_same(b - 1)
                    rotated(b - 1)

            dve.wait_ge(in_late, 112)
            router_and_values()
            gate(B - 1, 1)
            passes(dve, experts)
            expert_residual(B - 1)
            dve.wait_ge(x2_ready, after(B - 1, 1, 1))
            statistics(B - 1, ln3, st3, mv3, ve3)
            normalise(B - 1, rs3_ready, mv3, rs3, h3_ready, h3)
            weigh(0, 1)
            convolve(B - 1)
            route(B - 2)
            rotate_same(B - 2)
            rotated(B - 2)
            sum_values(0, 1)
            sum_values(0, 2)
            head_sums(0)
            route(B - 1)
            rotate_same(B - 1)
            choices(1)
            rotated(B - 1)
            pair_products(1)
            invert(0)
            pair_weights(1)
            weigh(1, 0)
            weigh(1, 1)
            sum_values(1, 1)
            sum_values(1, 2)
            head_sums(1)
            invert(1)
            scale_last()
            retention_residual(0)
            retention_residual(1)


_INS = {
    "x": (B, L, D), "w_in": (D, WIN), "conv_w": (MX * P, 4), "dt_bias": (P, 1), "a_log": (P, 1), "d": (H,),
    "norm_w": (HID,), "w_out": (HID, D), "ids": (B, L), "ctxT": (E, D, D), "w3": (D, 2 * DK + 2 * DV),
    "conv3_w": (D, 2), "router_w": (QH, QV, 2), "w_out3": (D, D),
}


def kernel(x, itok_BxS_13_99985, ctx_2048, L0_attn_W_in, L0_attn_conv_w, L0_attn_dt_bias, L0_attn_A_log, L0_attn_D,
           L0_attn_norm_w, L0_attn_W_out, L0_ffn_conv_w, L0_ffn_Wq, L0_ffn_Wk, L0_ffn_Wv, L0_ffn_Wg,
           L0_ffn_router_w, L0_ffn_Wout):
    import numpy as np
    import concourse.bacc as bacc
    from concourse.bass_utils import run_bass_kernel_spmd

    w_in = np.asarray(L0_attn_W_in).T
    dt_bias = np.asarray(L0_attn_dt_bias)
    a_log = np.asarray(L0_attn_A_log)
    arrays = {
        "x": x, "w_in": np.concatenate([w_in, w_in[:, -H:]], 1), "conv_w": L0_attn_conv_w,
        "dt_bias": np.concatenate([dt_bias, dt_bias])[:, None],
        "a_log": np.concatenate([np.zeros_like(a_log), a_log])[:, None],
        "d": L0_attn_D, "norm_w": L0_attn_norm_w, "w_out": np.asarray(L0_attn_W_out).T, "ids": itok_BxS_13_99985,
        "ctxT": np.asarray(ctx_2048).transpose(0, 2, 1),
        "w3": np.concatenate([np.asarray(w) for w in (L0_ffn_Wq, L0_ffn_Wk, L0_ffn_Wv, L0_ffn_Wg)], 1),
        "conv3_w": L0_ffn_conv_w, "router_w": L0_ffn_router_w, "w_out3": L0_ffn_Wout,
    }
    arrays = {k: np.ascontiguousarray(v) for k, v in arrays.items()}
    assert all(arrays[k].shape == s for k, s in _INS.items())
    arrays |= shape_constants()
    nc = bacc.Bacc("TRN2", target_bir_lowering=False, num_devices=1)
    t = {k: nc.dram_tensor(f"in_{k}", a.shape, mybir.dt.from_np(a.dtype), kind="ExternalInput").ap()
         for k, a in arrays.items()}
    out = nc.dram_tensor("out", (B, L, D), F32, kind="ExternalOutput").ap()
    decoder_layer(nc, t, out)
    r = run_bass_kernel_spmd(nc, [{f"in_{k}": a for k, a in arrays.items()}], core_ids=[0])
    return r.results[0]["out"]
```
